# Optimizing a Trainium2 kernel written in Bass

```python
import numpy as np
import jax
import jax.numpy as jnp

def _softmax(x, axis=-1):
    return jax.nn.softmax(x, axis=axis)

def _gelu(x):
    return jax.nn.gelu(x, approximate=True)

def _silu(x):
    return jax.nn.silu(x)

def _sigmoid(x):
    return jax.nn.sigmoid(x)

def _layernorm(x, axis=-1, eps=1e-05):
    m = jnp.mean(x, axis=axis, keepdims=True)
    v = jnp.var(x, axis=axis, keepdims=True)
    return (x - m) / jnp.sqrt(v + eps)

def _scatter_add(tgt, idx, src, axis=0):
    return tgt.at[idx].add(src)

def _segment_sum(src, seg, n):
    return jax.ops.segment_sum(src, seg, n)
kernel_name = 'mk_decoder_postln_d2_seqx_r8_51d4e7'

def setup_inputs(seed: int=0):
    np.random.seed(seed)
    _w = jnp.asarray

    def _rec_inputs():
        import jax
        import jax.numpy as jnp
        _rk = jax.random.key(seed)
        x = -0.000125 + 0.9999 * jax.random.normal(jax.random.fold_in(_rk, 1), (8, 256, 128), jnp.float32)
        _lenS = 256 - jax.random.randint(jax.random.fold_in(_rk, 7), (8,), 0, max(1, 256 // 4) + 1, jnp.int32)
        _lenS2 = 256 - jax.random.randint(jax.random.fold_in(_rk, 8), (8,), 0, max(1, 256 // 4) + 1, jnp.int32)
        _ctx_1024P = jax.random.normal(jax.random.fold_in(_rk, 11), (8, 16, 128), jnp.float32)
        _ctx_1024c = jax.random.dirichlet(jax.random.fold_in(_rk, 511), 0.3 * jnp.ones((16,), jnp.float32), (8, 256))
        _ctx_1024t = jnp.einsum('bsk,bkd->bsd', _ctx_1024c, _ctx_1024P)
        _ctx_1024t = _ctx_1024t * jax.lax.rsqrt(jnp.mean(jnp.square(_ctx_1024t)) + 1e-12) * 0.953939
        ctx_1024 = -1.52775e-05 + 0.999936 * (_ctx_1024t + 0.3 * jax.random.normal(jax.random.fold_in(_rk, 611), (8, 256, 128), jnp.float32))
        return (x, ctx_1024)
    x, ctx_1024 = _rec_inputs()

    def _L0_attn_setup():
        import jax, jax.numpy as jnp
        import numpy as np
        B, S, E = (2, 512, 128)
        H = 16
        W = 32

        def _chunk3(x):
            prev = jnp.pad(x[:, :-1], ((0, 0), (1, 0), (0, 0), (0, 0), (0, 0)))
            nxt = jnp.pad(x[:, 1:], ((0, 0), (0, 1), (0, 0), (0, 0), (0, 0)))
            return jnp.stack([prev, x, nxt], axis=-1)
        key = jax.random.key(seed)
        ks = jax.random.split(key, 4)
        hs = jax.random.normal(ks[0], (B, S, E), jnp.float32)

        def lin(k):
            kw, kb = jax.random.split(k)
            return (jax.random.normal(kw, (E, E), jnp.float32) * 0.02, jax.random.normal(kb, (E,), jnp.float32) * 0.02)
        Wq, bq = lin(ks[1])
        Wk, bk = lin(ks[2])
        Wv, bv = lin(ks[3])
        return {'hidden_states': hs, 'Wq': Wq, 'bq': bq, 'Wk': Wk, 'bk': bk, 'Wv': Wv, 'bv': bv}
    _L0_attn_all = _L0_attn_setup()
    _L0_attn_in = {k: v for k, v in _L0_attn_all.items() if k in ('Wq', 'bq', 'Wk', 'bk', 'Wv', 'bv')}
    del _L0_attn_all

    def _L0_xattn_setup():
        import jax, jax.numpy as jnp
        import numpy as np
        import math
        B, L, D, H = (8, 512, 128, 16)
        DK = D // H
        FACTOR = 1

        def _linear(x, W, b):
            return jnp.einsum('bld,od->blo', x, W) + b
        rng = jax.random.key(seed)
        ks = jax.random.split(rng, 11)
        s = 0.02
        return {'query': jax.random.normal(ks[0], (B, L, D), jnp.float32), 'key': jax.random.normal(ks[1], (B, L, D), jnp.float32), 'value': jax.random.normal(ks[2], (B, L, D), jnp.float32), 'Wq': jax.random.normal(ks[3], (D, D), jnp.float32) * s, 'bq': jax.random.normal(ks[4], (D,), jnp.float32) * s, 'Wk': jax.random.normal(ks[5], (D, D), jnp.float32) * s, 'bk': jax.random.normal(ks[6], (D,), jnp.float32) * s, 'Wv': jax.random.normal(ks[7], (D, D), jnp.float32) * s, 'bv': jax.random.normal(ks[8], (D,), jnp.float32) * s, 'Wo': jax.random.normal(ks[9], (D, D), jnp.float32) * s, 'bo': jax.random.normal(ks[10], (D,), jnp.float32) * s}
    _L0_xattn_all = _L0_xattn_setup()
    _L0_xattn_in = {k: v for k, v in _L0_xattn_all.items() if k in ('Wq', 'bq', 'Wk', 'bk', 'Wv', 'bv', 'Wo', 'bo')}
    del _L0_xattn_all

    def _L0_ffn_setup():
        import jax, jax.numpy as jnp
        import numpy as np
        NUM_EXPERTS = 8
        NUM_SELECTED = 2
        EXPERT_CAPACITY = 64
        NUM_GROUPS = 8

        def _routing(xg, w_router):
            G, T, H = xg.shape
            logits = jnp.einsum('gth,he->gte', xg, w_router)
            probs = jax.nn.softmax(logits, axis=-1)
            _gate, idx = jax.lax.top_k(probs, NUM_SELECTED)
            idx_kt = jnp.swapaxes(idx, 1, 2).reshape(G, -1)
            expert_mask = jax.nn.one_hot(idx_kt, NUM_EXPERTS, dtype=jnp.int32)
            priority = jnp.cumsum(expert_mask, axis=1) * expert_mask - 1
            priority = priority.reshape(G, NUM_SELECTED, T, NUM_EXPERTS)
            priority = jnp.swapaxes(priority, 1, 2).max(axis=2)
            dispatch = jax.nn.one_hot(priority, EXPERT_CAPACITY, dtype=xg.dtype)
            combine = probs[..., None] * dispatch
            return (dispatch, combine)
        key = jax.random.key(seed)
        k1, k2, k3, k4 = jax.random.split(key, 4)
        B, S, H, F = (8, 256, 128, 512)
        return {'x': jax.random.normal(k1, (B, S, H), jnp.float32), 'w_router': jax.random.normal(k2, (H, NUM_EXPERTS), jnp.float32) * 0.02, 'wi': jax.random.normal(k3, (NUM_EXPERTS, H, F), jnp.float32) * 0.02, 'wo': jax.random.normal(k4, (NUM_EXPERTS, F, H), jnp.float32) * 0.02}
    _L0_ffn_all = _L0_ffn_setup()
    _L0_ffn_in = {k: v for k, v in _L0_ffn_all.items() if k in ('w_router', 'wi', 'wo')}
    del _L0_ffn_all

    def _L1_attn_setup():
        import jax, jax.numpy as jnp
        import numpy as np
        DIM = 128
        HEADS = 16
        DIM_HEAD = 64
        INNER = HEADS * DIM_HEAD
        SCALE = DIM_HEAD ** (-0.5)

        def rotate_half(t):
            x1, x2 = jnp.split(t, 2, axis=-1)
            return jnp.concatenate((-x2, x1), axis=-1)

        def rotary_pos(n, d, dtype):
            inv_freq = 1.0 / 10000.0 ** (jnp.arange(0, d, 2, dtype=jnp.float32) / d)
            freqs = jnp.arange(n, dtype=jnp.float32)[:, None] * inv_freq[None, :]
            return jnp.concatenate((freqs, freqs), axis=-1).astype(dtype)

        def apply_rope(pos, t):
            return t * jnp.cos(pos) + rotate_half(t) * jnp.sin(pos)
        key = jax.random.key(seed)
        ks = jax.random.split(key, 5)
        x = jax.random.normal(ks[0], (2, 256, DIM), dtype=jnp.float32)
        gamma = jnp.ones((DIM,), dtype=jnp.float32)
        beta = jnp.zeros((DIM,), dtype=jnp.float32)
        Wq = jax.random.normal(ks[1], (DIM, INNER), dtype=jnp.float32) * 0.02
        Wkv = jax.random.normal(ks[2], (DIM, 2 * INNER), dtype=jnp.float32) * 0.02
        Wo = jax.random.normal(ks[3], (INNER, DIM), dtype=jnp.float32) * 0.02
        return {'x': x, 'gamma': gamma, 'beta': beta, 'Wq': Wq, 'Wkv': Wkv, 'Wo': Wo}
    _L1_attn_all = _L1_attn_setup()
    _L1_attn_in = {k: v for k, v in _L1_attn_all.items() if k in ('gamma', 'beta', 'Wq', 'Wkv', 'Wo')}
    del _L1_attn_all

    def _L1_xattn_setup():
        import jax, jax.numpy as jnp
        import numpy as np
        B, L, D = (8, 256, 128)
        key = jax.random.key(seed)
        k1, k2, k3 = jax.random.split(key, 3)
        enc_outputs = jax.random.normal(k1, (B, L, D), dtype=jnp.float32)
        x = jax.random.normal(k2, (B, L, D), dtype=jnp.float32)
        Wq = jax.random.normal(k3, (D, D), dtype=jnp.float32) * (1.0 / np.sqrt(D))
        return {'enc_outputs': enc_outputs, 'x': x, 'Wq': Wq}
    _L1_xattn_all = _L1_xattn_setup()
    _L1_xattn_in = {k: v for k, v in _L1_xattn_all.items() if k in ('Wq',)}
    del _L1_xattn_all

    def _L1_ffn_setup():
        import jax, jax.numpy as jnp
        import numpy as np
        EPS = 1e-06
        LN_EPS = 1e-05

        def _absmean_core(W):
            gamma = jnp.mean(jnp.abs(W)) + EPS
            Ws = W / gamma
            Wq = jnp.sign(Ws) * jnp.minimum(jnp.round(jnp.abs(Ws)), 1.0)
            return (Wq, gamma)

        @jax.custom_vjp
        def absmean(W):
            return _absmean_core(W)[0]

        def _absmean_fwd(W):
            Wq, gamma = _absmean_core(W)
            return (Wq, gamma)

        def _absmean_bwd(gamma, g):
            return (g / gamma,)
        absmean.defvjp(_absmean_fwd, _absmean_bwd)

        def layernorm(x, w, b, eps=LN_EPS):
            mu = jnp.mean(x, axis=-1, keepdims=True)
            var = jnp.mean((x - mu) ** 2, axis=-1, keepdims=True)
            return (x - mu) * jax.lax.rsqrt(var + eps) * w + b
        key = jax.random.key(seed)
        k1, k2, k3 = jax.random.split(key, 3)
        d, h = (128, 512)
        B, T = (8, 256)
        return {'x': jax.random.normal(k1, (B, T, d), jnp.float32), 'W_fc': jax.random.normal(k2, (h, d), jnp.float32), 'ln_w': jnp.ones((h,), jnp.float32), 'ln_b': jnp.zeros((h,), jnp.float32), 'W_proj': jax.random.normal(k3, (d, h), jnp.float32)}
    _L1_ffn_all = _L1_ffn_setup()
    _L1_ffn_in = {k: v for k, v in _L1_ffn_all.items() if k in ('W_fc', 'ln_w', 'ln_b', 'W_proj')}
    del _L1_ffn_all
    return {'x': x, 'ctx_1024': ctx_1024, 'L0_attn_Wq': _L0_attn_in['Wq'], 'L0_attn_bq': _L0_attn_in['bq'], 'L0_attn_Wk': _L0_attn_in['Wk'], 'L0_attn_bk': _L0_attn_in['bk'], 'L0_attn_Wv': _L0_attn_in['Wv'], 'L0_attn_bv': _L0_attn_in['bv'], 'L0_xattn_Wq': _L0_xattn_in['Wq'], 'L0_xattn_bq': _L0_xattn_in['bq'], 'L0_xattn_Wk': _L0_xattn_in['Wk'], 'L0_xattn_bk': _L0_xattn_in['bk'], 'L0_xattn_Wv': _L0_xattn_in['Wv'], 'L0_xattn_bv': _L0_xattn_in['bv'], 'L0_xattn_Wo': _L0_xattn_in['Wo'], 'L0_xattn_bo': _L0_xattn_in['bo'], 'L0_ffn_w_router': _L0_ffn_in['w_router'], 'L0_ffn_wi': _L0_ffn_in['wi'], 'L0_ffn_wo': _L0_ffn_in['wo'], 'L1_attn_gamma': _L1_attn_in['gamma'], 'L1_attn_beta': _L1_attn_in['beta'], 'L1_attn_Wq': _L1_attn_in['Wq'], 'L1_attn_Wkv': _L1_attn_in['Wkv'], 'L1_attn_Wo': _L1_attn_in['Wo'], 'L1_xattn_Wq': _L1_xattn_in['Wq'], 'L1_ffn_W_fc': _L1_ffn_in['W_fc'], 'L1_ffn_ln_w': _L1_ffn_in['ln_w'], 'L1_ffn_ln_b': _L1_ffn_in['ln_b'], 'L1_ffn_W_proj': _L1_ffn_in['W_proj']}

def reference(x, ctx_1024, L0_attn_Wq, L0_attn_bq, L0_attn_Wk, L0_attn_bk, L0_attn_Wv, L0_attn_bv, L0_xattn_Wq, L0_xattn_bq, L0_xattn_Wk, L0_xattn_bk, L0_xattn_Wv, L0_xattn_bv, L0_xattn_Wo, L0_xattn_bo, L0_ffn_w_router, L0_ffn_wi, L0_ffn_wo, L1_attn_gamma, L1_attn_beta, L1_attn_Wq, L1_attn_Wkv, L1_attn_Wo, L1_xattn_Wq, L1_ffn_W_fc, L1_ffn_ln_w, L1_ffn_ln_b, L1_ffn_W_proj):
    import jax
    import jax.numpy as jnp

    def _L0_attn_ref(hidden_states, Wq, bq, Wk, bk, Wv, bv):
        import jax, jax.numpy as jnp
        import numpy as np
        B, S, E = (2, 512, 128)
        H = 16
        W = 32

        def _chunk3(x):
            prev = jnp.pad(x[:, :-1], ((0, 0), (1, 0), (0, 0), (0, 0), (0, 0)))
            nxt = jnp.pad(x[:, 1:], ((0, 0), (0, 1), (0, 0), (0, 0), (0, 0)))
            return jnp.stack([prev, x, nxt], axis=-1)
        b, s, e = hidden_states.shape
        h, w = (H, W)
        d = e // h
        nc = s // w
        q = (hidden_states @ Wq.T + bq) * (1.0 / np.sqrt(d))
        k = hidden_states @ Wk.T + bk
        v = hidden_states @ Wv.T + bv
        q = q.reshape(b, s, h, d)
        k = k.reshape(b, s, h, d)
        v = v.reshape(b, s, h, d)
        cq = q.reshape(b, nc, w, h, d)
        ck3 = _chunk3(k.reshape(b, nc, w, h, d))
        scores = jnp.einsum('bcxhd,bcyhde->bcxhey', cq, ck3).reshape(b, s, h, 3 * w)
        ii = jnp.arange(w)[:, None]
        cc = jnp.arange(w + 1)[None, :]
        beg_mask = cc < w - ii
        end_mask = cc >= w - ii
        neg_inf = jnp.array(-jnp.inf, scores.dtype)
        beg = jnp.where(beg_mask[None, :, None, :], neg_inf, scores[:, :w, :, :w + 1])
        scores = scores.at[:, :w, :, :w + 1].set(beg)
        end = jnp.where(end_mask[None, :, None, :], neg_inf, scores[:, s - w:, :, 3 * w - (w + 1):])
        scores = scores.at[:, s - w:, :, 3 * w - (w + 1):].set(end)
        probs = jax.nn.softmax(scores.astype(jnp.float32), axis=-1).astype(hidden_states.dtype)
        cp = probs.reshape(b, nc, w, h, 3, w)
        cv3 = _chunk3(v.reshape(b, nc, w, h, d))
        attn = jnp.einsum('bcwhpd,bcdhep->bcwhe', cp, cv3).reshape(b, s, h, d)
        return attn.reshape(b, s, e)

    def _L0_xattn_ref(query, key, value, Wq, bq, Wk, bk, Wv, bv, Wo, bo):
        import jax, jax.numpy as jnp
        import numpy as np
        import math
        B, L, D, H = (8, 512, 128, 16)
        DK = D // H
        FACTOR = 1

        def _linear(x, W, b):
            return jnp.einsum('bld,od->blo', x, W) + b
        Bx, Lx, _ = query.shape
        Q = _linear(query, Wq, bq).reshape(Bx, Lx, H, DK).transpose(0, 2, 1, 3)
        K = _linear(key, Wk, bk).reshape(Bx, Lx, H, DK).transpose(0, 2, 1, 3)
        V = _linear(value, Wv, bv).reshape(Bx, Lx, H, DK).transpose(0, 2, 1, 3)
        Qf = jnp.fft.rfft(Q, axis=2)
        Kf = jnp.fft.rfft(K, axis=2)
        corr = jnp.fft.irfft(Qf * jnp.conj(Kf), n=Lx, axis=2)
        corr_mean = corr.mean(axis=-1)
        top_k = max(1, int(FACTOR * math.log(Lx + 1)))
        top_k = min(top_k, Lx)
        top_w, top_idx = jax.lax.top_k(corr_mean, top_k)
        top_w = jax.nn.softmax(top_w, axis=-1)
        pos = jnp.arange(Lx)
        out = jnp.zeros_like(V)
        for i in range(top_k):
            gidx = (pos[None, None, :] - top_idx[:, :, i, None]) % Lx
            rolled = jnp.take_along_axis(V, gidx[..., None], axis=2)
            out = out + top_w[:, :, i, None, None] * rolled
        out = out.transpose(0, 2, 1, 3).reshape(Bx, Lx, D)
        out = _linear(out, Wo, bo)
        return out

    def _L0_ffn_ref(x, w_router, wi, wo):
        import jax, jax.numpy as jnp
        import numpy as np
        NUM_EXPERTS = 8
        NUM_SELECTED = 2
        EXPERT_CAPACITY = 64
        NUM_GROUPS = 8

        def _routing(xg, w_router):
            G, T, H = xg.shape
            logits = jnp.einsum('gth,he->gte', xg, w_router)
            probs = jax.nn.softmax(logits, axis=-1)
            _gate, idx = jax.lax.top_k(probs, NUM_SELECTED)
            idx_kt = jnp.swapaxes(idx, 1, 2).reshape(G, -1)
            expert_mask = jax.nn.one_hot(idx_kt, NUM_EXPERTS, dtype=jnp.int32)
            priority = jnp.cumsum(expert_mask, axis=1) * expert_mask - 1
            priority = priority.reshape(G, NUM_SELECTED, T, NUM_EXPERTS)
            priority = jnp.swapaxes(priority, 1, 2).max(axis=2)
            dispatch = jax.nn.one_hot(priority, EXPERT_CAPACITY, dtype=xg.dtype)
            combine = probs[..., None] * dispatch
            return (dispatch, combine)
        B, S, H = x.shape
        T = B * S // NUM_GROUPS
        xg = x.reshape(NUM_GROUPS, T, H)
        dispatch, combine = _routing(xg, w_router)
        expert_in = jnp.einsum('gth,gtec->gech', xg, dispatch)
        h = jax.nn.gelu(jnp.einsum('gech,ehf->gecf', expert_in, wi))
        expert_out = jnp.einsum('gecf,efh->gech', h, wo)
        out = jnp.einsum('gech,gtec->gth', expert_out, combine)
        return out.reshape(B, S, H)

    def _L1_attn_ref(x, gamma, beta, Wq, Wkv, Wo):
        import jax, jax.numpy as jnp
        import numpy as np
        DIM = 128
        HEADS = 16
        DIM_HEAD = 64
        INNER = HEADS * DIM_HEAD
        SCALE = DIM_HEAD ** (-0.5)

        def rotate_half(t):
            x1, x2 = jnp.split(t, 2, axis=-1)
            return jnp.concatenate((-x2, x1), axis=-1)

        def rotary_pos(n, d, dtype):
            inv_freq = 1.0 / 10000.0 ** (jnp.arange(0, d, 2, dtype=jnp.float32) / d)
            freqs = jnp.arange(n, dtype=jnp.float32)[:, None] * inv_freq[None, :]
            return jnp.concatenate((freqs, freqs), axis=-1).astype(dtype)

        def apply_rope(pos, t):
            return t * jnp.cos(pos) + rotate_half(t) * jnp.sin(pos)
        b, n, _ = x.shape
        mu = jnp.mean(x, axis=-1, keepdims=True)
        var = jnp.var(x, axis=-1, keepdims=True)
        xn = (x - mu) / jnp.sqrt(var + 1e-05) * gamma + beta
        q = xn @ Wq
        kv = xn @ Wkv
        k, v = jnp.split(kv, 2, axis=-1)

        def to_heads(t):
            return t.reshape(b, n, HEADS, DIM_HEAD).transpose(0, 2, 1, 3)
        q, k, v = map(to_heads, (q, k, v))
        pos = rotary_pos(n, DIM_HEAD, x.dtype)
        q = apply_rope(pos, q)
        k = apply_rope(pos, k)
        q = q * SCALE
        sim = jnp.einsum('bhid,bhjd->bhij', q, k)
        neg = -jnp.finfo(sim.dtype).max
        causal_mask = jnp.triu(jnp.ones((n, n), dtype=bool), k=1)
        sim = jnp.where(causal_mask, neg, sim)
        attn = jax.nn.softmax(sim, axis=-1)
        out = jnp.einsum('bhij,bhjd->bhid', attn, v)
        out = out.transpose(0, 2, 1, 3).reshape(b, n, INNER)
        return out @ Wo

    def _L1_xattn_ref(enc_outputs, x, Wq):
        import jax, jax.numpy as jnp
        import numpy as np
        B, L, D = (8, 256, 128)
        d_k = x.shape[-1]
        q = jnp.einsum('bld,hd->blh', x, Wq)
        k = jnp.einsum('bld,hd->blh', enc_outputs, Wq)
        v = k
        scores = jnp.einsum('bqh,bkh->bqk', q, k) / jnp.sqrt(jnp.float32(d_k))
        Lq, Lk = (scores.shape[1], scores.shape[2])
        causal = jnp.tril(jnp.ones((Lq, Lk), dtype=bool))
        scores = jnp.where(causal, scores, -jnp.inf)
        attn = jax.nn.softmax(scores, axis=-1)
        return jnp.einsum('bqk,bkh->bqh', attn, v)

    def _L1_ffn_ref(x, W_fc, ln_w, ln_b, W_proj):
        import jax, jax.numpy as jnp
        import numpy as np
        EPS = 1e-06
        LN_EPS = 1e-05

        def _absmean_core(W):
            gamma = jnp.mean(jnp.abs(W)) + EPS
            Ws = W / gamma
            Wq = jnp.sign(Ws) * jnp.minimum(jnp.round(jnp.abs(Ws)), 1.0)
            return (Wq, gamma)

        @jax.custom_vjp
        def absmean(W):
            return _absmean_core(W)[0]

        def _absmean_fwd(W):
            Wq, gamma = _absmean_core(W)
            return (Wq, gamma)

        def _absmean_bwd(gamma, g):
            return (g / gamma,)
        absmean.defvjp(_absmean_fwd, _absmean_bwd)

        def layernorm(x, w, b, eps=LN_EPS):
            mu = jnp.mean(x, axis=-1, keepdims=True)
            var = jnp.mean((x - mu) ** 2, axis=-1, keepdims=True)
            return (x - mu) * jax.lax.rsqrt(var + eps) * w + b
        h = jnp.einsum('btd,hd->bth', x, absmean(W_fc))
        h = jax.nn.gelu(h, approximate=False)
        h = layernorm(h, ln_w, ln_b)
        return jnp.einsum('bth,dh->btd', h, absmean(W_proj))
    x = _layernorm(x + _L0_attn_ref(x, L0_attn_Wq, L0_attn_bq, L0_attn_Wk, L0_attn_bk, L0_attn_Wv, L0_attn_bv), axis=-1)
    x = _layernorm(x + _L0_xattn_ref(x, ctx_1024, ctx_1024, L0_xattn_Wq, L0_xattn_bq, L0_xattn_Wk, L0_xattn_bk, L0_xattn_Wv, L0_xattn_bv, L0_xattn_Wo, L0_xattn_bo), axis=-1)
    x = _layernorm(x + _L0_ffn_ref(x, L0_ffn_w_router, L0_ffn_wi, L0_ffn_wo), axis=-1)
    x = _layernorm(x + _L1_attn_ref(x, L1_attn_gamma, L1_attn_beta, L1_attn_Wq, L1_attn_Wkv, L1_attn_Wo), axis=-1)
    x = _layernorm(x + _L1_xattn_ref(ctx_1024, x, L1_xattn_Wq), axis=-1)
    x = _layernorm(x + _L1_ffn_ref(x, L1_ffn_W_fc, L1_ffn_ln_w, L1_ffn_ln_b, L1_ffn_W_proj), axis=-1)
    return x

_drawn_inputs = setup_inputs


def setup_inputs(seed=0):
    import zlib

    import numpy as np

    out = dict(_drawn_inputs(seed))
    spreads = {'L1_attn_gamma': (1.0, 0.6),
     'L1_attn_beta': (0.0, 0.612),
     'L1_ffn_ln_w': (1.0, 0.2),
     'L1_ffn_ln_b': (0.0, 0.1)}
    factors = {'L0_attn_Wq': 8.0,
     'L0_attn_bq': 8.0,
     'L0_attn_Wk': 8.0,
     'L0_attn_bk': 176.496,
     'L0_xattn_Wq': 2.708,
     'L0_xattn_bq': 200.0,
     'L0_xattn_Wk': 2.705,
     'L0_xattn_bk': 200.0,
     'L0_xattn_bv': 8.0,
     'L0_ffn_w_router': 5.066,
     'L0_ffn_wi': 4.551,
     'L0_ffn_wo': 4.462,
     'L1_attn_Wq': 8.0}
    for name, (base, spread) in spreads.items():
        noise = np.random.default_rng([zlib.crc32(name.encode()), seed]).standard_normal(out[name].shape)
        drawn = base * np.exp(spread * noise) if base else spread * noise
        out[name] = jnp.asarray(drawn.astype(out[name].dtype))
    for name, factor in factors.items():
        out[name] = (out[name] * factor).astype(out[name].dtype)
    return out
```

```python
import concourse.bass as bass
from concourse import mybir
from contextlib import ExitStack
import numpy as np

BATCH, SEQ, DIM = 8, 256, 128
ROWS = 2
PAIRS = BATCH // ROWS
TOPK = min(max(1, int(np.log(SEQ + 1))), SEQ)
TILES = ROWS * SEQ // 128
TOK = ROWS * SEQ
LN_EPS = 1e-5
ABS_EPS = 1e-6
DH = 64
INNER = 16 * DH
HP = INNER // 128
KEYS = 128 + SEQ
EXPERTS, CAP, FF = 8, 64, 512
HEADS, HD, CHUNK = 16, DIM // 16, 32
GROUPS = DIM // 32
CPT = 128 // CHUNK
WIN = 3 * CHUNK
PADDED = SEQ + 2 * CHUNK


class Signal:

    def __init__(self, sem, per):
        self.sem, self.per = sem, per

    def __call__(self, p, k):
        return self.sem, p * self.per + k + 1


def wait_alone(eng, first, least, sem, value):
    value = eng.to_reg(value)
    eng.wait_ge(first.sem, least)
    eng.wait_ge(sem, value)


def shape_constants():
    f = np.float32
    c = {}
    c["ident"] = np.eye(128, dtype=f)
    ch = np.arange(128)
    sub = (ch % 32) // HD
    c["qscale4"] = ((sub[:, None] == np.arange(4)) * (1.0 / np.sqrt(HD))).astype(f)
    pick = np.zeros((128, 4, 128), f)
    pickden = np.zeros((128, 4, HEADS), f)
    for k in range(128):
        pick[k, sub[k], k] = 1.0
        if k % HD == 0:
            pickden[k, sub[k], k // HD] = 1.0
    c["pick"], c["pickden"] = pick, pickden
    q = np.arange(128) % CHUNK
    edge = np.zeros((128, 2, WIN), f)
    y = np.arange(WIN)
    edge[:, 0] = np.where(y[None] < CHUNK - q[:, None], -1e30, 0)
    off = y[None] - (2 * CHUNK - 1)
    edge[:, 1] = np.where((off >= 0) & (off >= CHUNK - q[:, None]), -1e30, 0)
    c["edge"] = edge
    valid = np.ones((1, 3, WIN), f)
    valid[0, 0, :CHUNK] = 0
    valid[0, 2, 2 * CHUNK:] = 0
    c["valid"] = valid
    half = SEQ // 2
    n, k = np.arange(SEQ), np.arange(half)
    w = 2 * np.pi / SEQ
    re, im = np.cos(w * n[:, None] * k), -np.sin(w * n[:, None] * k)
    nyq = np.cos(np.pi * n)
    im0 = im.copy()
    im[:, 0] = nyq
    re_n = re.copy()
    re_n[:, 0] = nyq
    tiled = lambda t: t.reshape(2, 128, -1).transpose(1, 0, 2)
    c["F"] = tiled(np.concatenate([re, im], 1))
    c["F_im0"], c["F_reN"] = tiled(im0), tiled(re_n)
    twice = np.where(k == 0, 1.0, 2.0)[:, None] / SEQ
    inv_re, inv_im = re.T * twice, im.T * twice
    c["inv_re"], c["inv_im"] = inv_re, inv_im
    c["corr_re"] = inv_re / HD
    c["corr_re2"] = np.concatenate([nyq[None] / SEQ, inv_re[1:]]) / HD
    c["corr_im"] = np.concatenate([0 * nyq[None], inv_im[1:]]) / HD
    c["dc"] = SEQ * (np.arange(128)[None] == 0)
    inv_freq = (1.0 / (np.float32(10000.0) ** (np.arange(0, DH, 2, dtype=f) / np.float32(DH)))).astype(f)
    ang = (np.arange(SEQ, dtype=f)[:, None] * inv_freq[None]).astype(f).T.astype(np.float64)
    c["cos"], c["sin"] = np.tile(np.cos(ang), (4, 1)), np.tile(np.sin(ang), (4, 1))
    c["causal"] = np.where(np.arange(128)[None] > np.arange(128)[:, None], -1e30, 0)
    c["tri"] = np.triu(np.ones((128, 128)))
    c["iota"] = np.tile(np.arange(SEQ), (128, 1))
    return {k: np.ascontiguousarray(v, dtype=f) for k, v in c.items()}


def decoder(nc, a, out):
    f32, bf16 = mybir.dt.float32, mybir.dt.bfloat16
    ALU, ACT, AX = mybir.AluOpType, mybir.ActivationFunctionType, mybir.AxisListType
    ctx = ExitStack()
    with ctx:
        def sb(name, shape, dt=f32):
            return ctx.enter_context(nc.sbuf_tensor(name, shape, dt))

        class Arena:

            def __init__(self, name, words):
                self.all, self.at, self.words = sb(name, [128, words]), 0, words

            def restart(self):
                self.at = 0

            def __call__(self, shape):
                n = int(np.prod(shape[1:]))
                flat = self.all[0:shape[0], self.at:self.at + n]
                self.at += n
                assert self.at <= self.words, (self.at, self.words)
                names = " ".join("abcd"[:len(shape) - 1])
                return flat.rearrange(f"p ({names}) -> p {names}", **dict(zip("abcd", shape[1:])))

        signals = []

        def signal(name, per):
            signals.append(Signal(ctx.enter_context(nc.semaphore(name)), per))
            return signals[-1]

        ps = ctx.enter_context(nc.psum_tensor("ps", [128, 8, 512], f32))

        odd, even = Arena("odd", ODD_WORDS), Arena("even", EVEN_WORDS)

        ident = sb("ident_sb", [128, 128])
        identb = sb("identb", [128, 128], bf16)
        qscale4 = sb("qscale4_sb", [128, 4])
        qbias4 = sb("qbias4", [128, 4])
        pick = sb("pick_sb", [128, 4, 128])
        pickden = sb("pickden_sb", [128, 4, HEADS])
        edge = even([128, 2, WIN])
        edgeb = sb("edgeb", [128, 2, WIN], bf16)
        valid = sb("valid_sb", [1, 3, WIN])
        ones = sb("ones", [128, 128])
        minus_half = sb("minus_half", [128, 2])
        A_wq, A_wk, A_wv = (sb(f"A_w{n}_sb", [128, 128]) for n in "qkv")
        A_bq, A_bk = sb("A_bq_sb", [128, 1]), sb("A_bk_sb", [128, 1])
        A_bv = sb("A_bv_sb", [1, 128])
        loads_A = [(ident, a["ident"]), (A_wq, a["A_wq"]), (A_wk, a["A_wk"]), (A_wv, a["A_wv"]),
                   (A_bq, a["A_bq"]), (A_bk, a["A_bk"]), (A_bv, a["A_bv"]), (qscale4, a["qscale4"]),
                   (pick, a["pick"]), (pickden, a["pickden"]), (edge, a["edge"]), (valid, a["valid"])]

        Fm = sb("F_sb", [128, 2, SEQ])
        F_im0, F_reN = sb("F_im0_sb", [128, 2, 128]), sb("F_reN_sb", [128, 2, 128])
        inv_re, inv_im = sb("inv_re_sb", [128, SEQ]), sb("inv_im_sb", [128, SEQ])
        corr_re, corr_re2, corr_im = (sb(f"{n}_sb", [128, SEQ]) for n in ("corr_re", "corr_re2", "corr_im"))
        dc = sb("dc_sb", [1, 128])
        iota = sb("iota_sb", [128, SEQ])
        B_wq, B_wkv, B_wo = sb("B_wq_sb", [128, 128]), sb("B_wkv_sb", [128, 256]), sb("B_wo_sb", [128, 128])
        B_bq, B_bkv, B_bo = sb("B_bq_sb", [1, 128]), sb("B_bkv_sb", [1, 256]), sb("B_bo_sb", [1, 128])
        loads_B = [(Fm, a["F"]), (F_im0, a["F_im0"]), (F_reN, a["F_reN"]), (inv_re, a["inv_re"]),
                   (inv_im, a["inv_im"]), (corr_re, a["corr_re"]), (corr_re2, a["corr_re2"]),
                   (corr_im, a["corr_im"]), (dc, a["dc"]), (iota, a["iota"]), (B_wq, a["B_wq"]),
                   (B_wkv, a["B_wkv"]), (B_wo, a["B_wo"]), (B_bq, a["B_bq"]), (B_bkv, a["B_bkv"]),
                   (B_bo, a["B_bo"])]

        C_wr = sb("C_wr_sb", [128, EXPERTS])
        C_wi, C_wo = sb("C_wi_sb", [128, EXPERTS, FF]), sb("C_wo_sb", [128, EXPERTS, FF // 128, DIM])
        tri = even([128, 128])
        trib, onesb = sb("trib", [128, 128], bf16), sb("onesb", [128, 128], bf16)
        loads_C = [(C_wr, a["C_wr"]), (tri, a["tri"]), (C_wi, a["C_wi"]), (C_wo, a["C_wo"])]

        D_gamma, D_beta = sb("D_gamma_sb", [128, 1]), sb("D_beta_sb", [128, 1])
        D_w, D_wr = sb("D_w_sb", [128, 2, INNER]), sb("D_wr", [128, 2, INNER])
        D_wv, D_wo = sb("D_wv_sb", [128, INNER]), sb("D_wo_sb", [128, HP, DIM])
        cos, sin = sb("cos_sb", [128, SEQ]), sb("sin_sb", [128, SEQ])
        causal, causalb = even([128, 128]), sb("causalb", [128, 128], bf16)
        loads_D = [(D_gamma, a["D_gamma"]), (D_beta, a["D_beta"]), (D_w, a["D_w"]), (D_wv, a["D_wv"]),
                   (D_wo, a["D_wo"]), (cos, a["cos"]), (sin, a["sin"]), (causal, a["causal"])]
        E_w = sb("E_w_sb", [128, 128])
        F_w1r, F_w2r = even([128, FF]), even([128, FF // 128, DIM])
        F_w1, F_w2 = sb("F_w1", [128, FF]), sb("F_w2", [128, FF // 128, DIM])
        F_abs, F_sum = even([128, FF]), sb("F_sum", [128, 2])
        F_thr = sb("F_thr", [128, 2, 2])
        F_lw, F_lb = sb("F_lw_sb", [128, FF // 128]), sb("F_lb_sb", [128, FF // 128])
        loads_F = [(E_w, a["E_w"]), (F_w1r, a["F_w1"]), (F_w2r, a["F_w2"]), (F_lw, a["F_lw"]), (F_lb, a["F_lb"])]

        x0 = sb("x0", [128, TILES, DIM])
        x1 = sb("x1", [128, TILES, DIM])
        ysum = sb("ysum", [128, TILES, DIM])
        stats = sb("stats", [128, TILES, 6])
        mv = sb("mv", [128, TILES, 2])
        rstd = sb("rstd", [128, TILES, 1])

        A_xT = sb("A_xT", [128, ROWS, PADDED])
        A_kT = sb("A_kT", [128, ROWS, PADDED])
        A_q = odd([128, TOK // CHUNK, 4, CHUNK])
        A_v = odd([WIN, ROWS * SEQ // CHUNK, DIM])
        A_p = odd([128, 2, GROUPS, CPT, WIN])
        A_mx = sb("A_mx", [128, 2, GROUPS, CPT])
        A_pT = odd([WIN, CPT, GROUPS, 128])
        A_o = odd([128, 2, 4, 128])
        A_rd = sb("A_rd", [128, HEADS])

        even.restart()
        ctx0 = sb("ctx0", [128, TILES, DIM])
        x2 = sb("x2", [128, TILES, DIM])
        B_cF, B_xF = even([128, ROWS, SEQ]), even([128, ROWS, SEQ])
        B_kv = even([128, ROWS, 2, 2 * DIM])
        B_prod = even([128, 4, ROWS, DIM])
        B_R = even([128, 4, ROWS * HEADS])
        B_c = even([ROWS * HEADS, SEQ])
        B_top = sb("B_top", [ROWS * HEADS, 8])
        B_idx = sb("B_idx", [ROWS * HEADS, 8], mybir.dt.uint32)
        B_idxf = sb("B_idxf", [ROWS * HEADS, 8])
        B_w, B_e = sb("B_w", [ROWS * HEADS, TOPK]), sb("B_e", [ROWS * HEADS, TOPK])
        B_sum, B_rs = sb("B_sum", [ROWS * HEADS, 1]), sb("B_rs", [ROWS * HEADS, 1])
        B_g = even([ROWS * HEADS, TOPK, SEQ])
        B_gT = even([128, 2, ROWS * HEADS])
        B_G = even([128, 3, ROWS * HEADS])
        B_t = even([128, 4, ROWS, DIM])
        B_O = even([128, 2, ROWS, DIM])
        B_OT = even([128, TOK])

        odd.restart()
        C_xT = odd([128, TOK])
        C_top = sb("C_top", [128, TILES, 8])
        C_idx = sb("C_idx", [128, TILES, 8], mybir.dt.uint32)
        C_idxf = sb("C_idxf", [128, TILES, 2])
        C_m = sb("C_m", [128, TILES, 2, EXPERTS], bf16)
        C_p = odd([128, TILES, EXPERTS])
        C_sum = sb("C_sum", [128, TILES])
        C_mc = odd([128, TILES, 2, EXPERTS])
        C_slot = odd([128, TILES, EXPERTS])
        C_D = odd([128, TILES, EXPERTS, CAP])
        C_cb = odd([128, TILES, EXPERTS, CAP])
        C_in = odd([128, EXPERTS, ROWS, CAP])
        C_cT = odd([128, TILES, 4, 128])
        C_h = odd([128, 2, FF // 128, ROWS * CAP])
        C_eo = odd([128, ROWS, EXPERTS // 2, DIM])
        x3 = odd([128, TILES, DIM])

        even.restart()
        x4 = x1
        D_xn = x2
        D_xT = even([128, TOK])
        D_v = even([128, TILES, INNER])
        D_t = even([128, 2, 2, TOK])
        D_qk = even([128, 2, 2, TOK])
        D_mx, D_nb = sb("D_mx", [128, 2, 2, 2]), sb("D_nb", [128, 2, 2, 2])
        D_sum, D_rs = sb("D_sum", [128, 2, 2, 2]), sb("D_rs", [128, 2, 2, 2])
        D_p = even([128, 2, 2, KEYS])
        D_pT = even([128, 2, 2, KEYS])
        D_ao = even([128, 2, TILES, 128])
        D_aT = even([128, HP, TOK])

        odd.restart()
        x5 = x2
        E_cT, E_xT = odd([128, TOK]), odd([128, TOK])
        E_qT, E_kT = odd([128, TOK]), odd([128, TOK])
        E_v = odd([128, TILES, DIM])
        E_mx, E_nb = odd([128, 2, ROWS]), odd([128, 2, ROWS])
        E_sum, E_rs = odd([128, 2, ROWS]), odd([128, 2, ROWS])
        E_p, E_pT = odd([128, ROWS, KEYS]), odd([128, ROWS, KEYS])

        x6 = ysum
        F_xT = odd([128, TOK])
        F_h = odd([128, TILES, FF])
        F_nT = odd([128, FF // 128, TOK])

        w_A = signal("w_A", 0)
        dve_set, pool_set = signal("dve_set", 0), signal("pool_set", 0)
        x_in = signal("x_in", 16)
        out_done = signal("out_done", 16)
        moments_ok, rstd_ok = signal("moments_ok", LNS), signal("rstd_ok", 2 * LNS)
        vchain = signal("vchain", VCHAIN)
        A_xT_ps, A_xT_sb = signal("A_xT_ps", 1), signal("A_xT_sb", 1)
        A_q_ps, A_k_ps, A_v_ps = signal("A_q_ps", 1), signal("A_k_ps", 1), signal("A_v_ps", 4)
        A_q_sb, A_k_sb, A_v_sb = signal("A_q_sb", 1), signal("A_k_sb", 1), signal("A_v_sb", 4)
        A_s_ps = signal("A_s_ps", TILES)
        A_sub = signal("A_sub", TILES)
        A_exp = signal("A_exp", TILES)
        A_pT_ps, A_pT_sb = signal("A_pT_ps", 2 * TILES), signal("A_pT_sb", 2 * TILES)
        A_o_ps, A_o_sb = signal("A_o_ps", TILES), signal("A_o_sb", TILES)
        A_y_ps, A_y_sb = signal("A_y_ps", TILES), signal("A_y_sb", TILES)
        x1_ok = signal("x1_ok", ROWS)
        w_B, c_in = signal("w_B", 0), signal("c_in", 16)
        B_cF_ps, B_cF_sb = signal("B_cF_ps", 1), signal("B_cF_sb", 1)
        B_kv_ps, B_kv_sb = signal("B_kv_ps", ROWS), signal("B_kv_sb", ROWS)
        B_xF_ps, B_xF_sb = signal("B_xF_ps", 1), signal("B_xF_sb", 1)
        B_q_ps, B_R_ok, B_c_ps = signal("B_q_ps", 1), signal("B_R_ok", 1), signal("B_c_ps", 1)
        B_top_ok, B_exp = signal("B_top_ok", 1), signal("B_exp", 1)
        B_g_ok, B_gT_ps, B_gT_sb = signal("B_g_ok", 1), signal("B_gT_ps", 1), signal("B_gT_sb", 1)
        B_G_ps, B_G_sb = signal("B_G_ps", 1), signal("B_G_sb", 1)
        B_tp, B_Ore, B_Oim = signal("B_tp", 1), signal("B_Ore", 1), signal("B_Oim", 1)
        B_OT_ps, B_OT_sb, B_y_ps, B_y_sb = (signal(n, 1) for n in ("B_OT_ps", "B_OT_sb", "B_y_ps", "B_y_sb"))
        x2_ok = signal("x2_ok", ROWS)
        w_C = signal("w_C", 0)
        C_xT_ps, C_xT_sb, C_lg_ps = signal("C_xT_ps", 1), signal("C_xT_sb", 1), signal("C_lg_ps", 1)
        C_sub, C_exp, C_m_ok, C_pos_ps = (signal(n, 1) for n in ("C_sub", "C_exp", "C_m_ok", "C_pos_ps"))
        C_p_ok, C_D_ok, C_cb_ok = signal("C_p_ok", 1), signal("C_D_ok", TILES), signal("C_cb_ok", TILES)
        C_in_ps, C_in_sb = signal("C_in_ps", ROWS), signal("C_in_sb", ROWS)
        C_cT_ps, C_cT_sb = signal("C_cT_ps", TILES), signal("C_cT_sb", TILES)
        C_h_ps, C_h_sb = signal("C_h_ps", EXPERTS), signal("C_h_sb", EXPERTS)
        C_eo_ps, C_eo_sb = signal("C_eo_ps", 2), signal("C_eo_sb", 2)
        C_y_ps = signal("C_y_ps", 1)
        x3_ok = signal("x3_ok", ROWS)
        w_D, w_F = signal("w_D", 0), signal("w_F", 0)
        F_abs_ok, F_tot_ps, F_chain = signal("F_abs_ok", 0), signal("F_tot_ps", 0), signal("F_chain", 0)
        D_wr_ok = signal("D_wr_ok", 0)
        D_xn_ok = signal("D_xn_ok", ROWS)
        D_xT_ps, D_xT_sb = signal("D_xT_ps", 1), signal("D_xT_sb", 1)
        D_v_ps, D_v_sb = signal("D_v_ps", 2 * TILES), signal("D_v_sb", 2 * TILES)
        D_pr_ps, D_t_ok = signal("D_pr_ps", 2 * HP), signal("D_t_ok", 2 * HP)
        D_qk_ok = signal("D_qk_ok", 2 * HP)
        D_s_ps, D_nb_ok, D_exp = (signal(n, ROWS * HP) for n in ("D_s_ps", "D_nb_ok", "D_exp"))
        D_pT_ps, D_pT_sb, D_o_ps, D_o_sb = (signal(n, ROWS * HP) for n in ("D_pT_ps", "D_pT_sb", "D_o_ps", "D_o_sb"))
        D_aT_ps, D_aT_sb = signal("D_aT_ps", HP), signal("D_aT_sb", HP)
        D_y_ps = signal("D_y_ps", 1)
        x4_ok = signal("x4_ok", ROWS)
        E_cT_ps, E_cT_sb, E_xT_ps, E_xT_sb = (signal(n, 1) for n in ("E_cT_ps", "E_cT_sb", "E_xT_ps", "E_xT_sb"))
        E_k_ps, E_k_sb, E_v_ps, E_v_sb, E_q_ps, E_q_sb = \
            (signal(n, 1) for n in ("E_k_ps", "E_k_sb", "E_v_ps", "E_v_sb", "E_q_ps", "E_q_sb"))
        E_s_ps, E_nb_ok, E_exp, E_pT_ps, E_pT_sb, E_y_ps = \
            (signal(n, 1) for n in ("E_s_ps", "E_nb_ok", "E_exp", "E_pT_ps", "E_pT_sb", "E_y_ps"))
        x5_ok = signal("x5_ok", ROWS)
        F_xT_ps, F_xT_sb = signal("F_xT_ps", 1), signal("F_xT_sb", 1)
        F_h_ps, F_h_sb, F_n_ok = (signal(n, TILES) for n in ("F_h_ps", "F_h_sb", "F_n_ok"))
        F_nT_ps, F_nT_sb = signal("F_nT_ps", FF // 128), signal("F_nT_sb", FF // 128)
        F_y_ps = signal("F_y_ps", 1)
        x6_ok = signal("x6_ok", ROWS)

        block = ctx.enter_context(nc.Block())

        def stage_A_scalar(act, p):
            act.wait_ge(*A_xT_ps(p, 1))
            act.wait_ge(*A_v_ps(p, 0))
            act.activation(A_xT[:, :, CHUNK:CHUNK + SEQ], ps[:, 0, :].rearrange("p (r t) -> p r t", r=ROWS),
                           ACT.Copy).then_inc(A_xT_sb.sem, 1)
            act.wait_ge(*A_q_ps(p, 1))
            act.wait_ge(*A_s_ps(p, 0))
            for hl in range(4):
                last = act.activation(A_q[:, :, hl, :], ps[:, 1, :].rearrange("p (c q) -> p c q", q=CHUNK), ACT.Identity, bias=qbias4[:, hl:hl + 1],
                                      scale=qscale4[:, hl:hl + 1])
            last.then_inc(A_q_sb.sem, 1)
            act.wait_ge(*A_o_ps(p, 0))
            for i in range(4):
                act.wait_ge(*A_v_ps(p, i + 1))
                act.activation(A_v[:, 4 * i:4 * i + 4, :], ps[0:WIN, 4 + i, :], ACT.Copy).then_inc(A_v_sb.sem, 1)
            for t in range(TILES):
                act.wait_ge(*A_sub(p, t + 1))
                act.activation(A_p[:, t % 2], A_p[:, t % 2], ACT.Exp).then_inc(A_exp.sem, 1)
                for half in range(2):
                    act.wait_ge(*A_pT_ps(p, 2 * t + half + 1))
                    act.wait_ge(*A_o_ps(p, t))
                    act.activation(A_pT[:, 2 * half:2 * half + 2], ps[0:WIN, 4:6, :], ACT.Copy)\
                        .then_inc(A_pT_sb.sem, 1)

        def stage_A_tensor(pe, p):
            pe.wait_ge(*x_in(p, 16))
            pe.wait_ge(*A_y_sb(p, 0))
            for t in range(TILES):
                mm = pe.transpose(ps[:, 0, 128 * t:128 * t + 128], x0[:, t, :], ident[:])
            mm.then_inc(A_xT_ps.sem, 1)
            pe.wait_ge(*A_xT_sb(p, 1))
            xT = A_xT[:, :, CHUNK:CHUNK + SEQ]
            pe.matmul(ps[:, 1, :], A_wq[:], xT, start=True, stop=True).then_inc(A_q_ps.sem, 1)
            pe.matmul(ps[:, 2, :], A_wk[:], xT, start=True, stop=True).then_inc(A_k_ps.sem, 1)
            for i in range(4):
                for j in range(4):
                    r, c = divmod(4 * i + j, SEQ // CHUNK)
                    dst = ps[0:WIN, 4 + i, 128 * j:128 * j + 128]
                    pe.matmul(dst, A_xT[:, r, CHUNK * c:CHUNK * c + WIN], A_wv[:], start=True, stop=False)
                    mm = pe.matmul(dst, valid[:, (c > 0) + (c == SEQ // CHUNK - 1), :], A_bv[:], start=False, stop=True)
                mm.then_inc(A_v_ps.sem, 1)

            def scores(t):
                pe.wait_ge(*A_sub(p, t))
                for c in range(CPT):
                    r, cc = divmod(CPT * t + c, SEQ // CHUNK)
                    side = 0 if cc == 0 else 1 if cc == SEQ // CHUNK - 1 else None
                    for g in range(GROUPS):
                        part = slice(32 * g, 32 * g + 32)
                        mm = pe.matmul(ps[:, g, WIN * c:WIN * c + WIN], A_q[part, CPT * t + c].rearrange("p h q -> p (h q)"),
                                       A_kT[part, r, CHUNK * cc:CHUNK * cc + WIN],
                                       start=True, stop=side is None)
                    if side is not None:
                        for g in range(GROUPS):
                            mm = pe.matmul(ps[:, g, WIN * c:WIN * c + WIN], identb[:], edgeb[:, side, :],
                                           start=False, stop=True)
                mm.then_inc(A_s_ps.sem, 1)

            pe.wait_ge(*A_q_sb(p, 1))
            pe.wait_ge(*A_k_sb(p, 1))
            scores(0)
            pe.wait_ge(*A_v_sb(p, 4))
            for t in range(TILES):
                if t + 1 < TILES:
                    scores(t + 1)
                pe.wait_ge(*A_exp(p, t + 1))
                for half in range(2):
                    if t or half:
                        pe.wait_ge(*A_pT_sb(p, 2 * t + half))
                    pe.wait_ge(*A_y_sb(p, t))
                    for c in range(2):
                        for g in range(GROUPS):
                            mm = pe.transpose(ps[0:WIN, 4 + c, 128 * g:128 * g + 128],
                                              A_p[:, t % 2, g, 2 * half + c, :], ident[:])
                    mm.then_inc(A_pT_ps.sem, 1)
                pe.wait_ge(*A_pT_sb(p, 2 * t + 2))
                pe.wait_ge(*A_o_sb(p, t))
                for c in range(CPT):
                    for g in range(GROUPS):
                        part = slice(32 * g, 32 * g + 32)
                        o, den = (ps[part, b, :].rearrange("p (h c q) -> p h c q", h=4, c=CPT)[:, :, c, :] for b in (6, 7))
                        pe.matmul(o, A_v[:, CPT * t + c, part], A_pT[:, c, g, :], start=True, stop=True,
                                  tile_position=(0, 32 * g))
                        mm = pe.matmul(den, ones[0:WIN, part], A_pT[:, c, g, :], start=True, stop=True,
                                       tile_position=(0, 32 * g))
                mm.then_inc(A_o_ps.sem, 1)
                pe.wait_ge(*A_o_sb(p, t + 1))
                for hl in range(4):
                    pe.matmul(ps[:, 4, 0:128], A_o[:, 0, hl, :], pick[:, hl, :], start=hl == 0, stop=hl == 3)
                for hl in range(4):
                    mm = pe.matmul(ps[:, 4, 128:128 + HEADS], A_o[:, 1, hl, :], pickden[:, hl, :],
                                   start=hl == 0, stop=hl == 3)
                mm.then_inc(A_y_ps.sem, 1)

        def stage_A_vector(dve, p, link, moments):
            dve.wait_ge(*A_k_ps(p, 1))
            dve.wait_ge(*A_s_ps(p, 0))
            dve.tensor_scalar(A_kT[:, :, CHUNK:CHUNK + SEQ], ps[:, 2, :].rearrange("p (r t) -> p r t", r=ROWS),
                              A_bk[:], None, ALU.add).then_inc(A_k_sb.sem, 1)

            def softmax(t):
                dve.wait_ge(*A_s_ps(p, t + 1))
                s = ps[:, 0:GROUPS, 0:CPT * WIN].rearrange("p g (c k) -> p g c k", k=WIN)
                link(dve.tensor_reduce(A_mx[:, t % 2], s, AX.X, ALU.max))
                if t >= 2:
                    dve.wait_ge(*A_pT_ps(p, 2 * t - 2))
                else:
                    dve.wait_ge(*A_pT_ps(p, 0))
                dve.tensor_tensor(A_p[:, t % 2], s, A_mx[:, t % 2].unsqueeze(3).to_broadcast([128, GROUPS, CPT, WIN]),
                                  ALU.subtract).then_inc(A_sub.sem, 1)

            softmax(0)
            for t in range(TILES):
                if t + 1 < TILES:
                    softmax(t + 1)
                dve.wait_ge(*A_o_ps(p, t + 1))
                dve.wait_ge(*A_y_ps(p, t))
                dve.tensor_copy(A_o[:].rearrange("p k h q -> p k (h q)"), ps[:, 6:8, :]).then_inc(A_o_sb.sem, 1)
                dve.wait_ge(*A_y_ps(p, t + 1))
                dve.wait_ge(*out_done(p, 0))
                link(dve.reciprocal(A_rd[:], ps[:, 4, 128:128 + HEADS]))
                link(dve.tensor_tensor(ysum[:, t, :].rearrange("p (h d) -> p h d", d=HD),
                                       ps[:, 4, 0:128].rearrange("p (h d) -> p h d", d=HD),
                                       A_rd[:].unsqueeze(2).to_broadcast([128, HEADS, HD]), ALU.mult))
                ins = dve.tensor_tensor(ysum[:, t, :], ysum[:, t, :], x0[:, t, :], ALU.add)
                ins.then_inc(A_y_sb.sem, 1)
                dve.wait_ge(*A_y_sb(p, t + 1))
                if t % 2:
                    moments(t // 2)

        def stage_B_tensor(pe, p):
            pe.wait_ge(w_B.sem, 16 * len(loads_B))
            pe.wait_ge(*c_in(p, 16))
            pe.wait_ge(*A_y_sb(p, TILES))
            for r in range(ROWS):
                for t in range(2):
                    mm = pe.matmul(ps[:, 0, SEQ * r:SEQ * r + SEQ], ctx0[:, 2 * r + t, :], Fm[:, t, :],
                                   start=t == 0, stop=t == 1)
            mm.then_inc(B_cF_ps.sem, 1)
            pe.wait_ge(*B_cF_sb(p, 1))
            for r in range(ROWS):
                for part in range(2):
                    dst = ps[:, 1 + r, 256 * part:256 * part + 256]
                    mm = pe.matmul(dst, B_cF[:, r, 128 * part:128 * part + 128], B_wkv[:], start=True, stop=part == 1)
                    if part == 0:
                        mm = pe.matmul(dst, dc[:], B_bkv[:], start=False, stop=True)
                mm.then_inc(B_kv_ps.sem, 1)
            for r in range(ROWS):
                pe.wait_ge(*x1_ok(p, r + 1))
                for t in range(2):
                    mm = pe.matmul(ps[:, 3, SEQ * r:SEQ * r + SEQ], x1[:, 2 * r + t, :], Fm[:, t, :],
                                   start=t == 0, stop=t == 1)
            mm.then_inc(B_xF_ps.sem, 1)
            pe.wait_ge(*B_xF_sb(p, 1))
            for r in range(ROWS):
                for part in range(2):
                    dst = ps[:, 4, 256 * r + 128 * part:256 * r + 128 * part + 128]
                    mm = pe.matmul(dst, B_xF[:, r, 128 * part:128 * part + 128], B_wq[:], start=True, stop=part == 1)
                    if part == 0:
                        mm = pe.matmul(dst, dc[:], B_bq[:], start=False, stop=True)
            mm.then_inc(B_q_ps.sem, 1)
            pe.wait_ge(*B_R_ok(p, 1))
            corr = ps[0:ROWS * HEADS, 5, 0:SEQ]
            pe.matmul(corr, B_R[:, 0, :], corr_re[:], start=True, stop=False)
            pe.matmul(corr, B_R[:, 1, :], corr_re2[:], start=False, stop=False)
            pe.matmul(corr, B_R[:, 2, :], corr_im[:], start=False, stop=True).then_inc(B_c_ps.sem, 1)
            wait_alone(pe, w_B, 16 * len(loads_B), *B_g_ok(p, 1))
            for t in range(2):
                mm = pe.transpose(ps[:, 6, 32 * t:32 * t + 32], B_g[:, 0, 128 * t:128 * t + 128], ident[0:32, 0:32])
            mm.then_inc(B_gT_ps.sem, 1)
            pe.wait_ge(*B_gT_sb(p, 1))
            for i, table in enumerate((Fm[:, :, 0:128], F_im0[:], F_reN[:])):
                for t in range(2):
                    mm = pe.matmul(ps[:, 7, 32 * i:32 * i + 32], table[:, t, :], B_gT[:, t, :], start=t == 0, stop=t == 1)
            mm.then_inc(B_G_ps.sem, 1)
            pe.wait_ge(*B_Ore(p, 1))
            pe.wait_ge(*B_Oim(p, 1))
            for r in range(ROWS):
                dst = ps[:, 0, SEQ * r:SEQ * r + SEQ]
                pe.matmul(dst, B_O[:, 0, r, :], inv_re[:], start=True, stop=False)
                mm = pe.matmul(dst, B_O[:, 1, r, :], inv_im[:], start=False, stop=True)
            mm.then_inc(B_OT_ps.sem, 1)
            pe.wait_ge(*B_OT_sb(p, 1))
            for t in range(TILES):
                dst = ps[:, 1, 128 * t:128 * t + 128]
                pe.matmul(dst, B_OT[:, 128 * t:128 * t + 128], B_wo[:], start=True, stop=False)
                mm = pe.matmul(dst, ones[0:1, :], B_bo[:], start=False, stop=True)
            mm.then_inc(B_y_ps.sem, 1)

        def stage_B_scalar(act, p):
            act.wait_ge(*B_cF_ps(p, 1))
            act.activation(B_cF[:].rearrange("p r f -> p (r f)"), ps[:, 0, :], ACT.Copy).then_inc(B_cF_sb.sem, 1)
            for r in range(ROWS):
                act.wait_ge(*B_kv_ps(p, r + 1))
                act.activation(B_kv[:, r].rearrange("p a c -> p (a c)"), ps[:, 1 + r, :], ACT.Copy).then_inc(B_kv_sb.sem, 1)
            act.wait_ge(*B_xF_ps(p, 1))
            act.activation(B_xF[:].rearrange("p r f -> p (r f)"), ps[:, 3, :], ACT.Copy).then_inc(B_xF_sb.sem, 1)
            act.wait_ge(*B_top_ok(p, 1))
            act.activation(B_e[:], B_w[:], ACT.Exp, accum_out=B_sum[:]).then_inc(B_exp.sem, 1)
            act.wait_ge(*B_gT_ps(p, 1))
            act.activation(B_gT[:].rearrange("p t c -> p (t c)"), ps[:, 6, 0:64], ACT.Copy).then_inc(B_gT_sb.sem, 1)
            act.wait_ge(*B_G_ps(p, 1))
            act.activation(B_G[:].rearrange("p t c -> p (t c)"), ps[:, 7, 0:96], ACT.Copy).then_inc(B_G_sb.sem, 1)
            act.wait_ge(*B_OT_ps(p, 1))
            act.activation(B_OT[:], ps[:, 0, :], ACT.Copy).then_inc(B_OT_sb.sem, 1)

        def G_times_V(eng, dst, i, part):
            v = B_kv[:, :, part, DIM:].rearrange("p r (h d) -> p r h d", d=HD)
            g = B_G[:, i, :].rearrange("p (r h) -> p r h", r=ROWS).unsqueeze(3).to_broadcast([128, ROWS, HEADS, HD])
            return eng.tensor_tensor(B_t[:, dst].rearrange("p r (h d) -> p r h d", d=HD), v, g, ALU.mult)

        def stage_B_vector(dve, p, link, moments):
            dve.wait_ge(*B_q_ps(p, 1))
            dve.wait_ge(*B_kv_sb(p, ROWS))
            q = ps[:, 4, :].rearrange("p (r a c) -> p r a c", r=ROWS, a=2)
            k = B_kv[:, :, :, 0:DIM]
            dve.tensor_tensor(B_prod[:, 0:2].rearrange("p a r c -> p r a c"), q, k, ALU.mult)
            dve.tensor_tensor(B_prod[:, 2], q[:, :, 1, :], k[:, :, 0, :], ALU.mult)
            link(dve.tensor_tensor(B_prod[:, 3], q[:, :, 0, :], k[:, :, 1, :], ALU.mult))
            link(dve.tensor_reduce(B_R[:].rearrange("p k h -> p (k h)"),
                                   B_prod[:].rearrange("p k r (h d) -> p (k r h) d", d=HD), AX.X, ALU.add))
            dve.tensor_tensor(B_R[:, 2, :], B_R[:, 2, :], B_R[:, 3, :], ALU.subtract).then_inc(B_R_ok.sem, 1)
            dve.wait_ge(*B_c_ps(p, 1))
            link(dve.tensor_copy(B_c[:], ps[0:ROWS * HEADS, 5, 0:SEQ]), alone=True)
            link(dve.max(B_top[:], B_c[:]), alone=True)
            dve.max_index(B_idx[:], B_top[:], B_c[:]).then_inc(vchain.sem, 1)
            dve.tensor_scalar(B_w[:], B_top[:, 0:TOPK], B_top[:, 0:1], None, ALU.subtract).then_inc(B_top_ok.sem, 1)
            link(None)
            link(dve.tensor_copy(B_idxf[:], B_idx[:]))
            dve.wait_ge(*B_exp(p, 1))
            link(dve.reciprocal(B_rs[:], B_sum[:]))
            link(dve.tensor_scalar(B_e[:], B_e[:], B_rs[:], None, ALU.mult))
            for i in range(TOPK):
                ins = dve.tensor_scalar(B_g[:, i, :], iota[0:ROWS * HEADS, :], B_idxf[:, i:i + 1], B_e[:, i:i + 1],
                                        ALU.is_equal, ALU.mult)
            link(ins)
            dve.tensor_tensor(B_g[:, 0, :], B_g[:, 0, :], B_g[:, 4, :], ALU.add)
            link(dve.tensor_tensor(B_g[:, 1, :], B_g[:, 1, :], B_g[:, 2, :], ALU.add))
            link(dve.tensor_tensor(B_g[:, 0, :], B_g[:, 0, :], B_g[:, 3, :], ALU.add))
            dve.tensor_tensor(B_g[:, 0, :], B_g[:, 0, :], B_g[:, 1, :], ALU.add).then_inc(B_g_ok.sem, 1)
            dve.wait_ge(*B_G_sb(p, 1))
            G_times_V(dve, 0, 0, 0)
            link(G_times_V(dve, 1, 1, 1))
            dve.tensor_tensor(B_O[:, 0], B_t[:, 0], B_t[:, 1], ALU.subtract).then_inc(B_Ore.sem, 1)
            dve.wait_ge(*B_y_ps(p, 1))
            dve.wait_ge(*x1_ok(p, ROWS))
            link(dve.tensor_tensor(ysum[:].rearrange("p t c -> p (t c)"), ps[:, 1, :],
                                   x1[:].rearrange("p t c -> p (t c)"), ALU.add))
            for r in range(ROWS):
                moments(r)

        def stage_B_gpsimd(pool, p):
            pool.wait_ge(*B_G_sb(p, 1))
            G_times_V(pool, 2, 2, 1)
            G_times_V(pool, 3, 1, 0).then_inc(B_tp.sem, 1)
            pool.wait_ge(*B_tp(p, 1))
            pool.tensor_tensor(B_O[:, 1], B_t[:, 2], B_t[:, 3], ALU.add).then_inc(B_Oim.sem, 1)

        def stage_C_tensor(pe, p):
            pe.wait_ge(w_C.sem, 16 * len(loads_C))
            for t in range(TILES):
                pe.wait_ge(*x2_ok(p, t // 2 + 1))
                mm = pe.transpose(ps[:, 2, 128 * t:128 * t + 128], x2[:, t, :], ident[:])
            mm.then_inc(C_xT_ps.sem, 1)
            pe.wait_ge(*C_xT_sb(p, 1))
            for t in range(TILES):
                mm = pe.matmul(ps[:, 3, 8 * t:8 * t + 8], C_xT[:, 128 * t:128 * t + 128], C_wr[:], start=True, stop=True)
            mm.then_inc(C_lg_ps.sem, 1)
            pe.wait_ge(*C_m_ok(p, 1))
            for t in range(TILES):
                t0 = t - t % 2
                dst = ps[:, 4, 16 * t:16 * t + 16]
                both = lambda n: C_m[:, n].rearrange("p k e -> p (k e)")
                pe.matmul(dst, trib[:], both(t), start=True, stop=False)
                if t % 2:
                    pe.matmul(dst, onesb[:], both(t0), start=False, stop=False)
                pe.matmul(dst[:, 8:16], onesb[:], C_m[:, t0, 0], start=False, stop=False)
                mm = pe.matmul(dst[:, 8:16], onesb[:], C_m[:, t0 + 1, 0], start=False, stop=True)
            mm.then_inc(C_pos_ps.sem, 1)
            for r in range(ROWS):
                for t in range(2):
                    pe.wait_ge(*C_D_ok(p, 2 * r + t + 1))
                    mm = pe.matmul(ps[:, 5 + r, :], x2[:, 2 * r + t, :], C_D[:, 2 * r + t].rearrange("p e c -> p (e c)"),
                                   start=t == 0, stop=t == 1)
                mm.then_inc(C_in_ps.sem, 1)

            def combine_T(t):
                pe.wait_ge(*C_cb_ok(p, t + 1))
                if t >= 2:
                    pe.wait_ge(*C_cT_sb(p, t - 1))
                for j in range(4):
                    mm = pe.transpose(ps[:, (7, 0)[t % 2], 128 * j:128 * j + 128],
                                      C_cb[:, t, 2 * j:2 * j + 2, :].rearrange("p e c -> p (e c)"), ident[:])
                mm.then_inc(C_cT_ps.sem, 1)

            def up(e):
                if e >= 2:
                    pe.wait_ge(*C_h_sb(p, e - 1))
                for f in range(FF // 128):
                    mm = pe.matmul(ps[:, 1 + e % 2, 128 * f:128 * f + 128], C_wi[:, e, 128 * f:128 * f + 128],
                                   C_in[:, e].rearrange("p r c -> p (r c)"), start=True, stop=True)
                mm.then_inc(C_h_ps.sem, 1)

            def down(e):
                pe.wait_ge(*C_h_sb(p, e + 1))
                for f in range(FF // 128):
                    mm = pe.matmul(ps[:, 3 + e // 4, 128 * (e % 4):128 * (e % 4) + 128], C_h[:, e % 2, f, :],
                                   C_wo[:, e, f, :], start=f == 0, stop=f == FF // 128 - 1)
                if e % 4 == 3:
                    mm.then_inc(C_eo_ps.sem, 1)

            pe.wait_ge(*C_in_sb(p, ROWS))
            up(0)
            for e in range(EXPERTS):
                if e < TILES:
                    combine_T(e)
                if e + 1 < EXPERTS:
                    up(e + 1)
                down(e)
            pe.wait_ge(*C_cT_sb(p, TILES))
            pe.wait_ge(*C_eo_sb(p, 2))
            for t in range(TILES):
                for j in range(4):
                    mm = pe.matmul(ps[:, 5, 128 * t:128 * t + 128], C_cT[:, t, j, :], C_eo[:, t // 2, j, :],
                                   start=j == 0, stop=j == 3)
            mm.then_inc(C_y_ps.sem, 1)

        def stage_C_scalar(act, p):
            act.wait_ge(*C_xT_ps(p, 1))
            act.activation(C_xT[:], ps[:, 2, :], ACT.Copy).then_inc(C_xT_sb.sem, 1)
            act.wait_ge(*C_sub(p, 1))
            act.activation(C_p[:], C_p[:], ACT.Exp).then_inc(C_exp.sem, 1)
            for r in range(ROWS):
                act.wait_ge(*C_in_ps(p, r + 1))
                act.activation(C_in[:, :, r, :], ps[:, 5 + r, :].rearrange("p (e c) -> p e c", c=CAP), ACT.Copy)\
                    .then_inc(C_in_sb.sem, 1)
            for e in range(EXPERTS):
                act.wait_ge(*C_h_ps(p, e + 1))
                act.activation(C_h[:, e % 2].rearrange("p f s -> p (f s)"), ps[:, 1 + e % 2, :],
                               ACT.Gelu_apprx_tanh).then_inc(C_h_sb.sem, 1)

        def stage_C_vector(dve, p, link, moments):
            logits = ps[:, 3, 0:8 * TILES].rearrange("p (t e) -> p t e", e=8)
            wait_alone(dve, dve_set, 6, *C_lg_ps(p, 1))
            for t in range(TILES):
                ins = dve.max(C_top[:, t, :], logits[:, t, :])
            link(ins, alone=True)
            for t in range(TILES):
                ins = dve.max_index(C_idx[:, t, :], C_top[:, t, :], logits[:, t, :])
            ins.then_inc(vchain.sem, 1)
            dve.tensor_tensor(C_p[:], logits, C_top[:, :, 0:1].to_broadcast([128, TILES, EXPERTS]), ALU.subtract)\
               .then_inc(C_sub.sem, 1)
            link(None)
            link(dve.tensor_copy(C_idxf[:], C_idx[:, :, 0:2]))
            dve.tensor_tensor(C_m[:].rearrange("p t k e -> p (t k) e"),
                              iota[:, 0:EXPERTS].unsqueeze(1).to_broadcast([128, 2 * TILES, EXPERTS]),
                              C_idxf[:].rearrange("p t k -> p (t k)").unsqueeze(2).to_broadcast([128, 2 * TILES, EXPERTS]),
                              ALU.is_equal).then_inc(C_m_ok.sem, 1)
            dve.wait_ge(*C_exp(p, 1))
            link(dve.tensor_reduce(C_sum[:], C_p[:], AX.X, ALU.add))
            link(dve.reciprocal(C_sum[:], C_sum[:]))
            dve.tensor_tensor(C_p[:], C_p[:], C_sum[:].unsqueeze(2).to_broadcast([128, TILES, EXPERTS]), ALU.mult)\
               .then_inc(C_p_ok.sem, 1)
            dve.wait_ge(*C_pos_ps(p, 1))
            link(dve.tensor_tensor(C_mc[:].rearrange("p t k e -> p (t k e)"), C_m[:].rearrange("p t k e -> p (t k e)"),
                                   ps[:, 4, 0:16 * TILES], ALU.mult))
            link(dve.tensor_tensor(C_slot[:], C_mc[:, :, 0, :], C_mc[:, :, 1, :], ALU.add))
            for t in range(TILES):
                dve.tensor_tensor(C_D[:, t], iota[:, 1:1 + CAP].unsqueeze(1).to_broadcast([128, EXPERTS, CAP]),
                                  C_slot[:, t, :].unsqueeze(2).to_broadcast([128, EXPERTS, CAP]), ALU.is_equal)\
                   .then_inc(C_D_ok.sem, 1)
            for t in range(TILES):
                dve.wait_ge(*C_cT_ps(p, t + 1))
                dve.tensor_copy(C_cT[:, t].rearrange("p j k -> p (j k)"), ps[:, (7, 0)[t % 2], :]).then_inc(C_cT_sb.sem, 1)
            for half in range(2):
                dve.wait_ge(*C_eo_ps(p, half + 1))
                for r in range(ROWS):
                    for odd in range(2):
                        src = ps[64 * r:64 * r + 64, 3 + half, :].rearrange("p (j o c) -> p j o c", j=2, o=2)
                        ins = dve.tensor_copy(C_eo[64 * odd:64 * odd + 64, r, 2 * half:2 * half + 2, :], src[:, :, odd, :])
                ins.then_inc(C_eo_sb.sem, 1)
            dve.wait_ge(*C_y_ps(p, 1))
            dve.wait_ge(*x2_ok(p, ROWS))
            link(dve.tensor_tensor(ysum[:].rearrange("p t c -> p (t c)"), ps[:, 5, :],
                                   x2[:].rearrange("p t c -> p (t c)"), ALU.add))
            for r in range(ROWS):
                moments(r)

        def stage_C_gpsimd(pool, p):
            pool.wait_ge(*C_p_ok(p, 1))
            for t in range(TILES):
                pool.wait_ge(*C_D_ok(p, t + 1))
                pool.tensor_tensor(C_cb[:, t], C_D[:, t], C_p[:, t, :].unsqueeze(2).to_broadcast([128, EXPERTS, CAP]),
                                   ALU.mult).then_inc(C_cb_ok.sem, 1)

        UNITS = ROWS * HP

        def heads_of(u):
            hp, r = divmod(u, ROWS)
            return hp, r

        def stage_D_tensor(pe, p):
            pe.wait_ge(w_D.sem, 16 * len(loads_D))
            pe.wait_ge(D_wr_ok.sem, 2)
            for t in range(TILES):
                pe.wait_ge(*D_xn_ok(p, t // 2 + 1))
                mm = pe.transpose(ps[:, 6, 128 * t:128 * t + 128], D_xn[:, t, :], ident[:])
            mm.then_inc(D_xT_ps.sem, 1)
            pe.wait_ge(*D_xT_sb(p, 1))

            def project(hp, kind):
                n = 2 * hp + kind
                pe.wait_ge(*D_t_ok(p, n))
                if kind == 0 and hp >= 2:
                    pe.wait_ge(*D_aT_sb(p, hp - 2))
                cols = slice(128 * hp, 128 * hp + 128)
                pe.matmul(ps[:, 0, :], D_w[:, kind, cols], D_xT[:], start=True, stop=True)
                pe.matmul(ps[:, 1, :], D_wr[:, kind, cols], D_xT[:], start=True, stop=True).then_inc(D_pr_ps.sem, 1)

            def scores(u):
                hp, r = heads_of(u)
                pe.wait_ge(*D_qk_ok(p, 2 * hp + 2))
                pe.wait_ge(*D_exp(p, max(u - 1, 0)))
                for hh in range(2):
                    part = slice(64 * hh, 64 * hh + 64)
                    bank = 2 + 2 * (u % 2) + hh
                    q = D_qk[part, hp % 2, 0, SEQ * r:SEQ * r + SEQ]
                    k = D_qk[part, hp % 2, 1, SEQ * r:SEQ * r + SEQ]
                    pe.matmul(ps[:, bank, 0:128], q[:, 0:128], k[:, 0:128], start=True, stop=False)
                    pe.matmul(ps[:, bank, 0:128], identb[:], causalb[:], start=False, stop=True)
                    pe.matmul(ps[:, bank, 128:KEYS], q[:, 128:SEQ], k, start=True, stop=False)
                    mm = pe.matmul(ps[:, bank, SEQ:KEYS], identb[:], causalb[:], start=False, stop=True)
                mm.then_inc(D_s_ps.sem, 1)

            def attend(u):
                hp, r = heads_of(u)
                pe.wait_ge(*D_exp(p, u + 1))
                pe.wait_ge(*D_o_sb(p, u))
                for hh in range(2):
                    for b in range(3):
                        mm = pe.transpose(ps[:, 6 + hh, 128 * b:128 * b + 128], D_p[:, u % 2, hh, 128 * b:128 * b + 128],
                                          ident[:])
                mm.then_inc(D_pT_ps.sem, 1)
                pe.wait_ge(*D_pT_sb(p, u + 1))
                for hh in range(2):
                    v = [D_v[:, 2 * r + t, 128 * hp + 64 * hh:128 * hp + 64 * hh + 64] for t in range(2)]
                    pT = [D_pT[:, u % 2, hh, 128 * b:128 * b + 128] for b in range(3)]
                    o = ps[:, 6 + hh, KEYS:512]
                    pe.matmul(o[:, 0:64], pT[0], v[0], start=True, stop=True)
                    pe.matmul(o[:, 64:128], pT[1], v[0], start=True, stop=False)
                    mm = pe.matmul(o[:, 64:128], pT[2], v[1], start=False, stop=True)
                mm.then_inc(D_o_ps.sem, 1)

            def attended_T(hp):
                pe.wait_ge(*D_o_sb(p, ROWS * hp + ROWS))
                pe.wait_ge(*D_t_ok(p, min(2 * hp + 6, 2 * HP)))
                for t in range(TILES):
                    mm = pe.transpose(ps[:, 0, 128 * t:128 * t + 128], D_ao[:, hp % 2, t, :], ident[:])
                mm.then_inc(D_aT_ps.sem, 1)

            project(0, 0)
            project(0, 1)
            for t in range(TILES):
                for half in range(2):
                    n = 2 * t + half
                    if n >= 2:
                        pe.wait_ge(*D_v_sb(p, n - 1))
                    pe.matmul(ps[:, 6 + half, :], D_xT[:, 128 * t:128 * t + 128], D_wv[:, 512 * half:512 * half + 512],
                              start=True, stop=True).then_inc(D_v_ps.sem, 1)
            pe.wait_ge(*D_v_sb(p, 2 * TILES))
            for u in range(UNITS):
                hp, r = heads_of(u)
                scores(u)
                if r == 0 and hp + 1 < HP:
                    project(hp + 1, 0)
                if u >= 1:
                    attend(u - 1)
                if r == 0 and hp + 1 < HP:
                    project(hp + 1, 1)
                if r == 1 and hp >= 1:
                    attended_T(hp - 1)
            attend(UNITS - 1)
            pe.wait_ge(*D_aT_sb(p, HP - 1))
            attended_T(HP - 1)
            pe.wait_ge(*D_aT_sb(p, HP))
            for t in range(TILES):
                for hp in range(HP):
                    mm = pe.matmul(ps[:, 1, 128 * t:128 * t + 128], D_aT[:, hp, 128 * t:128 * t + 128], D_wo[:, hp, :],
                                   start=hp == 0, stop=hp == HP - 1)
            mm.then_inc(D_y_ps.sem, 1)

        def stage_D_scalar(act, p):
            act.wait_ge(*D_xT_ps(p, 1))
            act.activation(D_xT[:], ps[:, 6, :], ACT.Identity, bias=D_beta[:], scale=D_gamma[:]).then_inc(D_xT_sb.sem, 1)
            for n in range(2 * TILES):
                act.wait_ge(*D_v_ps(p, n + 1))
                act.activation(D_v[:, n // 2, 512 * (n % 2):512 * (n % 2) + 512], ps[:, 6 + n % 2, :], ACT.Copy)\
                    .then_inc(D_v_sb.sem, 1)

            def exps(u):
                act.wait_ge(*D_nb_ok(p, u + 1))
                act.wait_ge(*D_pT_ps(p, max(u - 1, 0)))
                act.wait_ge(*D_o_sb(p, max(u - 1, 0)))
                for hh in range(2):
                    for t, keys in ((0, slice(0, 128)), (1, slice(128, KEYS))):
                        ins = act.activation(D_p[:, u % 2, hh, keys], ps[:, 2 + 2 * (u % 2) + hh, keys], ACT.Exp,
                                             bias=D_nb[:, u % 2, t, hh:hh + 1], scale=DH ** -0.5,
                                             accum_out=D_sum[:, u % 2, t, hh:hh + 1])
                ins.then_inc(D_exp.sem, 1)

            def pT_copy(u):
                act.wait_ge(*D_pT_ps(p, u + 1))
                act.wait_ge(*D_o_ps(p, max(u - 1, 0)))
                act.activation(D_pT[:, u % 2], ps[:, 6:8, 0:KEYS], ACT.Copy).then_inc(D_pT_sb.sem, 1)

            def aT_copy(hp):
                act.wait_ge(*D_aT_ps(p, hp + 1))
                act.activation(D_aT[:, hp, :], ps[:, 0, :], ACT.Copy).then_inc(D_aT_sb.sem, 1)

            for u in range(UNITS):
                hp, r = heads_of(u)
                exps(u)
                if u >= 1:
                    pT_copy(u - 1)
                if r == 1 and hp >= 1:
                    aT_copy(hp - 1)
            pT_copy(UNITS - 1)
            aT_copy(HP - 1)

        def stage_D_vector(dve, p, link, moments):
            for r in range(ROWS):
                dve.wait_ge(*x3_ok(p, r + 1))
                moments(r, x3)

            def rope_parts(hp, kind):
                n = 2 * hp + kind
                dve.wait_ge(*D_pr_ps(p, n + 1))
                dve.wait_ge(*D_qk_ok(p, max(n - 1, 0)))
                for b, table in ((0, cos), (1, sin)):
                    ins = dve.tensor_tensor(D_t[:, kind, b, :].rearrange("p (r t) -> p r t", r=ROWS),
                                            ps[:, b, :].rearrange("p (r t) -> p r t", r=ROWS),
                                            table[:].unsqueeze(1).to_broadcast([128, ROWS, SEQ]), ALU.mult)
                ins.then_inc(D_t_ok.sem, 1)

            def maxima(u):
                dve.wait_ge(*D_s_ps(p, u + 1))
                s = ps[:, 2 + 2 * (u % 2):4 + 2 * (u % 2), :]
                dve.tensor_reduce(D_mx[:, u % 2, 0, :], s[:, :, 0:128], AX.X, ALU.max)
                link(dve.tensor_reduce(D_mx[:, u % 2, 1, :], s[:, :, 128:KEYS], AX.X, ALU.max))
                dve.wait_ge(*D_exp(p, max(u - 1, 0)))
                dve.tensor_scalar(D_nb[:, u % 2].rearrange("p t h -> p (t h)"), D_mx[:, u % 2].rearrange("p t h -> p (t h)"),
                                  -DH ** -0.5, None, ALU.mult).then_inc(D_nb_ok.sem, 1)

            def normalise(u):
                hp, r = heads_of(u)
                dve.wait_ge(*D_o_ps(p, u + 1))
                link(dve.reciprocal(D_rs[:, u % 2].rearrange("p t h -> p (t h)"),
                                    D_sum[:, u % 2].rearrange("p t h -> p (t h)")))
                dve.wait_ge(*D_aT_ps(p, max(hp - 1, 0)))
                dst = D_ao[:, hp % 2, 2 * r:2 * r + 2, :].rearrange("p t (h d) -> p h t d", d=DH)
                rs = D_rs[:, u % 2].rearrange("p t h -> p h t").unsqueeze(3).to_broadcast([128, 2, 2, DH])
                dve.tensor_tensor(dst, ps[:, 6:8, KEYS:512].rearrange("p h (t d) -> p h t d", d=DH), rs, ALU.mult)\
                   .then_inc(D_o_sb.sem, 1)

            rope_parts(0, 0)
            rope_parts(0, 1)
            for u in range(UNITS):
                hp, r = heads_of(u)
                maxima(u)
                if r == 0 and hp + 1 < HP:
                    rope_parts(hp + 1, 0)
                if u >= 1:
                    normalise(u - 1)
                if r == 0 and hp + 1 < HP:
                    rope_parts(hp + 1, 1)
            normalise(UNITS - 1)
            dve.wait_ge(*D_y_ps(p, 1))
            link(dve.tensor_tensor(ysum[:].rearrange("p t c -> p (t c)"), ps[:, 1, :],
                                   x3[:].rearrange("p t c -> p (t c)"), ALU.add))
            for r in range(ROWS):
                moments(r)

        def stage_D_gpsimd(pool, p):
            for n in range(2 * HP):
                hp, kind = divmod(n, 2)
                pool.wait_ge(*D_t_ok(p, n + 1))
                pool.wait_ge(*D_s_ps(p, max(ROWS * (hp - 1), 0)))
                pool.tensor_tensor(D_qk[:, hp % 2, kind, :], D_t[:, kind, 0, :], D_t[:, kind, 1, :], ALU.add)\
                    .then_inc(D_qk_ok.sem, 1)

        def stage_E_tensor(pe, p):
            pe.wait_ge(w_F.sem, 16 * len(loads_F))
            for t in range(TILES):
                mm = pe.transpose(ps[:, 5, 128 * t:128 * t + 128], ctx0[:, t, :], ident[:])
            mm.then_inc(E_cT_ps.sem, 1)
            pe.wait_ge(*E_cT_sb(p, 1))
            pe.matmul(ps[:, 0, :], E_w[:], E_cT[:], start=True, stop=True).then_inc(E_k_ps.sem, 1)
            for t in range(TILES):
                mm = pe.matmul(ps[:, 4, 128 * t:128 * t + 128], E_cT[:, 128 * t:128 * t + 128], E_w[:], start=True, stop=True)
            mm.then_inc(E_v_ps.sem, 1)
            for t in range(TILES):
                pe.wait_ge(*x4_ok(p, t // 2 + 1))
                mm = pe.transpose(ps[:, 6, 128 * t:128 * t + 128], x4[:, t, :], ident[:])
            mm.then_inc(E_xT_ps.sem, 1)
            pe.wait_ge(*E_xT_sb(p, 1))
            pe.matmul(ps[:, 1, :], E_w[:], E_xT[:], start=True, stop=True).then_inc(E_q_ps.sem, 1)
            pe.wait_ge(*E_q_sb(p, 1))
            pe.wait_ge(*E_k_sb(p, 1))
            for r in range(ROWS):
                q, k = (x[:, SEQ * r:SEQ * r + SEQ] for x in (E_qT, E_kT))
                pe.matmul(ps[:, 2 + r, 0:128], q[:, 0:128], k[:, 0:128], start=True, stop=False)
                pe.matmul(ps[:, 2 + r, 0:128], identb[:], causalb[:], start=False, stop=True)
                pe.matmul(ps[:, 2 + r, 128:KEYS], q[:, 128:SEQ], k, start=True, stop=False)
                mm = pe.matmul(ps[:, 2 + r, SEQ:KEYS], identb[:], causalb[:], start=False, stop=True)
            mm.then_inc(E_s_ps.sem, 1)
            pe.wait_ge(*E_exp(p, 1))
            for r in range(ROWS):
                for b in range(3):
                    mm = pe.transpose(ps[:, 6 + r, 128 * b:128 * b + 128], E_p[:, r, 128 * b:128 * b + 128], ident[:])
            mm.then_inc(E_pT_ps.sem, 1)
            pe.wait_ge(*E_v_sb(p, 1))
            pe.wait_ge(*E_pT_sb(p, 1))
            for r in range(ROWS):
                pT = [E_pT[:, r, 128 * b:128 * b + 128] for b in range(3)]
                o = ps[:, 5, SEQ * r:SEQ * r + SEQ]
                pe.matmul(o[:, 0:128], pT[0], E_v[:, 2 * r, :], start=True, stop=True)
                pe.matmul(o[:, 128:256], pT[1], E_v[:, 2 * r, :], start=True, stop=False)
                mm = pe.matmul(o[:, 128:256], pT[2], E_v[:, 2 * r + 1, :], start=False, stop=True)
            mm.then_inc(E_y_ps.sem, 1)

        def stage_E_scalar(act, p):
            act.wait_ge(*E_cT_ps(p, 1))
            act.activation(E_cT[:], ps[:, 5, :], ACT.Copy).then_inc(E_cT_sb.sem, 1)
            act.wait_ge(*E_k_ps(p, 1))
            act.activation(E_kT[:], ps[:, 0, :], ACT.Copy).then_inc(E_k_sb.sem, 1)
            act.wait_ge(*E_v_ps(p, 1))
            act.activation(E_v[:].rearrange("p t c -> p (t c)"), ps[:, 4, :], ACT.Copy).then_inc(E_v_sb.sem, 1)
            act.wait_ge(*E_xT_ps(p, 1))
            act.activation(E_xT[:], ps[:, 6, :], ACT.Copy).then_inc(E_xT_sb.sem, 1)
            act.wait_ge(*E_q_ps(p, 1))
            act.activation(E_qT[:], ps[:, 1, :], ACT.Copy).then_inc(E_q_sb.sem, 1)
            act.wait_ge(*E_nb_ok(p, 1))
            for r in range(ROWS):
                for t, keys in ((0, slice(0, 128)), (1, slice(128, KEYS))):
                    ins = act.activation(E_p[:, r, keys], ps[:, 2 + r, keys], ACT.Exp, bias=E_nb[:, t, r:r + 1],
                                         scale=float(DIM ** -0.5), accum_out=E_sum[:, t, r:r + 1])
            ins.then_inc(E_exp.sem, 1)
            act.wait_ge(*E_pT_ps(p, 1))
            act.activation(E_pT[:], ps[:, 6:8, 0:KEYS], ACT.Copy).then_inc(E_pT_sb.sem, 1)

        def stage_E_vector(dve, p, link, moments):
            dve.wait_ge(*E_s_ps(p, 1))
            dve.tensor_reduce(E_mx[:, 0, :], ps[:, 2:4, 0:128], AX.X, ALU.max)
            link(dve.tensor_reduce(E_mx[:, 1, :], ps[:, 2:4, 128:KEYS], AX.X, ALU.max))
            dve.tensor_scalar(E_nb[:].rearrange("p t r -> p (t r)"), E_mx[:].rearrange("p t r -> p (t r)"),
                              -float(DIM ** -0.5), None, ALU.mult).then_inc(E_nb_ok.sem, 1)
            dve.wait_ge(*E_exp(p, 1))
            link(dve.reciprocal(E_rs[:].rearrange("p t r -> p (t r)"), E_sum[:].rearrange("p t r -> p (t r)")))
            dve.wait_ge(*E_y_ps(p, 1))
            dve.wait_ge(*x4_ok(p, ROWS))
            y = ysum[:].rearrange("p (r t) c -> p r t c", r=ROWS)
            link(dve.tensor_tensor(y, ps[:, 5, :].rearrange("p (r t c) -> p r t c", r=ROWS, t=2),
                                   E_rs[:].rearrange("p t r -> p r t").unsqueeze(3).to_broadcast([128, ROWS, 2, DIM]),
                                   ALU.mult))
            link(dve.tensor_tensor(ysum[:], ysum[:], x4[:], ALU.add))
            for r in range(ROWS):
                moments(r)

        def stage_F_tensor(pe, p):
            for t in range(TILES):
                pe.wait_ge(*x5_ok(p, t // 2 + 1))
                mm = pe.transpose(ps[:, 0, 128 * t:128 * t + 128], x5[:, t, :], ident[:])
            mm.then_inc(F_xT_ps.sem, 1)
            pe.wait_ge(*F_xT_sb(p, 1))
            pe.wait_ge(F_chain.sem, 7)
            for t in range(TILES):
                pe.matmul(ps[:, 1 + t, :], F_xT[:, 128 * t:128 * t + 128], F_w1[:], start=True, stop=True)\
                  .then_inc(F_h_ps.sem, 1)
            pe.wait_ge(*F_n_ok(p, TILES))
            for k in range(FF // 128):
                if k >= 2:
                    pe.wait_ge(*F_nT_sb(p, k - 1))
                for t in range(TILES):
                    mm = pe.transpose(ps[:, 5 + k % 2, 128 * t:128 * t + 128], F_h[:, t, 128 * k:128 * k + 128], ident[:])
                mm.then_inc(F_nT_ps.sem, 1)
            pe.wait_ge(*F_nT_sb(p, FF // 128))
            for t in range(TILES):
                for k in range(FF // 128):
                    mm = pe.matmul(ps[:, 7, 128 * t:128 * t + 128], F_nT[:, k, 128 * t:128 * t + 128], F_w2[:, k, :],
                                   start=k == 0, stop=k == FF // 128 - 1)
            mm.then_inc(F_y_ps.sem, 1)

        def stage_F_scalar(act, p):
            act.wait_ge(*F_xT_ps(p, 1))
            act.activation(F_xT[:], ps[:, 0, :], ACT.Copy).then_inc(F_xT_sb.sem, 1)
            for t in range(TILES):
                act.wait_ge(*F_h_ps(p, t + 1))
                act.activation(F_h[:, t, :], ps[:, 1 + t, :], ACT.Gelu).then_inc(F_h_sb.sem, 1)
            for k in range(FF // 128):
                act.wait_ge(*F_nT_ps(p, k + 1))
                act.activation(F_nT[:, k, :], ps[:, 5 + k % 2, :], ACT.Identity, bias=F_lb[:, k:k + 1],
                               scale=F_lw[:, k:k + 1]).then_inc(F_nT_sb.sem, 1)

        def stage_F_vector(dve, p, link, moments):
            for r in range(ROWS):
                dve.wait_ge(*F_h_sb(p, 2 * r + 2))
                dve.wait_ge(*x5_ok(p, ROWS))
                moments(r, F_h)
            dve.wait_ge(*F_y_ps(p, 1))
            link(dve.tensor_tensor(ysum[:].rearrange("p t c -> p (t c)"), ps[:, 7, :],
                                   x5[:].rearrange("p t c -> p (t c)"), ALU.add))
            for r in range(ROWS):
                moments(r)

        def ternary_vector(dve):
            dve.wait_ge(F_tot_ps.sem, 1)
            dve.tensor_scalar(F_thr[:, 0, :], ps[:, 7, 0:2], 1.0 / (DIM * FF), ABS_EPS, ALU.mult, ALU.add)\
               .then_inc(F_chain.sem, 1)
            dve.wait_ge(F_chain.sem, 1)
            dve.tensor_scalar(F_thr[:, 1, :], F_thr[:, 0, :], -0.5, None, ALU.mult).then_inc(F_chain.sem, 1)
            dve.wait_ge(F_chain.sem, 2)
            dve.tensor_scalar(F_thr[:, 0, :], F_thr[:, 0, :], 0.5, None, ALU.mult).then_inc(F_chain.sem, 1)
            dve.wait_ge(F_chain.sem, 3)
            for i, (w, raw) in enumerate(((F_w1[:], F_w1r[:]), (F_w2[:].rearrange("p k c -> p (k c)"),
                                                              F_w2r[:].rearrange("p k c -> p (k c)")))):
                dve.tensor_scalar(w, raw, F_thr[:, 0, i:i + 1], None, ALU.is_gt)
                dve.tensor_scalar(F_abs[:], raw, F_thr[:, 1, i:i + 1], None, ALU.is_lt).then_inc(F_chain.sem, 1)
                dve.wait_ge(F_chain.sem, 4 + 2 * i)
                dve.tensor_tensor(w, w, F_abs[:], ALU.subtract).then_inc(F_chain.sem, 1)
                dve.wait_ge(F_chain.sem, 5 + 2 * i)

        @block.sync
        def _(sp):
            for dst, src in loads_A:
                sp.dma_start(dst[:], src).then_inc(w_A.sem, 16)
            for s in signals:
                if s.per:
                    sp.sem_inc(s.sem, 1)
            for dst, src in loads_B:
                sp.dma_start(dst[:], src).then_inc(w_B.sem, 16)
            for dst, src in loads_C:
                sp.dma_start(dst[:], src).then_inc(w_C.sem, 16)
            for dst, src in loads_D:
                sp.dma_start(dst[:], src).then_inc(w_D.sem, 16)
            for dst, src in loads_F:
                sp.dma_start(dst[:], src).then_inc(w_F.sem, 16)
            with sp.Fori(0, PAIRS) as p:
                sp.wait_ge(*E_cT_ps(p, 0))
                sp.dma_start(ctx0[:], a["ctx"][bass.ds(p * ROWS, ROWS), :, :].rearrange("r (t q) d -> q (r t) d", q=128)).then_inc(c_in.sem, 16)
                sp.wait_ge(*A_y_sb(p, 0))
                sp.dma_start(x0[:], a["x"][bass.ds(p * ROWS, ROWS), :, :].rearrange("r (t q) d -> q (r t) d", q=128)).then_inc(x_in.sem, 16)
                sp.wait_ge(*x6_ok(p, ROWS))
                sp.dma_start(out[bass.ds(p * ROWS, ROWS), :, :].rearrange("r (t q) d -> q (r t) d", q=128), x6[:]).then_inc(out_done.sem, 16)
            sp.wait_ge(out_done.sem, 16 * PAIRS + 1)

        @block.gpsimd
        def _(pool):
            pool.memset(ones[:], 1.0).then_inc(pool_set.sem, 1)
            pool.memset(minus_half[:], -0.5).then_inc(pool_set.sem, 1)
            pool.memset(A_xT[:], 0.0).then_inc(pool_set.sem, 1)
            pool.memset(A_kT[:], 0.0).then_inc(pool_set.sem, 1)
            pool.wait_ge(pool_set.sem, 4)
            pool.wait_ge(w_D.sem, 16 * len(loads_D))
            halves = lambda w: w[:].rearrange("p a (h b d) -> p (a h) b d", b=2, d=DH // 2)
            pool.tensor_scalar(halves(D_wr)[:, :, 0, :], halves(D_w)[:, :, 1, :], -1.0, None, ALU.mult).then_inc(D_wr_ok.sem, 1)
            pool.tensor_copy(halves(D_wr)[:, :, 1, :], halves(D_w)[:, :, 0, :]).then_inc(D_wr_ok.sem, 1)
            with pool.Fori(0, PAIRS) as p:

                def layernorm(dst, r, n, ready, src=ysum, each=False):
                    two = slice(2 * r, 2 * r + 2)
                    wait_alone(pool, pool_set, 4, *moments_ok(p, n))
                    pool.tensor_scalar(rstd[:, two, :], mv[:, two, 1:2], LN_EPS, None, ALU.add)\
                        .then_inc(rstd_ok.sem, 1)
                    pool.wait_ge(*rstd_ok(p, 2 * n - 1))
                    pool.tensor_tensor(rstd[:, two, :], rstd[:, two, :], minus_half[:, 0:2].unsqueeze(2), ALU.pow)\
                        .then_inc(rstd_ok.sem, 1)
                    wait_alone(pool, pool_set, 4, *rstd_ok(p, 2 * n))
                    for t in (2 * r, 2 * r + 1):
                        ins = pool.tensor_scalar(dst[:, t, :], src[:, t, :], mv[:, t, 0:1], rstd[:, t, :],
                                                 ALU.subtract, ALU.mult)
                        if each:
                            ins.then_inc(ready.sem, 1)
                    if not each:
                        ins.then_inc(ready.sem, 1)

                for r in range(ROWS):
                    layernorm(x1, r, r + 1, x1_ok)
                stage_B_gpsimd(pool, p)
                for r in range(ROWS):
                    layernorm(x2, r, 2 + r + 1, x2_ok)
                stage_C_gpsimd(pool, p)
                for r in range(ROWS):
                    layernorm(x3, r, 4 + r + 1, x3_ok)
                for r in range(ROWS):
                    layernorm(D_xn, r, 6 + r + 1, D_xn_ok, x3)
                stage_D_gpsimd(pool, p)
                for r in range(ROWS):
                    layernorm(x4, r, 8 + r + 1, x4_ok)
                for r in range(ROWS):
                    layernorm(x5, r, 10 + r + 1, x5_ok)
                for r in range(ROWS):
                    layernorm(F_h, r, 12 + r + 1, F_n_ok, F_h, each=True)
                for r in range(ROWS):
                    layernorm(x6, r, 14 + r + 1, x6_ok)

        @block.scalar
        def _(act):
            act.wait_ge(w_A.sem, 16 * len(loads_A))
            act.wait_ge(pool_set.sem, 4)
            act.wait_ge(dve_set.sem, 6)
            act.wait_ge(w_F.sem, 16 * len(loads_F))
            for i, raw in enumerate((F_w1r[:], F_w2r[:].rearrange("p k c -> p (k c)"))):
                ins = act.activation(F_abs[:], raw, ACT.Abs, accum_out=F_sum[:, i:i + 1])
                ins.then_inc(F_abs_ok.sem, 1)
                act.wait_ge(F_abs_ok.sem, i + 1)
            with act.Fori(0, PAIRS) as p:
                stage_A_scalar(act, p)
                stage_B_scalar(act, p)
                stage_C_scalar(act, p)
                stage_D_scalar(act, p)
                stage_E_scalar(act, p)
                stage_F_scalar(act, p)

        @block.tensor
        def _(pe):
            pe.wait_ge(w_A.sem, 16 * len(loads_A))
            pe.wait_ge(pool_set.sem, 4)
            pe.wait_ge(dve_set.sem, 6)
            pe.wait_ge(F_abs_ok.sem, 2)
            pe.matmul(ps[:, 7, 0:2], ones[:], F_sum[:], start=True, stop=True).then_inc(F_tot_ps.sem, 1)
            pe.wait_ge(F_chain.sem, 7)
            with pe.Fori(0, PAIRS) as p:
                stage_A_tensor(pe, p)
                stage_B_tensor(pe, p)
                stage_C_tensor(pe, p)
                stage_D_tensor(pe, p)
                stage_E_tensor(pe, p)
                stage_F_tensor(pe, p)

        @block.vector
        def _(dve):
            dve.wait_ge(w_A.sem, 16 * len(loads_A))
            dve.tensor_copy(identb[:], ident[:]).then_inc(dve_set.sem, 1)
            dve.tensor_copy(edgeb[:], edge[:]).then_inc(dve_set.sem, 1)
            dve.tensor_scalar(qbias4[:], qscale4[:], A_bq[:], None, ALU.mult).then_inc(dve_set.sem, 1)
            dve.wait_ge(w_C.sem, 16 * len(loads_C))
            dve.tensor_copy(trib[:], tri[:]).then_inc(dve_set.sem, 1)
            dve.memset(onesb[:], 1.0).then_inc(dve_set.sem, 1)
            dve.wait_ge(w_D.sem, 16 * len(loads_D))
            dve.tensor_copy(causalb[:], causal[:]).then_inc(dve_set.sem, 1)
            dve.wait_ge(w_F.sem, 16 * len(loads_F))
            ternary_vector(dve)
            dve.wait_ge(dve_set.sem, 6)
            with dve.Fori(0, PAIRS) as p:
                links = [0]

                def link(ins, alone=False):
                    links[0] += 1
                    if ins is not None:
                        ins.then_inc(vchain.sem, 1)
                    if alone:
                        wait_alone(dve, dve_set, 6, *vchain(p, links[0]))
                    else:
                        dve.wait_ge(*vchain(p, links[0]))

                def moments(r, src=ysum):
                    for t in (2 * r, 2 * r + 1):
                        ins = dve.bn_stats(stats[:, t, :], src[:, t, :])
                    link(ins, alone=True)
                    for t in (2 * r, 2 * r + 1):
                        ins = dve.bn_aggr(mv[:, t, :], stats[:, t, :])
                    ins.then_inc(moments_ok.sem, 1)

                stage_A_vector(dve, p, link, moments)
                stage_B_vector(dve, p, link, moments)
                stage_C_vector(dve, p, link, moments)
                stage_D_vector(dve, p, link, moments)
                stage_E_vector(dve, p, link, moments)
                stage_F_vector(dve, p, link, moments)
            assert links[0] == VCHAIN, links[0]


ODD_WORDS, EVEN_WORDS = 10368, 16896
VCHAIN = 87
LNS = ROWS * 8


def kernel(**inputs):
    import concourse.bacc as bacc
    from concourse.bass_utils import run_bass_kernel_spmd as run

    arrays = dict(shape_constants())
    i = inputs
    arrays["x"] = i["x"]
    for n in "qkv":
        arrays[f"A_w{n}"] = i[f"L0_attn_W{n}"].T
    arrays["A_bq"], arrays["A_bk"] = i["L0_attn_bq"][:, None], i["L0_attn_bk"][:, None]
    arrays["A_bv"] = i["L0_attn_bv"][None]
    for n in "qo":
        arrays[f"B_w{n}"], arrays[f"B_b{n}"] = i[f"L0_xattn_W{n}"].T, i[f"L0_xattn_b{n}"][None]
    arrays["B_wkv"] = np.concatenate([i["L0_xattn_Wk"].T, i["L0_xattn_Wv"].T], 1)
    arrays["B_bkv"] = np.concatenate([i["L0_xattn_bk"], i["L0_xattn_bv"]])[None]
    arrays["C_wr"] = i["L0_ffn_w_router"]
    arrays["C_wi"] = i["L0_ffn_wi"].transpose(1, 0, 2)
    arrays["C_wo"] = i["L0_ffn_wo"].reshape(EXPERTS, FF // 128, 128, DIM).transpose(2, 0, 1, 3)
    arrays["D_gamma"], arrays["D_beta"] = i["L1_attn_gamma"][:, None], i["L1_attn_beta"][:, None]
    arrays["D_w"] = np.stack([i["L1_attn_Wq"], i["L1_attn_Wkv"][:, :INNER]], 1)
    arrays["D_wv"] = i["L1_attn_Wkv"][:, INNER:]
    arrays["D_wo"] = i["L1_attn_Wo"].reshape(HP, 128, DIM).transpose(1, 0, 2)
    arrays["E_w"] = i["L1_xattn_Wq"].T
    arrays["F_w1"] = i["L1_ffn_W_fc"].T
    arrays["F_w2"] = i["L1_ffn_W_proj"].T.reshape(FF // 128, 128, DIM).transpose(1, 0, 2)
    arrays["F_lw"], arrays["F_lb"] = (i[f"L1_ffn_ln_{n}"].reshape(FF // 128, 128).T for n in "wb")
    arrays["ctx"] = i["ctx_1024"]
    arrays = {k: np.ascontiguousarray(v) for k, v in arrays.items()}
    nc = bacc.Bacc("TRN2", target_bir_lowering=False, num_devices=1)
    aps = {k: nc.dram_tensor(f"in_{k}", v.shape, mybir.dt.from_np(v.dtype), kind="ExternalInput").ap()
           for k, v in arrays.items()}
    out = nc.dram_tensor("out", (BATCH, SEQ, DIM), mybir.dt.float32, kind="ExternalOutput").ap()
    decoder(nc, aps, out)
    r = run(nc, [{f"in_{k}": v for k, v in arrays.items()}], core_ids=[0])
    return r.results[0]["out"]
```

```python
import concourse.bass as bass
from concourse import mybir
from contextlib import ExitStack
import numpy as np

BATCH, SEQ, DIM = 8, 256, 128
ROWS = 2
PAIRS = BATCH // ROWS
TOPK = min(max(1, int(np.log(SEQ + 1))), SEQ)
TILES = ROWS * SEQ // 128
TOK = ROWS * SEQ
LN_EPS = 1e-5
ABS_EPS = 1e-6
DH = 64
INNER = 16 * DH
HP = INNER // 128
KEYS = 128 + SEQ
EXPERTS, CAP, FF = 8, 64, 512
HEADS, HD, CHUNK = 16, DIM // 16, 32
GROUPS = DIM // 32
CPT = 128 // CHUNK
WIN = 3 * CHUNK
PADDED = SEQ + 2 * CHUNK


class Signal:

    def __init__(self, sem, per):
        self.sem, self.per = sem, per

    def __call__(self, p, k):
        return self.sem, p * self.per + k + 1


def wait_alone(eng, first, least, sem, value):
    value = eng.to_reg(value)
    eng.wait_ge(first.sem, least)
    eng.wait_ge(sem, value)


def shape_constants():
    f = np.float32
    c = {}
    c["ident"] = np.eye(128, dtype=f)
    ch = np.arange(128)
    sub = (ch % 32) // HD
    c["qscale4"] = ((sub[:, None] == np.arange(4)) * (1.0 / np.sqrt(HD))).astype(f)
    c["own"] = np.arange(128)[:, None] // CHUNK == np.arange(4)
    c["fold"] = np.arange(128)[:, None] % CHUNK == np.arange(CHUNK)
    q = np.arange(128) % CHUNK
    edge = np.zeros((128, 2, WIN), f)
    y = np.arange(WIN)
    edge[:, 0] = np.where(y[None] < CHUNK - q[:, None], -1e30, 0)
    off = y[None] - (2 * CHUNK - 1)
    edge[:, 1] = np.where((off >= 0) & (off >= CHUNK - q[:, None]), -1e30, 0)
    c["edge"] = edge
    valid = np.ones((1, 3, WIN), f)
    valid[0, 0, :CHUNK] = 0
    valid[0, 2, 2 * CHUNK:] = 0
    c["valid"] = valid
    half = SEQ // 2
    n, k = np.arange(SEQ), np.arange(half)
    w = 2 * np.pi / SEQ
    re, im = np.cos(w * n[:, None] * k), -np.sin(w * n[:, None] * k)
    nyq = np.cos(np.pi * n)
    im0 = im.copy()
    im[:, 0] = nyq
    re_n = re.copy()
    re_n[:, 0] = nyq
    tiled = lambda t: t.reshape(2, 128, -1).transpose(1, 0, 2)
    c["F"] = tiled(np.concatenate([re, im], 1))
    c["F_im0"], c["F_reN"] = tiled(im0), tiled(re_n)
    twice = np.where(k == 0, 1.0, 2.0)[:, None] / SEQ
    inv_re, inv_im = re.T * twice, im.T * twice
    c["inv_re"], c["inv_im"] = inv_re, inv_im
    c["corr_re"] = inv_re / HD
    c["corr_re2"] = np.concatenate([nyq[None] / SEQ, inv_re[1:]]) / HD
    c["corr_im"] = np.concatenate([0 * nyq[None], inv_im[1:]]) / HD
    c["dc"] = SEQ * (np.arange(128)[None] == 0)
    inv_freq = (1.0 / (np.float32(10000.0) ** (np.arange(0, DH, 2, dtype=f) / np.float32(DH)))).astype(f)
    ang = (np.arange(SEQ, dtype=f)[:, None] * inv_freq[None]).astype(f).T.astype(np.float64)
    c["cos"], c["sin"] = np.tile(np.cos(ang), (4, 1)), np.tile(np.sin(ang), (4, 1))
    c["causal"] = np.where(np.arange(128)[None] > np.arange(128)[:, None], -1e30, 0)
    c["tri"] = np.triu(np.ones((128, 128)))
    c["iota"] = np.tile(np.arange(SEQ), (128, 1))
    return {k: np.ascontiguousarray(v, dtype=f) for k, v in c.items()}


def decoder(nc, a, out):
    f32, bf16 = mybir.dt.float32, mybir.dt.bfloat16
    ALU, ACT, AX = mybir.AluOpType, mybir.ActivationFunctionType, mybir.AxisListType
    ctx = ExitStack()
    with ctx:
        def sb(name, shape, dt=f32):
            return ctx.enter_context(nc.sbuf_tensor(name, shape, dt))

        class Arena:

            def __init__(self, name, words):
                self.all, self.at, self.words = sb(name, [128, words]), 0, words

            def restart(self):
                self.at = 0

            def __call__(self, shape):
                n = int(np.prod(shape[1:]))
                flat = self.all[0:shape[0], self.at:self.at + n]
                self.at += n
                assert self.at <= self.words, (self.at, self.words)
                names = " ".join("abcd"[:len(shape) - 1])
                return flat.rearrange(f"p ({names}) -> p {names}", **dict(zip("abcd", shape[1:])))

        signals = []

        def signal(name, per):
            signals.append(Signal(ctx.enter_context(nc.semaphore(name)), per))
            return signals[-1]

        ps = ctx.enter_context(nc.psum_tensor("ps", [128, 8, 512], f32))

        odd, even = Arena("odd", ODD_WORDS), Arena("even", EVEN_WORDS)

        ident = sb("ident_sb", [128, 128])
        identb = sb("identb", [128, 128], bf16)
        qscale4 = sb("qscale4_sb", [128, 4])
        qbias4 = sb("qbias4", [128, 4])
        own, fold = sb("own_sb", [128, 4]), sb("fold_sb", [128, CHUNK])
        edge = even([128, 2, WIN])
        edgeb = sb("edgeb", [128, 2, WIN], bf16)
        valid = sb("valid_sb", [1, 3, WIN])
        ones = sb("ones", [128, 128])
        minus_half = sb("minus_half", [128, TILES])
        A_wq, A_wk, A_wv = (sb(f"A_w{n}_sb", [128, 128]) for n in "qkv")
        A_bq, A_bk = sb("A_bq_sb", [128, 1]), sb("A_bk_sb", [128, 1])
        A_bv = sb("A_bv_sb", [1, 128])
        loads_A = [(ident, a["ident"]), (A_wq, a["A_wq"]), (A_wk, a["A_wk"]), (A_wv, a["A_wv"]),
                   (A_bq, a["A_bq"]), (A_bk, a["A_bk"]), (A_bv, a["A_bv"]), (qscale4, a["qscale4"]),
                   (own, a["own"]), (fold, a["fold"]), (edge, a["edge"]), (valid, a["valid"])]

        Fm = sb("F_sb", [128, 2, SEQ])
        F_im0, F_reN = sb("F_im0_sb", [128, 2, 128]), sb("F_reN_sb", [128, 2, 128])
        inv_re, inv_im = sb("inv_re_sb", [128, SEQ]), sb("inv_im_sb", [128, SEQ])
        corr_re, corr_re2, corr_im = (sb(f"{n}_sb", [128, SEQ]) for n in ("corr_re", "corr_re2", "corr_im"))
        dc = sb("dc_sb", [1, 128])
        iota = sb("iota_sb", [128, SEQ])
        B_wq, B_wkv, B_wo = sb("B_wq_sb", [128, 128]), sb("B_wkv_sb", [128, 256]), sb("B_wo_sb", [128, 128])
        B_bq, B_bkv, B_bo = sb("B_bq_sb", [1, 128]), sb("B_bkv_sb", [1, 256]), sb("B_bo_sb", [1, 128])
        loads_B = [(Fm, a["F"]), (F_im0, a["F_im0"]), (F_reN, a["F_reN"]), (inv_re, a["inv_re"]),
                   (inv_im, a["inv_im"]), (corr_re, a["corr_re"]), (corr_re2, a["corr_re2"]),
                   (corr_im, a["corr_im"]), (dc, a["dc"]), (iota, a["iota"]), (B_wq, a["B_wq"]),
                   (B_wkv, a["B_wkv"]), (B_wo, a["B_wo"]), (B_bq, a["B_bq"]), (B_bkv, a["B_bkv"]),
                   (B_bo, a["B_bo"])]

        C_wr = sb("C_wr_sb", [128, EXPERTS])
        C_wi, C_wo = sb("C_wi_sb", [128, EXPERTS, FF]), sb("C_wo_sb", [128, EXPERTS, FF // 128, DIM])
        tri = even([128, 128])
        trib, onesb = sb("trib", [128, 128], bf16), sb("onesb", [128, 128], bf16)
        loads_C = [(C_wr, a["C_wr"]), (tri, a["tri"]), (C_wi, a["C_wi"]), (C_wo, a["C_wo"])]

        D_gamma, D_beta = sb("D_gamma_sb", [128, 1]), sb("D_beta_sb", [128, 1])
        D_w, D_wr = sb("D_w_sb", [128, 2, INNER]), sb("D_wr", [128, 2, INNER])
        D_wv, D_wo = sb("D_wv_sb", [128, INNER]), sb("D_wo_sb", [128, HP, DIM])
        cos, sin = sb("cos_sb", [128, SEQ]), sb("sin_sb", [128, SEQ])
        causal, causalb = even([128, 128]), sb("causalb", [128, 128], bf16)
        loads_D = [(D_gamma, a["D_gamma"]), (D_beta, a["D_beta"]), (D_w, a["D_w"]), (D_wv, a["D_wv"]),
                   (D_wo, a["D_wo"]), (cos, a["cos"]), (sin, a["sin"]), (causal, a["causal"])]
        E_w = sb("E_w_sb", [128, 128])
        F_w1r, F_w2r = even([128, FF]), even([128, FF // 128, DIM])
        F_w1, F_w2 = sb("F_w1", [128, FF]), sb("F_w2", [128, FF // 128, DIM])
        F_abs, F_sum = even([128, FF]), sb("F_sum", [128, 2])
        F_thr = sb("F_thr", [128, 2, 2])
        F_lw, F_lb = sb("F_lw_sb", [128, FF // 128]), sb("F_lb_sb", [128, FF // 128])
        loads_F = [(E_w, a["E_w"]), (F_w1r, a["F_w1"]), (F_w2r, a["F_w2"]), (F_lw, a["F_lw"]), (F_lb, a["F_lb"])]

        x0 = sb("x0", [128, TILES, DIM])
        x1 = sb("x1", [128, TILES, DIM])
        ysum = sb("ysum", [128, TILES, DIM])
        stats = sb("stats", [128, TILES, 6])
        mv = sb("mv", [128, TILES, 2])
        rstd = sb("rstd", [128, TILES, 1])

        A_xT = sb("A_xT", [128, ROWS, PADDED])
        A_kT = sb("A_kT", [128, ROWS, PADDED])
        A_q = odd([128, TOK // CHUNK, 4, CHUNK])
        A_v = odd([WIN, ROWS * SEQ // CHUNK, GROUPS, 33])
        A_p = odd([128, 2, GROUPS, CPT, WIN])
        A_mx = sb("A_mx", [128, 2, GROUPS, CPT])
        A_pT = odd([WIN, CPT, GROUPS, 128])
        A_rs, A_rso = sb("A_rs", [128, 2, 8]), sb("A_rso", [128, 2, 8, 4])
        A_o = odd([128, CPT, GROUPS, 32])

        even.restart()
        ctx0 = sb("ctx0", [128, TILES, DIM])
        x2 = sb("x2", [128, TILES, DIM])
        B_cF, B_xF = even([128, ROWS, SEQ]), even([128, ROWS, SEQ])
        B_kv = even([128, ROWS, 2, 2 * DIM])
        B_prod = even([128, 4, ROWS, DIM])
        B_R = even([128, 4, ROWS * HEADS])
        B_c = even([ROWS * HEADS, SEQ])
        B_top = sb("B_top", [ROWS * HEADS, 8])
        B_idx = sb("B_idx", [ROWS * HEADS, 8], mybir.dt.uint32)
        B_idxf = sb("B_idxf", [ROWS * HEADS, 8])
        B_w, B_e = sb("B_w", [ROWS * HEADS, TOPK]), sb("B_e", [ROWS * HEADS, TOPK])
        B_sum, B_rs = sb("B_sum", [ROWS * HEADS, 1]), sb("B_rs", [ROWS * HEADS, 1])
        B_g = even([ROWS * HEADS, TOPK, SEQ])
        B_gT = even([128, 2, ROWS * HEADS])
        B_G = even([128, 3, ROWS * HEADS])
        B_t = even([128, 4, ROWS, DIM])
        B_O = even([128, 2, ROWS, DIM])
        B_OT = even([128, TOK])

        odd.restart()
        C_xT = odd([128, TOK])
        C_top = sb("C_top", [128, TILES, 8])
        C_idx = sb("C_idx", [128, TILES, 8], mybir.dt.uint32)
        C_idxf = sb("C_idxf", [128, TILES, 2])
        C_m = sb("C_m", [128, TILES, 2, EXPERTS], bf16)
        C_p = odd([128, TILES, EXPERTS])
        C_sum = sb("C_sum", [128, TILES])
        C_mc = odd([128, TILES, 2, EXPERTS])
        C_slot = odd([128, TILES, EXPERTS])
        C_D = odd([128, TILES, EXPERTS, CAP])
        C_cb = odd([128, TILES, EXPERTS, CAP])
        C_in = odd([128, EXPERTS, ROWS, CAP])
        C_cT = odd([128, TILES, 4, 128])
        C_h = odd([128, 2, FF // 128, ROWS * CAP])
        C_eo = odd([128, ROWS, EXPERTS // 2, DIM])
        x3 = odd([128, TILES, DIM])

        even.restart()
        x4 = x1
        D_xn = x2
        D_xT = even([128, TOK])
        D_v = even([128, TILES, INNER])
        D_t = even([128, 2, 2, TOK])
        D_qk = even([128, 2, 2, TOK])
        D_mx, D_nb = sb("D_mx", [128, 2, 2, 2]), sb("D_nb", [128, 2, 2, 2])
        D_sum, D_rs = sb("D_sum", [128, 2, 2, 2]), sb("D_rs", [128, 2, 2, 2])
        D_p = even([128, 2, 2, KEYS])
        D_pT = even([128, 2, 2, KEYS])
        D_ao = even([128, HP, TILES, 128])
        D_aT = even([128, 2, TOK])

        odd.restart()
        x5 = x2
        E_cT, E_xT = odd([128, TOK]), odd([128, TOK])
        E_qT, E_kT = odd([128, TOK]), odd([128, TOK])
        E_v = odd([128, TILES, DIM])
        E_mx, E_nb = odd([128, 2, ROWS]), odd([128, 2, ROWS])
        E_sum, E_rs = odd([128, 2, ROWS]), odd([128, 2, ROWS])
        E_p, E_pT = odd([128, ROWS, KEYS]), odd([128, ROWS, KEYS])

        x6 = ysum
        F_xT = odd([128, TOK])
        F_h = odd([128, TILES, FF])
        F_nT = odd([128, FF // 128, TOK])

        w_A = signal("w_A", 0)
        dve_set, pool_set = signal("dve_set", 0), signal("pool_set", 0)
        x_in = signal("x_in", 16)
        out_done = signal("out_done", 16)
        var_ok, rstd_ok = signal("var_ok", LNS), signal("rstd_ok", LNS)
        vchain = signal("vchain", VCHAIN)
        A_xT_ps, A_xT_sb = signal("A_xT_ps", 1), signal("A_xT_sb", 1)
        A_q_ps, A_k_ps, A_v_ps = signal("A_q_ps", 1), signal("A_k_ps", 1), signal("A_v_ps", 4)
        A_q_sb, A_k_sb, A_v_sb = signal("A_q_sb", 1), signal("A_k_sb", 1), signal("A_v_sb", 4)
        A_s_ps = signal("A_s_ps", TILES)
        A_sub = signal("A_sub", TILES)
        A_exp = signal("A_exp", TILES)
        A_pT_ps, A_pT_sb = signal("A_pT_ps", CPT * TILES), signal("A_pT_sb", CPT * TILES)
        A_ones = signal("A_ones", 1)
        A_o_ps, A_o_sb = signal("A_o_ps", TILES), signal("A_o_sb", TILES)
        A_y_ps, A_y_sb = signal("A_y_ps", TILES), signal("A_y_sb", TILES)
        x1_ok = signal("x1_ok", ROWS)
        w_B, c_in = signal("w_B", 0), signal("c_in", 16)
        B_cF_ps, B_cF_sb = signal("B_cF_ps", 1), signal("B_cF_sb", 1)
        B_kv_ps, B_kv_sb = signal("B_kv_ps", ROWS), signal("B_kv_sb", ROWS)
        B_xF_ps, B_xF_sb = signal("B_xF_ps", 1), signal("B_xF_sb", 1)
        B_q_ps, B_R_ok, B_c_ps = signal("B_q_ps", 1), signal("B_R_ok", 1), signal("B_c_ps", 1)
        B_top_ok, B_exp = signal("B_top_ok", 1), signal("B_exp", 1)
        B_g_ok, B_gT_ps, B_gT_sb = signal("B_g_ok", 1), signal("B_gT_ps", 1), signal("B_gT_sb", 1)
        B_G_ps, B_G_sb = signal("B_G_ps", 1), signal("B_G_sb", 1)
        B_tp, B_Ore, B_Oim = signal("B_tp", 1), signal("B_Ore", 1), signal("B_Oim", 1)
        B_OT_ps, B_OT_sb, B_y_ps, B_y_sb = (signal(n, 1) for n in ("B_OT_ps", "B_OT_sb", "B_y_ps", "B_y_sb"))
        x2_ok = signal("x2_ok", ROWS)
        w_C = signal("w_C", 0)
        C_xT_ps, C_xT_sb, C_lg_ps = signal("C_xT_ps", 1), signal("C_xT_sb", 1), signal("C_lg_ps", 1)
        C_sub, C_exp, C_m_ok, C_pos_ps = (signal(n, 1) for n in ("C_sub", "C_exp", "C_m_ok", "C_pos_ps"))
        C_p_ok, C_D_ok, C_cb_ok = signal("C_p_ok", 1), signal("C_D_ok", TILES), signal("C_cb_ok", TILES)
        C_in_ps, C_in_sb = signal("C_in_ps", ROWS), signal("C_in_sb", ROWS)
        C_cT_ps, C_cT_sb = signal("C_cT_ps", TILES), signal("C_cT_sb", TILES)
        C_h_ps, C_h_sb = signal("C_h_ps", EXPERTS), signal("C_h_sb", EXPERTS)
        C_eo_ps, C_eo_sb = signal("C_eo_ps", 2), signal("C_eo_sb", 2)
        C_y_ps = signal("C_y_ps", 1)
        x3_ok = signal("x3_ok", ROWS)
        w_D, w_F = signal("w_D", 0), signal("w_F", 0)
        F_abs_ok, F_tot_ps, F_chain = signal("F_abs_ok", 0), signal("F_tot_ps", 0), signal("F_chain", 0)
        D_wr_ok = signal("D_wr_ok", 0)
        D_xn_ok = signal("D_xn_ok", ROWS)
        D_xT_ps, D_xT_sb = signal("D_xT_ps", 1), signal("D_xT_sb", 1)
        D_v_ps, D_v_sb = signal("D_v_ps", 2 * TILES), signal("D_v_sb", 2 * TILES)
        D_pr_ps, D_t_ok = signal("D_pr_ps", 2 * HP), signal("D_t_ok", 2 * HP)
        D_qk_ok = signal("D_qk_ok", 2 * HP)
        D_s_ps, D_nb_ok, D_exp = (signal(n, ROWS * HP) for n in ("D_s_ps", "D_nb_ok", "D_exp"))
        D_pT_ps, D_pT_sb, D_o_ps, D_o_sb = (signal(n, ROWS * HP) for n in ("D_pT_ps", "D_pT_sb", "D_o_ps", "D_o_sb"))
        D_aT_ps, D_aT_sb = signal("D_aT_ps", HP), signal("D_aT_sb", HP)
        D_wo_ps = signal("D_wo_ps", HP)
        x4_ok = signal("x4_ok", ROWS)
        E_cT_ps, E_cT_sb, E_xT_ps, E_xT_sb = (signal(n, 1) for n in ("E_cT_ps", "E_cT_sb", "E_xT_ps", "E_xT_sb"))
        E_k_ps, E_k_sb, E_v_ps, E_v_sb, E_q_ps, E_q_sb = \
            (signal(n, 1) for n in ("E_k_ps", "E_k_sb", "E_v_ps", "E_v_sb", "E_q_ps", "E_q_sb"))
        E_s_ps, E_nb_ok, E_exp, E_pT_ps, E_pT_sb, E_y_ps = \
            (signal(n, 1) for n in ("E_s_ps", "E_nb_ok", "E_exp", "E_pT_ps", "E_pT_sb", "E_y_ps"))
        x5_ok = signal("x5_ok", ROWS)
        F_xT_ps, F_xT_sb = signal("F_xT_ps", 1), signal("F_xT_sb", 1)
        F_h_ps, F_h_sb, F_n_ok = signal("F_h_ps", TILES), signal("F_h_sb", TILES), signal("F_n_ok", ROWS)
        F_nT_ps, F_nT_sb = signal("F_nT_ps", FF // 128), signal("F_nT_sb", FF // 128)
        F_y_ps = signal("F_y_ps", 1)
        x6_ok = signal("x6_ok", ROWS)

        block = ctx.enter_context(nc.Block())

        def stage_A_scalar(act, p):
            act.wait_ge(*A_xT_ps(p, 1))
            act.wait_ge(*A_v_ps(p, 0))
            act.activation(A_xT[:, :, CHUNK:CHUNK + SEQ], ps[:, 0, :].rearrange("p (r t) -> p r t", r=ROWS),
                           ACT.Copy).then_inc(A_xT_sb.sem, 1)
            act.wait_ge(*A_q_ps(p, 1))
            act.wait_ge(*A_s_ps(p, 0))
            for hl in range(4):
                last = act.activation(A_q[:, :, hl, :], ps[:, 1, :].rearrange("p (c q) -> p c q", q=CHUNK), ACT.Identity, bias=qbias4[:, hl:hl + 1],
                                      scale=qscale4[:, hl:hl + 1])
            last.then_inc(A_q_sb.sem, 1)
            act.wait_ge(*A_o_ps(p, 0))
            for i in range(4):
                act.wait_ge(*A_v_ps(p, i + 1))
                act.activation(A_v[:, 4 * i:4 * i + 4, :, 0:32],
                               ps[0:WIN, 4 + i, :].rearrange("p (w g c) -> p w g c", g=GROUPS, c=32), ACT.Copy)\
                    .then_inc(A_v_sb.sem, 1)
            for t in range(TILES):
                act.wait_ge(*A_sub(p, t + 1))
                act.activation(A_p[:, t % 2], A_p[:, t % 2], ACT.Exp).then_inc(A_exp.sem, 1)
                act.wait_ge(*A_o_ps(p, t))
                for c in range(CPT):
                    act.wait_ge(*A_pT_ps(p, CPT * t + c + 1))
                    act.activation(A_pT[:, c].rearrange("p g k -> p (g k)"), ps[0:WIN, 4 + c % 2, :], ACT.Copy)\
                        .then_inc(A_pT_sb.sem, 1)

        def stage_A_tensor(pe, p):
            pe.wait_ge(*x_in(p, 16))
            pe.wait_ge(*A_y_sb(p, 0))
            for t in range(TILES):
                mm = pe.transpose(ps[:, 0, 128 * t:128 * t + 128], x0[:, t, :], ident[:])
            mm.then_inc(A_xT_ps.sem, 1)
            pe.wait_ge(*A_xT_sb(p, 1))
            xT = A_xT[:, :, CHUNK:CHUNK + SEQ]
            pe.matmul(ps[:, 1, :], A_wq[:], xT, start=True, stop=True).then_inc(A_q_ps.sem, 1)
            pe.matmul(ps[:, 2, :], A_wk[:], xT, start=True, stop=True).then_inc(A_k_ps.sem, 1)
            for i in range(4):
                for j in range(4):
                    r, c = divmod(4 * i + j, SEQ // CHUNK)
                    dst = ps[0:WIN, 4 + i, 128 * j:128 * j + 128]
                    pe.matmul(dst, A_xT[:, r, CHUNK * c:CHUNK * c + WIN], A_wv[:], start=True, stop=False)
                    mm = pe.matmul(dst, valid[:, (c > 0) + (c == SEQ // CHUNK - 1), :], A_bv[:], start=False, stop=True)
                mm.then_inc(A_v_ps.sem, 1)

            def scores(t):
                pe.wait_ge(*A_sub(p, t))
                for c in range(CPT):
                    r, cc = divmod(CPT * t + c, SEQ // CHUNK)
                    side = 0 if cc == 0 else 1 if cc == SEQ // CHUNK - 1 else None
                    for g in range(GROUPS):
                        part = slice(32 * g, 32 * g + 32)
                        mm = pe.matmul(ps[:, g, WIN * c:WIN * c + WIN], A_q[part, CPT * t + c].rearrange("p h q -> p (h q)"),
                                       A_kT[part, r, CHUNK * cc:CHUNK * cc + WIN],
                                       start=True, stop=side is None)
                    if side is not None:
                        for g in range(GROUPS):
                            mm = pe.matmul(ps[:, g, WIN * c:WIN * c + WIN], identb[:], edgeb[:, side, :],
                                           start=False, stop=True)
                mm.then_inc(A_s_ps.sem, 1)

            def attend(t):
                pe.wait_ge(*A_exp(p, t + 1))

                def turn(c):
                    pe.wait_ge(*A_pT_sb(p, max(CPT * t + c - 1, 0)))
                    for g in range(GROUPS):
                        mm = pe.transpose(ps[0:WIN, 4 + c % 2, 128 * g:128 * g + 128], A_p[:, t % 2, g, c, :], ident[:])
                    mm.then_inc(A_pT_ps.sem, 1)

                turn(0)
                turn(1)
                pe.wait_ge(*A_o_sb(p, t))
                for c in range(CPT):
                    if c == 2:
                        pe.wait_ge(*A_y_sb(p, t))
                    pe.wait_ge(*A_pT_sb(p, CPT * t + c + 1))
                    for g in range(GROUPS):
                        col = 33 * (GROUPS * (c % 2) + g)
                        mm = pe.matmul(ps[:, 6 + c // 2, col:col + 33], A_pT[:, c, g, :], A_v[:, CPT * t + c, g, :],
                                       start=True, stop=True)
                    if c + 2 < CPT:
                        turn(c + 2)
                mm.then_inc(A_o_ps.sem, 1)

            def fold_heads(t):
                pe.wait_ge(*A_o_sb(p, t + 1))
                pe.wait_ge(*A_y_sb(p, t))
                for c in range(CPT):
                    mm = pe.matmul(ps[32 * c:32 * c + 32, 7, 384:512], fold[:], A_o[:, c].rearrange("p g k -> p (g k)"),
                                   start=True, stop=True, tile_position=(0, 32 * c))
                mm.then_inc(A_y_ps.sem, 1)

            pe.wait_ge(*A_q_sb(p, 1))
            pe.wait_ge(*A_k_sb(p, 1))
            scores(0)
            pe.wait_ge(*A_v_sb(p, 4))
            pe.wait_ge(*A_ones(p, 1))
            for t in range(TILES):
                if t + 1 < TILES:
                    scores(t + 1)
                if t >= 1:
                    fold_heads(t - 1)
                attend(t)
            fold_heads(TILES - 1)

        def stage_A_vector(dve, p, link, layernorm):
            dve.wait_ge(*A_k_ps(p, 1))
            dve.wait_ge(*A_s_ps(p, 0))
            dve.tensor_scalar(A_kT[:, :, CHUNK:CHUNK + SEQ], ps[:, 2, :].rearrange("p (r t) -> p r t", r=ROWS),
                              A_bk[:], None, ALU.add).then_inc(A_k_sb.sem, 1)

            def softmax(t):
                dve.wait_ge(*A_s_ps(p, t + 1))
                s = ps[:, 0:GROUPS, 0:CPT * WIN].rearrange("p g (c k) -> p g c k", k=WIN)
                link(dve.tensor_reduce(A_mx[:, t % 2], s, AX.X, ALU.max))
                dve.wait_ge(*A_pT_ps(p, CPT * max(t - 1, 0)))
                dve.tensor_tensor(A_p[:, t % 2], s, A_mx[:, t % 2].unsqueeze(3).to_broadcast([128, GROUPS, CPT, WIN]),
                                  ALU.subtract).then_inc(A_sub.sem, 1)

            def own_heads(t):
                dve.wait_ge(*A_o_ps(p, t + 1))
                o = ps[:, 6:8, 0:2 * GROUPS * 33].rearrange("p b (x k) -> p b x k", k=33)
                link(dve.reciprocal(A_rs[:], o[:, :, :, 32]))
                link(dve.tensor_tensor(A_rso[:].rearrange("p b x h -> p (b x) h"),
                                       A_rs[:].rearrange("p b x -> p (b x)").unsqueeze(2).to_broadcast([128, 16, 4]),
                                       own[:].unsqueeze(1).to_broadcast([128, 16, 4]), ALU.mult))
                dve.wait_ge(*A_y_ps(p, t))
                for b in range(2):
                    ins = dve.tensor_tensor(A_o[:, 2 * b:2 * b + 2].rearrange("p c g (h d) -> p (c g) h d", d=HD),
                                            o[:, b, :, 0:32].rearrange("p x (h d) -> p x h d", d=HD),
                                            A_rso[:, b].unsqueeze(3).to_broadcast([128, 8, 4, HD]), ALU.mult)
                ins.then_inc(A_o_sb.sem, 1)

            def residual(t):
                dve.wait_ge(*A_y_ps(p, t + 1))
                dve.wait_ge(*out_done(p, 0))
                dve.tensor_tensor(ysum[:, t, :], ps[:, 7, 384:512], x0[:, t, :], ALU.add).then_inc(A_y_sb.sem, 1)

            softmax(0)
            for t in range(TILES):
                if t + 1 < TILES:
                    softmax(t + 1)
                if t >= 1:
                    residual(t - 1)
                own_heads(t)
            residual(TILES - 1)
            dve.wait_ge(*A_y_sb(p, TILES))
            layernorm(x1, 1, x1_ok)

        def stage_B_tensor(pe, p):
            pe.wait_ge(w_B.sem, 16 * len(loads_B))
            pe.wait_ge(*c_in(p, 16))
            pe.wait_ge(*A_y_sb(p, TILES))
            for r in range(ROWS):
                for t in range(2):
                    mm = pe.matmul(ps[:, 0, SEQ * r:SEQ * r + SEQ], ctx0[:, 2 * r + t, :], Fm[:, t, :],
                                   start=t == 0, stop=t == 1)
            mm.then_inc(B_cF_ps.sem, 1)
            pe.wait_ge(*B_cF_sb(p, 1))
            for r in range(ROWS):
                for part in range(2):
                    dst = ps[:, 1 + r, 256 * part:256 * part + 256]
                    mm = pe.matmul(dst, B_cF[:, r, 128 * part:128 * part + 128], B_wkv[:], start=True, stop=part == 1)
                    if part == 0:
                        mm = pe.matmul(dst, dc[:], B_bkv[:], start=False, stop=True)
                mm.then_inc(B_kv_ps.sem, 1)
            for r in range(ROWS):
                pe.wait_ge(*x1_ok(p, r + 1))
                for t in range(2):
                    mm = pe.matmul(ps[:, 3, SEQ * r:SEQ * r + SEQ], x1[:, 2 * r + t, :], Fm[:, t, :],
                                   start=t == 0, stop=t == 1)
            mm.then_inc(B_xF_ps.sem, 1)
            pe.wait_ge(*B_xF_sb(p, 1))
            for r in range(ROWS):
                for part in range(2):
                    dst = ps[:, 4, 256 * r + 128 * part:256 * r + 128 * part + 128]
                    mm = pe.matmul(dst, B_xF[:, r, 128 * part:128 * part + 128], B_wq[:], start=True, stop=part == 1)
                    if part == 0:
                        mm = pe.matmul(dst, dc[:], B_bq[:], start=False, stop=True)
            mm.then_inc(B_q_ps.sem, 1)
            pe.wait_ge(*B_R_ok(p, 1))
            corr = ps[0:ROWS * HEADS, 5, 0:SEQ]
            pe.matmul(corr, B_R[:, 0, :], corr_re[:], start=True, stop=False)
            pe.matmul(corr, B_R[:, 1, :], corr_re2[:], start=False, stop=False)
            pe.matmul(corr, B_R[:, 2, :], corr_im[:], start=False, stop=True).then_inc(B_c_ps.sem, 1)
            wait_alone(pe, w_B, 16 * len(loads_B), *B_g_ok(p, 1))
            for t in range(2):
                mm = pe.transpose(ps[:, 6, 32 * t:32 * t + 32], B_g[:, 0, 128 * t:128 * t + 128], ident[0:32, 0:32])
            mm.then_inc(B_gT_ps.sem, 1)
            pe.wait_ge(*B_gT_sb(p, 1))
            for i, table in enumerate((Fm[:, :, 0:128], F_im0[:], F_reN[:])):
                for t in range(2):
                    mm = pe.matmul(ps[:, 7, 32 * i:32 * i + 32], table[:, t, :], B_gT[:, t, :], start=t == 0, stop=t == 1)
            mm.then_inc(B_G_ps.sem, 1)
            pe.wait_ge(*B_Ore(p, 1))
            pe.wait_ge(*B_Oim(p, 1))
            for r in range(ROWS):
                dst = ps[:, 0, SEQ * r:SEQ * r + SEQ]
                pe.matmul(dst, B_O[:, 0, r, :], inv_re[:], start=True, stop=False)
                mm = pe.matmul(dst, B_O[:, 1, r, :], inv_im[:], start=False, stop=True)
            mm.then_inc(B_OT_ps.sem, 1)
            pe.wait_ge(*B_OT_sb(p, 1))
            for t in range(TILES):
                dst = ps[:, 1, 128 * t:128 * t + 128]
                pe.matmul(dst, B_OT[:, 128 * t:128 * t + 128], B_wo[:], start=True, stop=False)
                mm = pe.matmul(dst, ones[0:1, :], B_bo[:], start=False, stop=True)
            mm.then_inc(B_y_ps.sem, 1)

        def stage_B_scalar(act, p):
            act.wait_ge(*B_cF_ps(p, 1))
            act.activation(B_cF[:].rearrange("p r f -> p (r f)"), ps[:, 0, :], ACT.Copy).then_inc(B_cF_sb.sem, 1)
            for r in range(ROWS):
                act.wait_ge(*B_kv_ps(p, r + 1))
                act.activation(B_kv[:, r].rearrange("p a c -> p (a c)"), ps[:, 1 + r, :], ACT.Copy).then_inc(B_kv_sb.sem, 1)
            act.wait_ge(*B_xF_ps(p, 1))
            act.activation(B_xF[:].rearrange("p r f -> p (r f)"), ps[:, 3, :], ACT.Copy).then_inc(B_xF_sb.sem, 1)
            act.wait_ge(*B_top_ok(p, 1))
            act.activation(B_e[:], B_w[:], ACT.Exp, accum_out=B_sum[:]).then_inc(B_exp.sem, 1)
            act.wait_ge(*B_gT_ps(p, 1))
            act.activation(B_gT[:].rearrange("p t c -> p (t c)"), ps[:, 6, 0:64], ACT.Copy).then_inc(B_gT_sb.sem, 1)
            act.wait_ge(*B_G_ps(p, 1))
            act.activation(B_G[:].rearrange("p t c -> p (t c)"), ps[:, 7, 0:96], ACT.Copy).then_inc(B_G_sb.sem, 1)
            act.wait_ge(*B_OT_ps(p, 1))
            act.activation(B_OT[:], ps[:, 0, :], ACT.Copy).then_inc(B_OT_sb.sem, 1)

        def G_times_V(eng, dst, i, part):
            v = B_kv[:, :, part, DIM:].rearrange("p r (h d) -> p r h d", d=HD)
            g = B_G[:, i, :].rearrange("p (r h) -> p r h", r=ROWS).unsqueeze(3).to_broadcast([128, ROWS, HEADS, HD])
            return eng.tensor_tensor(B_t[:, dst].rearrange("p r (h d) -> p r h d", d=HD), v, g, ALU.mult)

        def stage_B_vector(dve, p, link, layernorm):
            dve.wait_ge(*B_q_ps(p, 1))
            dve.wait_ge(*B_kv_sb(p, ROWS))
            q = ps[:, 4, :].rearrange("p (r a c) -> p r a c", r=ROWS, a=2)
            k = B_kv[:, :, :, 0:DIM]
            dve.tensor_tensor(B_prod[:, 0:2].rearrange("p a r c -> p r a c"), q, k, ALU.mult)
            dve.tensor_tensor(B_prod[:, 2], q[:, :, 1, :], k[:, :, 0, :], ALU.mult)
            link(dve.tensor_tensor(B_prod[:, 3], q[:, :, 0, :], k[:, :, 1, :], ALU.mult))
            link(dve.tensor_reduce(B_R[:].rearrange("p k h -> p (k h)"),
                                   B_prod[:].rearrange("p k r (h d) -> p (k r h) d", d=HD), AX.X, ALU.add))
            dve.tensor_tensor(B_R[:, 2, :], B_R[:, 2, :], B_R[:, 3, :], ALU.subtract).then_inc(B_R_ok.sem, 1)
            dve.wait_ge(*B_c_ps(p, 1))
            link(dve.tensor_copy(B_c[:], ps[0:ROWS * HEADS, 5, 0:SEQ]), alone=True)
            link(dve.max(B_top[:], B_c[:]), alone=True)
            dve.max_index(B_idx[:], B_top[:], B_c[:]).then_inc(vchain.sem, 1)
            dve.tensor_scalar(B_w[:], B_top[:, 0:TOPK], B_top[:, 0:1], None, ALU.subtract).then_inc(B_top_ok.sem, 1)
            link(None)
            link(dve.tensor_copy(B_idxf[:], B_idx[:]))
            dve.wait_ge(*B_exp(p, 1))
            link(dve.reciprocal(B_rs[:], B_sum[:]))
            link(dve.tensor_scalar(B_e[:], B_e[:], B_rs[:], None, ALU.mult))
            for i in range(TOPK):
                ins = dve.tensor_scalar(B_g[:, i, :], iota[0:ROWS * HEADS, :], B_idxf[:, i:i + 1], B_e[:, i:i + 1],
                                        ALU.is_equal, ALU.mult)
            link(ins)
            dve.tensor_tensor(B_g[:, 0, :], B_g[:, 0, :], B_g[:, 4, :], ALU.add)
            link(dve.tensor_tensor(B_g[:, 1, :], B_g[:, 1, :], B_g[:, 2, :], ALU.add))
            link(dve.tensor_tensor(B_g[:, 0, :], B_g[:, 0, :], B_g[:, 3, :], ALU.add))
            dve.tensor_tensor(B_g[:, 0, :], B_g[:, 0, :], B_g[:, 1, :], ALU.add).then_inc(B_g_ok.sem, 1)
            dve.wait_ge(*B_G_sb(p, 1))
            G_times_V(dve, 0, 0, 0)
            link(G_times_V(dve, 1, 1, 1))
            dve.tensor_tensor(B_O[:, 0], B_t[:, 0], B_t[:, 1], ALU.subtract).then_inc(B_Ore.sem, 1)
            dve.wait_ge(*B_y_ps(p, 1))
            dve.wait_ge(*x1_ok(p, ROWS))
            link(dve.tensor_tensor(ysum[:].rearrange("p t c -> p (t c)"), ps[:, 1, :],
                                   x1[:].rearrange("p t c -> p (t c)"), ALU.add))
            layernorm(x2, 2, x2_ok)

        def stage_B_gpsimd(pool, p):
            pool.wait_ge(*B_G_sb(p, 1))
            G_times_V(pool, 2, 2, 1)
            G_times_V(pool, 3, 1, 0).then_inc(B_tp.sem, 1)
            pool.wait_ge(*B_tp(p, 1))
            pool.tensor_tensor(B_O[:, 1], B_t[:, 2], B_t[:, 3], ALU.add).then_inc(B_Oim.sem, 1)

        def stage_C_tensor(pe, p):
            pe.wait_ge(w_C.sem, 16 * len(loads_C))
            for t in range(TILES):
                pe.wait_ge(*x2_ok(p, t // 2 + 1))
                mm = pe.transpose(ps[:, 2, 128 * t:128 * t + 128], x2[:, t, :], ident[:])
            mm.then_inc(C_xT_ps.sem, 1)
            pe.wait_ge(*C_xT_sb(p, 1))
            for t in range(TILES):
                mm = pe.matmul(ps[:, 3, 8 * t:8 * t + 8], C_xT[:, 128 * t:128 * t + 128], C_wr[:], start=True, stop=True)
            mm.then_inc(C_lg_ps.sem, 1)
            pe.wait_ge(*C_m_ok(p, 1))
            for t in range(TILES):
                t0 = t - t % 2
                dst = ps[:, 4, 16 * t:16 * t + 16]
                both = lambda n: C_m[:, n].rearrange("p k e -> p (k e)")
                pe.matmul(dst, trib[:], both(t), start=True, stop=False)
                if t % 2:
                    pe.matmul(dst, onesb[:], both(t0), start=False, stop=False)
                pe.matmul(dst[:, 8:16], onesb[:], C_m[:, t0, 0], start=False, stop=False)
                mm = pe.matmul(dst[:, 8:16], onesb[:], C_m[:, t0 + 1, 0], start=False, stop=True)
            mm.then_inc(C_pos_ps.sem, 1)
            for r in range(ROWS):
                for t in range(2):
                    pe.wait_ge(*C_D_ok(p, 2 * r + t + 1))
                    mm = pe.matmul(ps[:, 5 + r, :], x2[:, 2 * r + t, :], C_D[:, 2 * r + t].rearrange("p e c -> p (e c)"),
                                   start=t == 0, stop=t == 1)
                mm.then_inc(C_in_ps.sem, 1)

            def combine_T(t):
                pe.wait_ge(*C_cb_ok(p, t + 1))
                if t >= 2:
                    pe.wait_ge(*C_cT_sb(p, t - 1))
                for j in range(4):
                    mm = pe.transpose(ps[:, (7, 0)[t % 2], 128 * j:128 * j + 128],
                                      C_cb[:, t, 2 * j:2 * j + 2, :].rearrange("p e c -> p (e c)"), ident[:])
                mm.then_inc(C_cT_ps.sem, 1)

            def up(e):
                if e >= 2:
                    pe.wait_ge(*C_h_sb(p, e - 1))
                for f in range(FF // 128):
                    mm = pe.matmul(ps[:, 1 + e % 2, 128 * f:128 * f + 128], C_wi[:, e, 128 * f:128 * f + 128],
                                   C_in[:, e].rearrange("p r c -> p (r c)"), start=True, stop=True)
                mm.then_inc(C_h_ps.sem, 1)

            def down(e):
                pe.wait_ge(*C_h_sb(p, e + 1))
                for f in range(FF // 128):
                    mm = pe.matmul(ps[:, 3 + e // 4, 128 * (e % 4):128 * (e % 4) + 128], C_h[:, e % 2, f, :],
                                   C_wo[:, e, f, :], start=f == 0, stop=f == FF // 128 - 1)
                if e % 4 == 3:
                    mm.then_inc(C_eo_ps.sem, 1)

            pe.wait_ge(*C_in_sb(p, ROWS))
            up(0)
            for e in range(EXPERTS):
                if e < TILES:
                    combine_T(e)
                if e + 1 < EXPERTS:
                    up(e + 1)
                down(e)
            pe.wait_ge(*C_cT_sb(p, TILES))
            pe.wait_ge(*C_eo_sb(p, 2))
            for t in range(TILES):
                for j in range(4):
                    mm = pe.matmul(ps[:, 5, 128 * t:128 * t + 128], C_cT[:, t, j, :], C_eo[:, t // 2, j, :],
                                   start=j == 0, stop=j == 3)
            mm.then_inc(C_y_ps.sem, 1)

        def stage_C_scalar(act, p):
            act.wait_ge(*C_xT_ps(p, 1))
            act.activation(C_xT[:], ps[:, 2, :], ACT.Copy).then_inc(C_xT_sb.sem, 1)
            act.wait_ge(*C_sub(p, 1))
            act.activation(C_p[:], C_p[:], ACT.Exp).then_inc(C_exp.sem, 1)
            for r in range(ROWS):
                act.wait_ge(*C_in_ps(p, r + 1))
                act.activation(C_in[:, :, r, :], ps[:, 5 + r, :].rearrange("p (e c) -> p e c", c=CAP), ACT.Copy)\
                    .then_inc(C_in_sb.sem, 1)
            for e in range(EXPERTS):
                act.wait_ge(*C_h_ps(p, e + 1))
                act.activation(C_h[:, e % 2].rearrange("p f s -> p (f s)"), ps[:, 1 + e % 2, :],
                               ACT.Gelu_apprx_tanh).then_inc(C_h_sb.sem, 1)

        def stage_C_vector(dve, p, link, layernorm):
            logits = ps[:, 3, 0:8 * TILES].rearrange("p (t e) -> p t e", e=8)
            wait_alone(dve, dve_set, 6, *C_lg_ps(p, 1))
            for t in range(TILES):
                ins = dve.max(C_top[:, t, :], logits[:, t, :])
            link(ins, alone=True)
            for t in range(TILES):
                ins = dve.max_index(C_idx[:, t, :], C_top[:, t, :], logits[:, t, :])
            ins.then_inc(vchain.sem, 1)
            dve.tensor_tensor(C_p[:], logits, C_top[:, :, 0:1].to_broadcast([128, TILES, EXPERTS]), ALU.subtract)\
               .then_inc(C_sub.sem, 1)
            link(None)
            link(dve.tensor_copy(C_idxf[:], C_idx[:, :, 0:2]))
            dve.tensor_tensor(C_m[:].rearrange("p t k e -> p (t k) e"),
                              iota[:, 0:EXPERTS].unsqueeze(1).to_broadcast([128, 2 * TILES, EXPERTS]),
                              C_idxf[:].rearrange("p t k -> p (t k)").unsqueeze(2).to_broadcast([128, 2 * TILES, EXPERTS]),
                              ALU.is_equal).then_inc(C_m_ok.sem, 1)
            dve.wait_ge(*C_exp(p, 1))
            link(dve.tensor_reduce(C_sum[:], C_p[:], AX.X, ALU.add))
            link(dve.reciprocal(C_sum[:], C_sum[:]))
            dve.tensor_tensor(C_p[:], C_p[:], C_sum[:].unsqueeze(2).to_broadcast([128, TILES, EXPERTS]), ALU.mult)\
               .then_inc(C_p_ok.sem, 1)
            dve.wait_ge(*C_pos_ps(p, 1))
            link(dve.tensor_tensor(C_mc[:].rearrange("p t k e -> p (t k e)"), C_m[:].rearrange("p t k e -> p (t k e)"),
                                   ps[:, 4, 0:16 * TILES], ALU.mult))
            link(dve.tensor_tensor(C_slot[:], C_mc[:, :, 0, :], C_mc[:, :, 1, :], ALU.add))
            for t in range(TILES):
                dve.tensor_tensor(C_D[:, t], iota[:, 1:1 + CAP].unsqueeze(1).to_broadcast([128, EXPERTS, CAP]),
                                  C_slot[:, t, :].unsqueeze(2).to_broadcast([128, EXPERTS, CAP]), ALU.is_equal)\
                   .then_inc(C_D_ok.sem, 1)
            for t in range(TILES):
                dve.wait_ge(*C_cT_ps(p, t + 1))
                dve.tensor_copy(C_cT[:, t].rearrange("p j k -> p (j k)"), ps[:, (7, 0)[t % 2], :]).then_inc(C_cT_sb.sem, 1)
            for half in range(2):
                dve.wait_ge(*C_eo_ps(p, half + 1))
                for r in range(ROWS):
                    for odd in range(2):
                        src = ps[64 * r:64 * r + 64, 3 + half, :].rearrange("p (j o c) -> p j o c", j=2, o=2)
                        ins = dve.tensor_copy(C_eo[64 * odd:64 * odd + 64, r, 2 * half:2 * half + 2, :], src[:, :, odd, :])
                ins.then_inc(C_eo_sb.sem, 1)
            dve.wait_ge(*C_y_ps(p, 1))
            dve.wait_ge(*x2_ok(p, ROWS))
            link(dve.tensor_tensor(ysum[:].rearrange("p t c -> p (t c)"), ps[:, 5, :],
                                   x2[:].rearrange("p t c -> p (t c)"), ALU.add))
            layernorm(x3, 3, x3_ok)

        def stage_C_gpsimd(pool, p):
            pool.wait_ge(*C_p_ok(p, 1))
            for t in range(TILES):
                pool.wait_ge(*C_D_ok(p, t + 1))
                pool.tensor_tensor(C_cb[:, t], C_D[:, t], C_p[:, t, :].unsqueeze(2).to_broadcast([128, EXPERTS, CAP]),
                                   ALU.mult).then_inc(C_cb_ok.sem, 1)

        UNITS = ROWS * HP
        AHEAD = 4

        def heads_of(u):
            hp, r = divmod(u, ROWS)
            return hp, r

        def stage_D_tensor(pe, p):
            pe.wait_ge(w_D.sem, 16 * len(loads_D))
            pe.wait_ge(D_wr_ok.sem, 2)
            for t in range(TILES):
                pe.wait_ge(*D_xn_ok(p, t // 2 + 1))
                mm = pe.transpose(ps[:, 6, 128 * t:128 * t + 128], D_xn[:, t, :], ident[:])
            mm.then_inc(D_xT_ps.sem, 1)
            pe.wait_ge(*D_xT_sb(p, 1))

            def project(hp, kind):
                n = 2 * hp + kind
                pe.wait_ge(*D_t_ok(p, n))
                cols = slice(128 * hp, 128 * hp + 128)
                pe.matmul(ps[:, 0, :], D_w[:, kind, cols], D_xT[:], start=True, stop=True)
                pe.matmul(ps[:, 1, :], D_wr[:, kind, cols], D_xT[:], start=True, stop=True).then_inc(D_pr_ps.sem, 1)

            def scores(u):
                hp, r = heads_of(u)
                pe.wait_ge(*D_qk_ok(p, 2 * hp + 2))
                pe.wait_ge(*D_exp(p, max(u - 1, 0)))
                for hh in range(2):
                    part = slice(64 * hh, 64 * hh + 64)
                    bank = 2 + 2 * (u % 2) + hh
                    q = D_qk[part, hp % 2, 0, SEQ * r:SEQ * r + SEQ]
                    k = D_qk[part, hp % 2, 1, SEQ * r:SEQ * r + SEQ]
                    pe.matmul(ps[:, bank, 0:128], q[:, 0:128], k[:, 0:128], start=True, stop=False)
                    pe.matmul(ps[:, bank, 0:128], identb[:], causalb[:], start=False, stop=True)
                    pe.matmul(ps[:, bank, 128:KEYS], q[:, 128:SEQ], k, start=True, stop=False)
                    mm = pe.matmul(ps[:, bank, SEQ:KEYS], identb[:], causalb[:], start=False, stop=True)
                mm.then_inc(D_s_ps.sem, 1)

            def turn(u):
                pe.wait_ge(*D_exp(p, u + 1))
                pe.wait_ge(*D_o_sb(p, u))
                for hh in range(2):
                    for b in range(3):
                        mm = pe.transpose(ps[:, 6 + hh, 128 * b:128 * b + 128], D_p[:, u % 2, hh, 128 * b:128 * b + 128],
                                          ident[:])
                mm.then_inc(D_pT_ps.sem, 1)

            def attend(u):
                hp, r = heads_of(u)
                pe.wait_ge(*D_pT_sb(p, u + 1))
                for hh in range(2):
                    v = [D_v[:, 2 * r + t, 128 * hp + 64 * hh:128 * hp + 64 * hh + 64] for t in range(2)]
                    pT = [D_pT[:, u % 2, hh, 128 * b:128 * b + 128] for b in range(3)]
                    o = ps[:, 6 + hh, KEYS:512]
                    pe.matmul(o[:, 0:64], pT[0], v[0], start=True, stop=True)
                    pe.matmul(o[:, 64:128], pT[1], v[0], start=True, stop=False)
                    mm = pe.matmul(o[:, 64:128], pT[2], v[1], start=False, stop=True)
                mm.then_inc(D_o_ps.sem, 1)

            for n in range(AHEAD):
                project(*divmod(n, 2))
            for t in range(TILES):
                for half in range(2):
                    n = 2 * t + half
                    if n >= 2:
                        pe.wait_ge(*D_v_sb(p, n - 1))
                    pe.matmul(ps[:, 6 + half, :], D_xT[:, 128 * t:128 * t + 128], D_wv[:, 512 * half:512 * half + 512],
                              start=True, stop=True).then_inc(D_v_ps.sem, 1)
            pe.wait_ge(*D_v_sb(p, 2 * TILES))
            scores(0)
            for u in range(UNITS):
                if u + 1 < UNITS:
                    scores(u + 1)
                turn(u)
                if u + AHEAD < 2 * HP:
                    project(*divmod(u + AHEAD, 2))
                attend(u)
            pe.wait_ge(*D_o_sb(p, UNITS))
            for hp in range(HP + 1):
                if hp < HP:
                    pe.wait_ge(*D_aT_sb(p, max(hp - 1, 0)))
                    for t in range(TILES):
                        mm = pe.transpose(ps[:, hp % 2, 128 * t:128 * t + 128], D_ao[:, hp, t, :], ident[:])
                    mm.then_inc(D_aT_ps.sem, 1)
                if hp > 0:
                    pe.wait_ge(*D_aT_sb(p, hp))
                    for t in range(TILES):
                        mm = pe.matmul(ps[:, 2 + t, 0:128], D_aT[:, (hp - 1) % 2, 128 * t:128 * t + 128],
                                       D_wo[:, hp - 1, :], start=hp == 1, stop=hp == HP)
                    mm.then_inc(D_wo_ps.sem, 1)

        def stage_D_scalar(act, p):
            act.wait_ge(*D_xT_ps(p, 1))
            act.activation(D_xT[:], ps[:, 6, :], ACT.Identity, bias=D_beta[:], scale=D_gamma[:]).then_inc(D_xT_sb.sem, 1)
            for n in range(2 * TILES):
                act.wait_ge(*D_v_ps(p, n + 1))
                act.activation(D_v[:, n // 2, 512 * (n % 2):512 * (n % 2) + 512], ps[:, 6 + n % 2, :], ACT.Copy)\
                    .then_inc(D_v_sb.sem, 1)

            def exps(u):
                act.wait_ge(*D_nb_ok(p, u + 1))
                act.wait_ge(*D_pT_ps(p, max(u - 1, 0)))
                act.wait_ge(*D_o_sb(p, max(u - 1, 0)))
                for hh in range(2):
                    for t, keys in ((0, slice(0, 128)), (1, slice(128, KEYS))):
                        ins = act.activation(D_p[:, u % 2, hh, keys], ps[:, 2 + 2 * (u % 2) + hh, keys], ACT.Exp,
                                             bias=D_nb[:, u % 2, t, hh:hh + 1], scale=DH ** -0.5,
                                             accum_out=D_sum[:, u % 2, t, hh:hh + 1])
                ins.then_inc(D_exp.sem, 1)

            def pT_copy(u):
                act.wait_ge(*D_pT_ps(p, u + 1))
                act.wait_ge(*D_o_ps(p, max(u - 1, 0)))
                act.activation(D_pT[:, u % 2], ps[:, 6:8, 0:KEYS], ACT.Copy).then_inc(D_pT_sb.sem, 1)

            exps(0)
            for u in range(UNITS):
                pT_copy(u)
                if u + 1 < UNITS:
                    exps(u + 1)
            for hp in range(0, HP, 2):
                act.wait_ge(*D_aT_ps(p, hp + 1))
                act.wait_ge(*D_aT_sb(p, hp))
                act.wait_ge(*D_wo_ps(p, max(hp - 1, 0)))
                act.activation(D_aT[:, 0, :], ps[:, 0, :], ACT.Copy).then_inc(D_aT_sb.sem, 1)

        def stage_D_vector(dve, p, link, layernorm):
            layernorm(D_xn, 4, D_xn_ok, x3)

            def rope_parts(hp, kind):
                n = 2 * hp + kind
                dve.wait_ge(*D_pr_ps(p, n + 1))
                dve.wait_ge(*D_qk_ok(p, max(n - 1, 0)))
                for b, table in ((0, cos), (1, sin)):
                    ins = dve.tensor_tensor(D_t[:, kind, b, :].rearrange("p (r t) -> p r t", r=ROWS),
                                            ps[:, b, :].rearrange("p (r t) -> p r t", r=ROWS),
                                            table[:].unsqueeze(1).to_broadcast([128, ROWS, SEQ]), ALU.mult)
                ins.then_inc(D_t_ok.sem, 1)

            def maxima(u):
                dve.wait_ge(*D_s_ps(p, u + 1))
                s = ps[:, 2 + 2 * (u % 2):4 + 2 * (u % 2), :]
                dve.tensor_reduce(D_mx[:, u % 2, 0, :], s[:, :, 0:128], AX.X, ALU.max)
                link(dve.tensor_reduce(D_mx[:, u % 2, 1, :], s[:, :, 128:KEYS], AX.X, ALU.max))
                dve.wait_ge(*D_exp(p, max(u - 1, 0)))
                dve.tensor_scalar(D_nb[:, u % 2].rearrange("p t h -> p (t h)"), D_mx[:, u % 2].rearrange("p t h -> p (t h)"),
                                  -DH ** -0.5, None, ALU.mult).then_inc(D_nb_ok.sem, 1)

            def normalise(u):
                hp, r = heads_of(u)
                dve.wait_ge(*D_o_ps(p, u + 1))
                link(dve.reciprocal(D_rs[:, u % 2].rearrange("p t h -> p (t h)"),
                                    D_sum[:, u % 2].rearrange("p t h -> p (t h)")))
                dst = D_ao[:, hp, 2 * r:2 * r + 2, :].rearrange("p t (h d) -> p h t d", d=DH)
                rs = D_rs[:, u % 2].rearrange("p t h -> p h t").unsqueeze(3).to_broadcast([128, 2, 2, DH])
                dve.tensor_tensor(dst, ps[:, 6:8, KEYS:512].rearrange("p h (t d) -> p h t d", d=DH), rs, ALU.mult)\
                   .then_inc(D_o_sb.sem, 1)

            for n in range(AHEAD):
                rope_parts(*divmod(n, 2))
            maxima(0)
            for u in range(UNITS):
                if u + 1 < UNITS:
                    maxima(u + 1)
                if u + AHEAD < 2 * HP:
                    rope_parts(*divmod(u + AHEAD, 2))
                normalise(u)
            for hp in range(1, HP, 2):
                dve.wait_ge(*D_aT_ps(p, hp + 1))
                dve.wait_ge(*D_aT_sb(p, hp))
                dve.wait_ge(*D_wo_ps(p, max(hp - 1, 0)))
                dve.tensor_copy(D_aT[:, 1, :], ps[:, 1, :]).then_inc(D_aT_sb.sem, 1)
            dve.wait_ge(*D_wo_ps(p, HP))
            link(dve.tensor_tensor(ysum[:], ps[:, 2:2 + TILES, 0:128], x3[:], ALU.add))
            layernorm(x4, 5, x4_ok)

        def stage_D_gpsimd(pool, p):
            for n in range(2 * HP):
                hp, kind = divmod(n, 2)
                pool.wait_ge(*D_t_ok(p, n + 1))
                pool.wait_ge(*D_s_ps(p, max(ROWS * (hp - 1), 0)))
                pool.tensor_tensor(D_qk[:, hp % 2, kind, :], D_t[:, kind, 0, :], D_t[:, kind, 1, :], ALU.add)\
                    .then_inc(D_qk_ok.sem, 1)

        def stage_E_tensor(pe, p):
            pe.wait_ge(w_F.sem, 16 * len(loads_F))
            for t in range(TILES):
                mm = pe.transpose(ps[:, 7, 128 * t:128 * t + 128], ctx0[:, t, :], ident[:])
            mm.then_inc(E_cT_ps.sem, 1)
            pe.wait_ge(*E_cT_sb(p, 1))
            pe.matmul(ps[:, 0, :], E_w[:], E_cT[:], start=True, stop=True).then_inc(E_k_ps.sem, 1)
            for t in range(TILES):
                mm = pe.matmul(ps[:, 6, 128 * t:128 * t + 128], E_cT[:, 128 * t:128 * t + 128], E_w[:], start=True, stop=True)
            mm.then_inc(E_v_ps.sem, 1)
            for t in range(TILES):
                pe.wait_ge(*x4_ok(p, t // 2 + 1))
                mm = pe.transpose(ps[:, 1, 128 * t:128 * t + 128], x4[:, t, :], ident[:])
            mm.then_inc(E_xT_ps.sem, 1)
            pe.wait_ge(*E_xT_sb(p, 1))
            pe.matmul(ps[:, 7, :], E_w[:], E_xT[:], start=True, stop=True).then_inc(E_q_ps.sem, 1)
            pe.wait_ge(*E_q_sb(p, 1))
            pe.wait_ge(*E_k_sb(p, 1))
            for r in range(ROWS):
                q, k = (x[:, SEQ * r:SEQ * r + SEQ] for x in (E_qT, E_kT))
                pe.matmul(ps[:, 2 + r, 0:128], q[:, 0:128], k[:, 0:128], start=True, stop=False)
                pe.matmul(ps[:, 2 + r, 0:128], identb[:], causalb[:], start=False, stop=True)
                pe.matmul(ps[:, 2 + r, 128:KEYS], q[:, 128:SEQ], k, start=True, stop=False)
                mm = pe.matmul(ps[:, 2 + r, SEQ:KEYS], identb[:], causalb[:], start=False, stop=True)
            mm.then_inc(E_s_ps.sem, 1)
            pe.wait_ge(*E_exp(p, 1))
            for r in range(ROWS):
                for b in range(3):
                    mm = pe.transpose(ps[:, 4 + r, 128 * b:128 * b + 128], E_p[:, r, 128 * b:128 * b + 128], ident[:])
            mm.then_inc(E_pT_ps.sem, 1)
            pe.wait_ge(*E_v_sb(p, 1))
            pe.wait_ge(*E_pT_sb(p, 1))
            for r in range(ROWS):
                pT = [E_pT[:, r, 128 * b:128 * b + 128] for b in range(3)]
                o = ps[:, 6, SEQ * r:SEQ * r + SEQ]
                pe.matmul(o[:, 0:128], pT[0], E_v[:, 2 * r, :], start=True, stop=True)
                pe.matmul(o[:, 128:256], pT[1], E_v[:, 2 * r, :], start=True, stop=False)
                mm = pe.matmul(o[:, 128:256], pT[2], E_v[:, 2 * r + 1, :], start=False, stop=True)
            mm.then_inc(E_y_ps.sem, 1)

        def stage_E_scalar(act, p):
            act.wait_ge(*E_cT_ps(p, 1))
            act.activation(E_cT[:], ps[:, 7, :], ACT.Copy).then_inc(E_cT_sb.sem, 1)
            act.wait_ge(*E_k_ps(p, 1))
            act.activation(E_kT[:], ps[:, 0, :], ACT.Copy).then_inc(E_k_sb.sem, 1)
            act.wait_ge(*E_v_ps(p, 1))
            act.activation(E_v[:].rearrange("p t c -> p (t c)"), ps[:, 6, :], ACT.Copy).then_inc(E_v_sb.sem, 1)
            act.wait_ge(*E_xT_ps(p, 1))
            act.activation(E_xT[:], ps[:, 1, :], ACT.Copy).then_inc(E_xT_sb.sem, 1)
            act.wait_ge(*E_q_ps(p, 1))
            act.activation(E_qT[:], ps[:, 7, :], ACT.Copy).then_inc(E_q_sb.sem, 1)
            act.wait_ge(*E_nb_ok(p, 1))
            for r in range(ROWS):
                for t, keys in ((0, slice(0, 128)), (1, slice(128, KEYS))):
                    ins = act.activation(E_p[:, r, keys], ps[:, 2 + r, keys], ACT.Exp, bias=E_nb[:, t, r:r + 1],
                                         scale=float(DIM ** -0.5), accum_out=E_sum[:, t, r:r + 1])
            ins.then_inc(E_exp.sem, 1)
            act.wait_ge(*E_pT_ps(p, 1))
            act.activation(E_pT[:], ps[:, 4:6, 0:KEYS], ACT.Copy).then_inc(E_pT_sb.sem, 1)

        def stage_E_vector(dve, p, link, layernorm):
            dve.wait_ge(*E_s_ps(p, 1))
            dve.tensor_reduce(E_mx[:, 0, :], ps[:, 2:4, 0:128], AX.X, ALU.max)
            link(dve.tensor_reduce(E_mx[:, 1, :], ps[:, 2:4, 128:KEYS], AX.X, ALU.max))
            dve.tensor_scalar(E_nb[:].rearrange("p t r -> p (t r)"), E_mx[:].rearrange("p t r -> p (t r)"),
                              -float(DIM ** -0.5), None, ALU.mult).then_inc(E_nb_ok.sem, 1)
            dve.wait_ge(*E_exp(p, 1))
            link(dve.reciprocal(E_rs[:].rearrange("p t r -> p (t r)"), E_sum[:].rearrange("p t r -> p (t r)")))
            dve.wait_ge(*E_y_ps(p, 1))
            dve.wait_ge(*x4_ok(p, ROWS))
            y = ysum[:].rearrange("p (r t) c -> p r t c", r=ROWS)
            link(dve.tensor_tensor(y, ps[:, 6, :].rearrange("p (r t c) -> p r t c", r=ROWS, t=2),
                                   E_rs[:].rearrange("p t r -> p r t").unsqueeze(3).to_broadcast([128, ROWS, 2, DIM]),
                                   ALU.mult))
            link(dve.tensor_tensor(ysum[:], ysum[:], x4[:], ALU.add))
            layernorm(x5, 6, x5_ok)

        def stage_F_tensor(pe, p):
            for t in range(TILES):
                pe.wait_ge(*x5_ok(p, t // 2 + 1))
                mm = pe.transpose(ps[:, 0, 128 * t:128 * t + 128], x5[:, t, :], ident[:])
            mm.then_inc(F_xT_ps.sem, 1)
            pe.wait_ge(*F_xT_sb(p, 1))
            pe.wait_ge(F_chain.sem, 7)
            for t in range(TILES):
                pe.matmul(ps[:, 1 + t, :], F_xT[:, 128 * t:128 * t + 128], F_w1[:], start=True, stop=True)\
                  .then_inc(F_h_ps.sem, 1)
            pe.wait_ge(*F_n_ok(p, ROWS))
            for k in range(FF // 128):
                if k >= 2:
                    pe.wait_ge(*F_nT_sb(p, k - 1))
                for t in range(TILES):
                    mm = pe.transpose(ps[:, 5 + k % 2, 128 * t:128 * t + 128], F_h[:, t, 128 * k:128 * k + 128], ident[:])
                mm.then_inc(F_nT_ps.sem, 1)
            pe.wait_ge(*F_nT_sb(p, FF // 128))
            for t in range(TILES):
                for k in range(FF // 128):
                    mm = pe.matmul(ps[:, 7, 128 * t:128 * t + 128], F_nT[:, k, 128 * t:128 * t + 128], F_w2[:, k, :],
                                   start=k == 0, stop=k == FF // 128 - 1)
            mm.then_inc(F_y_ps.sem, 1)

        def stage_F_scalar(act, p):
            act.wait_ge(*F_xT_ps(p, 1))
            act.activation(F_xT[:], ps[:, 0, :], ACT.Copy).then_inc(F_xT_sb.sem, 1)
            for t in range(TILES):
                act.wait_ge(*F_h_ps(p, t + 1))
                act.activation(F_h[:, t, :], ps[:, 1 + t, :], ACT.Gelu).then_inc(F_h_sb.sem, 1)
            for k in range(FF // 128):
                act.wait_ge(*F_nT_ps(p, k + 1))
                act.activation(F_nT[:, k, :], ps[:, 5 + k % 2, :], ACT.Identity, bias=F_lb[:, k:k + 1],
                               scale=F_lw[:, k:k + 1]).then_inc(F_nT_sb.sem, 1)

        def stage_F_vector(dve, p, link, layernorm):
            dve.wait_ge(*F_h_sb(p, TILES))
            layernorm(F_h, 7, F_n_ok, F_h)
            dve.wait_ge(*F_y_ps(p, 1))
            link(dve.tensor_tensor(ysum[:].rearrange("p t c -> p (t c)"), ps[:, 7, :],
                                   x5[:].rearrange("p t c -> p (t c)"), ALU.add))
            layernorm(x6, 8, x6_ok)

        def ternary_vector(dve):
            dve.wait_ge(F_tot_ps.sem, 1)
            dve.tensor_scalar(F_thr[:, 0, :], ps[:, 7, 0:2], 1.0 / (DIM * FF), ABS_EPS, ALU.mult, ALU.add)\
               .then_inc(F_chain.sem, 1)
            dve.wait_ge(F_chain.sem, 1)
            dve.tensor_scalar(F_thr[:, 1, :], F_thr[:, 0, :], -0.5, None, ALU.mult).then_inc(F_chain.sem, 1)
            dve.wait_ge(F_chain.sem, 2)
            dve.tensor_scalar(F_thr[:, 0, :], F_thr[:, 0, :], 0.5, None, ALU.mult).then_inc(F_chain.sem, 1)
            dve.wait_ge(F_chain.sem, 3)
            for i, (w, raw) in enumerate(((F_w1[:], F_w1r[:]), (F_w2[:].rearrange("p k c -> p (k c)"),
                                                              F_w2r[:].rearrange("p k c -> p (k c)")))):
                dve.tensor_scalar(w, raw, F_thr[:, 0, i:i + 1], None, ALU.is_gt)
                dve.tensor_scalar(F_abs[:], raw, F_thr[:, 1, i:i + 1], None, ALU.is_lt).then_inc(F_chain.sem, 1)
                dve.wait_ge(F_chain.sem, 4 + 2 * i)
                dve.tensor_tensor(w, w, F_abs[:], ALU.subtract).then_inc(F_chain.sem, 1)
                dve.wait_ge(F_chain.sem, 5 + 2 * i)

        @block.sync
        def _(sp):
            for dst, src in loads_A:
                sp.dma_start(dst[:], src).then_inc(w_A.sem, 16)
            for s in signals:
                if s.per:
                    sp.sem_inc(s.sem, 1)
            for dst, src in loads_B:
                sp.dma_start(dst[:], src).then_inc(w_B.sem, 16)
            for dst, src in loads_C:
                sp.dma_start(dst[:], src).then_inc(w_C.sem, 16)
            for dst, src in loads_D:
                sp.dma_start(dst[:], src).then_inc(w_D.sem, 16)
            for dst, src in loads_F:
                sp.dma_start(dst[:], src).then_inc(w_F.sem, 16)
            with sp.Fori(0, PAIRS) as p:
                sp.wait_ge(*E_cT_ps(p, 0))
                sp.dma_start(ctx0[:], a["ctx"][bass.ds(p * ROWS, ROWS), :, :].rearrange("r (t q) d -> q (r t) d", q=128)).then_inc(c_in.sem, 16)
                sp.wait_ge(*A_y_sb(p, 0))
                sp.dma_start(x0[:], a["x"][bass.ds(p * ROWS, ROWS), :, :].rearrange("r (t q) d -> q (r t) d", q=128)).then_inc(x_in.sem, 16)
                sp.wait_ge(*x6_ok(p, ROWS))
                sp.dma_start(out[bass.ds(p * ROWS, ROWS), :, :].rearrange("r (t q) d -> q (r t) d", q=128), x6[:]).then_inc(out_done.sem, 16)
            sp.wait_ge(out_done.sem, 16 * PAIRS + 1)

        @block.gpsimd
        def _(pool):
            pool.memset(ones[:], 1.0).then_inc(pool_set.sem, 1)
            pool.memset(minus_half[:], -0.5).then_inc(pool_set.sem, 1)
            pool.memset(A_xT[:], 0.0).then_inc(pool_set.sem, 1)
            pool.memset(A_kT[:], 0.0).then_inc(pool_set.sem, 1)
            pool.wait_ge(pool_set.sem, 4)
            pool.wait_ge(w_D.sem, 16 * len(loads_D))
            halves = lambda w: w[:].rearrange("p a (h b d) -> p (a h) b d", b=2, d=DH // 2)
            pool.tensor_scalar(halves(D_wr)[:, :, 0, :], halves(D_w)[:, :, 1, :], -1.0, None, ALU.mult).then_inc(D_wr_ok.sem, 1)
            pool.tensor_copy(halves(D_wr)[:, :, 1, :], halves(D_w)[:, :, 0, :]).then_inc(D_wr_ok.sem, 1)
            with pool.Fori(0, PAIRS) as p:

                def power(n):
                    pool.wait_ge(*var_ok(p, n))
                    pool.tensor_tensor(rstd[:], rstd[:], minus_half[:].unsqueeze(2), ALU.pow).then_inc(rstd_ok.sem, 1)

                wait_alone(pool, pool_set, 4, *F_y_ps(p, 0))
                pool.memset(A_v[:, :, :, 32:33], 1.0).then_inc(A_ones.sem, 1)
                power(1)
                stage_B_gpsimd(pool, p)
                power(2)
                stage_C_gpsimd(pool, p)
                power(3)
                power(4)
                stage_D_gpsimd(pool, p)
                for n in range(5, LNS + 1):
                    power(n)

        @block.scalar
        def _(act):
            act.wait_ge(w_A.sem, 16 * len(loads_A))
            act.wait_ge(pool_set.sem, 4)
            act.wait_ge(dve_set.sem, 6)
            act.wait_ge(w_F.sem, 16 * len(loads_F))
            for i, raw in enumerate((F_w1r[:], F_w2r[:].rearrange("p k c -> p (k c)"))):
                ins = act.activation(F_abs[:], raw, ACT.Abs, accum_out=F_sum[:, i:i + 1])
                ins.then_inc(F_abs_ok.sem, 1)
                act.wait_ge(F_abs_ok.sem, i + 1)
            with act.Fori(0, PAIRS) as p:
                stage_A_scalar(act, p)
                stage_B_scalar(act, p)
                stage_C_scalar(act, p)
                stage_D_scalar(act, p)
                stage_E_scalar(act, p)
                stage_F_scalar(act, p)

        @block.tensor
        def _(pe):
            pe.wait_ge(w_A.sem, 16 * len(loads_A))
            pe.wait_ge(pool_set.sem, 4)
            pe.wait_ge(dve_set.sem, 6)
            pe.wait_ge(F_abs_ok.sem, 2)
            pe.matmul(ps[:, 7, 0:2], ones[:], F_sum[:], start=True, stop=True).then_inc(F_tot_ps.sem, 1)
            pe.wait_ge(F_chain.sem, 7)
            with pe.Fori(0, PAIRS) as p:
                stage_A_tensor(pe, p)
                stage_B_tensor(pe, p)
                stage_C_tensor(pe, p)
                stage_D_tensor(pe, p)
                stage_E_tensor(pe, p)
                stage_F_tensor(pe, p)

        @block.vector
        def _(dve):
            dve.wait_ge(w_A.sem, 16 * len(loads_A))
            dve.tensor_copy(identb[:], ident[:]).then_inc(dve_set.sem, 1)
            dve.tensor_copy(edgeb[:], edge[:]).then_inc(dve_set.sem, 1)
            dve.tensor_scalar(qbias4[:], qscale4[:], A_bq[:], None, ALU.mult).then_inc(dve_set.sem, 1)
            dve.wait_ge(w_C.sem, 16 * len(loads_C))
            dve.tensor_copy(trib[:], tri[:]).then_inc(dve_set.sem, 1)
            dve.memset(onesb[:], 1.0).then_inc(dve_set.sem, 1)
            dve.wait_ge(w_D.sem, 16 * len(loads_D))
            dve.tensor_copy(causalb[:], causal[:]).then_inc(dve_set.sem, 1)
            dve.wait_ge(w_F.sem, 16 * len(loads_F))
            ternary_vector(dve)
            dve.wait_ge(dve_set.sem, 6)
            with dve.Fori(0, PAIRS) as p:
                links = [0]

                def link(ins, alone=False):
                    links[0] += 1
                    if ins is not None:
                        ins.then_inc(vchain.sem, 1)
                    if alone:
                        wait_alone(dve, dve_set, 6, *vchain(p, links[0]))
                    else:
                        dve.wait_ge(*vchain(p, links[0]))

                def layernorm(dst, n, ready, src=ysum):
                    for t in range(TILES):
                        ins = dve.bn_stats(stats[:, t, :], src[:, t, :])
                    link(ins, alone=True)
                    for t in range(TILES):
                        ins = dve.bn_aggr(mv[:, t, :], stats[:, t, :])
                    link(ins)
                    dve.tensor_scalar(rstd[:], mv[:, :, 1:2], LN_EPS, None, ALU.add).then_inc(var_ok.sem, 1)
                    dve.wait_ge(*rstd_ok(p, n))
                    for t in range(TILES):
                        ins = dve.tensor_scalar(dst[:, t, :], src[:, t, :], mv[:, t, 0:1], rstd[:, t, :],
                                                ALU.subtract, ALU.mult)
                        if t % 2:
                            ins.then_inc(ready.sem, 1)
                    wait_alone(dve, dve_set, 6, *ready(p, ROWS))

                stage_A_vector(dve, p, link, layernorm)
                stage_B_vector(dve, p, link, layernorm)
                stage_C_vector(dve, p, link, layernorm)
                stage_D_vector(dve, p, link, layernorm)
                stage_E_vector(dve, p, link, layernorm)
                stage_F_vector(dve, p, link, layernorm)
            assert links[0] == VCHAIN, links[0]


ODD_WORDS, EVEN_WORDS = 10368, 16896
VCHAIN = 87
LNS = 8


def kernel(**inputs):
    import concourse.bacc as bacc
    from concourse.bass_utils import run_bass_kernel_spmd as run

    arrays = dict(shape_constants())
    i = inputs
    arrays["x"] = i["x"]
    for n in "qkv":
        arrays[f"A_w{n}"] = i[f"L0_attn_W{n}"].T
    arrays["A_bq"], arrays["A_bk"] = i["L0_attn_bq"][:, None], i["L0_attn_bk"][:, None]
    arrays["A_bv"] = i["L0_attn_bv"][None]
    for n in "qo":
        arrays[f"B_w{n}"], arrays[f"B_b{n}"] = i[f"L0_xattn_W{n}"].T, i[f"L0_xattn_b{n}"][None]
    arrays["B_wkv"] = np.concatenate([i["L0_xattn_Wk"].T, i["L0_xattn_Wv"].T], 1)
    arrays["B_bkv"] = np.concatenate([i["L0_xattn_bk"], i["L0_xattn_bv"]])[None]
    arrays["C_wr"] = i["L0_ffn_w_router"]
    arrays["C_wi"] = i["L0_ffn_wi"].transpose(1, 0, 2)
    arrays["C_wo"] = i["L0_ffn_wo"].reshape(EXPERTS, FF // 128, 128, DIM).transpose(2, 0, 1, 3)
    arrays["D_gamma"], arrays["D_beta"] = i["L1_attn_gamma"][:, None], i["L1_attn_beta"][:, None]
    arrays["D_w"] = np.stack([i["L1_attn_Wq"], i["L1_attn_Wkv"][:, :INNER]], 1)
    arrays["D_wv"] = i["L1_attn_Wkv"][:, INNER:]
    arrays["D_wo"] = i["L1_attn_Wo"].reshape(HP, 128, DIM).transpose(1, 0, 2)
    arrays["E_w"] = i["L1_xattn_Wq"].T
    arrays["F_w1"] = i["L1_ffn_W_fc"].T
    arrays["F_w2"] = i["L1_ffn_W_proj"].T.reshape(FF // 128, 128, DIM).transpose(1, 0, 2)
    arrays["F_lw"], arrays["F_lb"] = (i[f"L1_ffn_ln_{n}"].reshape(FF // 128, 128).T for n in "wb")
    arrays["ctx"] = i["ctx_1024"]
    arrays = {k: np.ascontiguousarray(v) for k, v in arrays.items()}
    nc = bacc.Bacc("TRN2", target_bir_lowering=False, num_devices=1)
    aps = {k: nc.dram_tensor(f"in_{k}", v.shape, mybir.dt.from_np(v.dtype), kind="ExternalInput").ap()
           for k, v in arrays.items()}
    out = nc.dram_tensor("out", (BATCH, SEQ, DIM), mybir.dt.float32, kind="ExternalOutput").ap()
    decoder(nc, aps, out)
    r = run(nc, [{f"in_{k}": v for k, v in arrays.items()}], core_ids=[0])
    return r.results[0]["out"]
```

```python
import concourse.bass as bass
from concourse import mybir
from contextlib import ExitStack
import numpy as np

BATCH, SEQ, DIM = 8, 256, 128
ROWS = 2
PAIRS = BATCH // ROWS
TOPK = min(max(1, int(np.log(SEQ + 1))), SEQ)
TILES = ROWS * SEQ // 128
TOK = ROWS * SEQ
LN_EPS = 1e-5
ABS_EPS = 1e-6
DH = 64
INNER = 16 * DH
HP = INNER // 128
KEYS = 128 + SEQ
EXPERTS, CAP, FF = 8, 64, 512
HEADS, HD, CHUNK = 16, DIM // 16, 32
GROUPS = DIM // 32
CHUNKS = ROWS * SEQ // CHUNK
CPU = 2
A_UNITS = CHUNKS // CPU
SLOTS = 3 * A_UNITS
WIN = 3 * CHUNK
PADDED = SEQ + 2 * CHUNK


class Signal:

    def __init__(self, sem, per):
        self.sem, self.per = sem, per

    def __call__(self, p, k):
        return self.sem, p * self.per + k + 1


def wait_alone(eng, first, least, sem, value):
    if not isinstance(value, int):
        value = eng.to_reg(value)
        eng.wait_ge(first.sem, least)
    eng.wait_ge(sem, value)


def shape_constants():
    f = np.float32
    c = {}
    c["ident"] = np.eye(128, dtype=f)
    ch = np.arange(128)
    c["qscale"] = (ch[:, None] // HD == np.arange(HEADS)) * (1.0 / np.sqrt(HD))
    c["own"] = np.arange(128)[:, None] // CHUNK == np.arange(4)
    c["fold"] = np.arange(128)[:, None] % CHUNK == np.arange(CHUNK)
    q = np.arange(128) % CHUNK
    edge = np.zeros((128, 2, WIN), f)
    y = np.arange(WIN)
    edge[:, 0] = np.where(y[None] < CHUNK - q[:, None], -1e30, 0)
    off = y[None] - (2 * CHUNK - 1)
    edge[:, 1] = np.where((off >= 0) & (off >= CHUNK - q[:, None]), -1e30, 0)
    c["edge"] = edge.reshape(128, 2 * WIN)
    valid = np.ones((1, 3, WIN), f)
    valid[0, 0, :CHUNK] = 0
    valid[0, 2, 2 * CHUNK:] = 0
    c["valid"] = valid
    half = SEQ // 2
    n, k = np.arange(SEQ), np.arange(half)
    w = 2 * np.pi / SEQ
    re, im = np.cos(w * n[:, None] * k), -np.sin(w * n[:, None] * k)
    nyq = np.cos(np.pi * n)
    im0 = im.copy()
    im[:, 0] = nyq
    re_n = re.copy()
    re_n[:, 0] = nyq
    tiled = lambda t: t.reshape(2, 128, -1).transpose(1, 0, 2)
    c["F"] = tiled(np.concatenate([re, im], 1))
    c["F_im0"], c["F_reN"] = tiled(im0), tiled(re_n)
    twice = np.where(k == 0, 1.0, 2.0)[:, None] / SEQ
    inv_re, inv_im = re.T * twice, im.T * twice
    c["inv_re"], c["inv_im"] = inv_re, inv_im
    c["corr_re"] = inv_re / HD
    c["corr_re2"] = np.concatenate([nyq[None] / SEQ, inv_re[1:]]) / HD
    c["corr_im"] = np.concatenate([0 * nyq[None], inv_im[1:]]) / HD
    c["dc"] = SEQ * (np.arange(128)[None] == 0)
    inv_freq = (1.0 / (np.float32(10000.0) ** (np.arange(0, DH, 2, dtype=f) / np.float32(DH)))).astype(f)
    ang = (np.arange(SEQ, dtype=f)[:, None] * inv_freq[None]).astype(f).T.astype(np.float64)
    c["cos"], c["sin"] = np.tile(np.cos(ang), (4, 1)), np.tile(np.sin(ang), (4, 1))
    c["sin"][np.arange(128) % DH >= DH // 2] *= -1
    c["causal"] = np.where(np.arange(128)[None] > np.arange(128)[:, None], -1e30, 0)
    c["tri"] = np.triu(np.ones((128, 128)))
    c["iota"] = np.tile(np.arange(SEQ), (128, 1))
    return {k: np.ascontiguousarray(v, dtype=f) for k, v in c.items()}


def decoder(nc, a, out):
    f32, bf16 = mybir.dt.float32, mybir.dt.bfloat16
    ALU, ACT, AX = mybir.AluOpType, mybir.ActivationFunctionType, mybir.AxisListType
    ctx = ExitStack()
    with ctx:
        def sb(name, shape, dt=f32):
            return ctx.enter_context(nc.sbuf_tensor(name, shape, dt))

        class Arena:

            def __init__(self, name, words):
                self.all, self.at, self.words = sb(name, [128, words]), 0, words

            def restart(self, at=0):
                self.at = at

            def __call__(self, shape):
                n = int(np.prod(shape[1:]))
                flat = self.all[0:shape[0], self.at:self.at + n]
                self.at += n
                assert self.at <= self.words, (self.at, self.words)
                names = " ".join("abcd"[:len(shape) - 1])
                return flat.rearrange(f"p ({names}) -> p {names}", **dict(zip("abcd", shape[1:])))

        signals = []

        def signal(name, per):
            signals.append(Signal(ctx.enter_context(nc.semaphore(name)), per))
            return signals[-1]

        ps = ctx.enter_context(nc.psum_tensor("ps", [128, 8, 512], f32))

        odd, even = Arena("odd", ODD_WORDS), Arena("even", EVEN_WORDS)

        def packed(name, parts):
            whole, at = sb(name + "_sb", [128, sum(PACKS[name].values())]), 0
            views = []
            for width in PACKS[name].values():
                views.append(whole[:, at:at + width])
                at += width
            assert len(views) == parts
            return whole, views

        pack_A, (ident, A_wq, A_wk, A_wv, A_bq, A_bk, qscale, own, fold) = packed("pack_A", 9)
        even.restart(A_Q_WORDS)
        raw_pack = even([128, sum(PACKS["pack_raw"].values())])
        edge, tri, causal = raw_pack[:, 0:2 * WIN], raw_pack[:, 2 * WIN:2 * WIN + 128], raw_pack[:, 2 * WIN + 128:]
        identb = sb("identb", [128, 128], bf16)
        edgeb = sb("edgeb", [128, 2, WIN], bf16)
        valid = sb("valid_sb", [1, 3, WIN])
        ones = sb("ones", [128, 128])
        minus_half = sb("minus_half", [128, 2 * TILES])
        A_bv = sb("A_bv_sb", [1, 128])
        A_vbias = sb("A_vbias", [WIN, 3, 128])
        loads_A = [(pack_A, a["pack_A"]), (raw_pack, a["pack_raw"]), (A_bv, a["A_bv"]), (valid, a["valid"])]

        Fm = sb("F_sb", [128, 2, SEQ])
        F_im0, F_reN = sb("F_im0_sb", [128, 2, 128]), sb("F_reN_sb", [128, 2, 128])
        inv_re, inv_im = sb("inv_re_sb", [128, SEQ]), sb("inv_im_sb", [128, SEQ])
        corr_re, corr_re2, corr_im = (sb(f"{n}_sb", [128, SEQ]) for n in ("corr_re", "corr_re2", "corr_im"))
        dc = sb("dc_sb", [1, 128])
        iota = sb("iota_sb", [128, SEQ])
        B_wq, B_wkv, B_wo = sb("B_wq_sb", [128, 128]), sb("B_wkv_sb", [128, 256]), sb("B_wo_sb", [128, 128])
        B_bq, B_bkv, B_bo = sb("B_bq_sb", [1, 128]), sb("B_bkv_sb", [1, 256]), sb("B_bo_sb", [1, 128])
        loads_B = [(Fm, a["F"]), (F_im0, a["F_im0"]), (F_reN, a["F_reN"]), (inv_re, a["inv_re"]),
                   (inv_im, a["inv_im"]), (corr_re, a["corr_re"]), (corr_re2, a["corr_re2"]),
                   (corr_im, a["corr_im"]), (dc, a["dc"]), (iota, a["iota"]), (B_wq, a["B_wq"]),
                   (B_wkv, a["B_wkv"]), (B_wo, a["B_wo"]), (B_bq, a["B_bq"]), (B_bkv, a["B_bkv"]),
                   (B_bo, a["B_bo"])]

        C_wr = sb("C_wr_sb", [128, EXPERTS])
        C_wi, C_wo = sb("C_wi_sb", [128, EXPERTS, FF]), sb("C_wo_sb", [128, EXPERTS, FF // 128, DIM])
        trib, onesb = sb("trib", [128, 128], bf16), sb("onesb", [128, 128], bf16)
        loads_C = [(C_wr, a["C_wr"]), (C_wi, a["C_wi"]), (C_wo, a["C_wo"])]

        D_gamma, D_beta = sb("D_gamma_sb", [128, 1]), sb("D_beta_sb", [128, 1])
        D_w = sb("D_w_sb", [128, 2, INNER])
        D_wv, D_wo = sb("D_wv_sb", [128, INNER]), sb("D_wo_sb", [128, HP, DIM])
        cos, sin = sb("cos_sb", [128, SEQ]), sb("sin_sb", [128, SEQ])
        causalb = sb("causalb", [128, 128], bf16)
        loads_D = [(D_gamma, a["D_gamma"]), (D_beta, a["D_beta"]), (D_w, a["D_w"]), (D_wv, a["D_wv"]),
                   (D_wo, a["D_wo"]), (cos, a["cos"]), (sin, a["sin"])]
        E_w = sb("E_w_sb", [128, 128])
        F_w1r, F_w2r = even([128, FF]), even([128, FF // 128, DIM])
        F_w1, F_w2 = sb("F_w1", [128, FF]), sb("F_w2", [128, FF // 128, DIM])
        F_abs, F_sum = even([128, FF]), sb("F_sum", [128, 2])
        F_thr = sb("F_thr", [128, 2, 2])
        F_lw, F_lb = sb("F_lw_sb", [128, FF // 128]), sb("F_lb_sb", [128, FF // 128])
        loads_F = [(E_w, a["E_w"]), (F_w1r, a["F_w1"]), (F_w2r, a["F_w2"]), (F_lw, a["F_lw"]), (F_lb, a["F_lb"])]

        x0 = sb("x0", [128, TILES, DIM])
        x1 = sb("x1", [128, TILES, DIM])
        ysum = sb("ysum", [128, TILES, DIM])
        stats = sb("stats", [128, TILES, 6])
        mv = sb("mv", [128, TILES, 2])
        rstd = sb("rstd", [128, 2, TILES])

        A_xT = sb("A_xT", [128, ROWS, PADDED])
        A_kT = sb("A_kT", [128, ROWS, PADDED])
        A_v = odd([WIN, ROWS * SEQ // CHUNK, GROUPS, 33])
        A_p = odd([128, 2, CPU, GROUPS, WIN])
        A_mx = sb("A_mx", [128, 2, CPU * GROUPS])
        A_pT = odd([WIN, 2, CPU, GROUPS, 128])
        A_rs, A_rso = sb("A_rs", [128, 8]), sb("A_rso", [128, 8, 4])
        A_o = sb("A_o", [128, 2, CPU, GROUPS, 32])

        even.restart()
        A_qr = even([128, TOK])
        A_q = even([128, TOK // CHUNK, HEADS, CHUNK])
        after_A_q = even.at
        assert after_A_q == A_Q_WORDS
        ctx0 = sb("ctx0", [128, TILES, DIM])
        x2 = sb("x2", [128, TILES, DIM])
        B_cF, B_xF = even([128, ROWS, SEQ]), even([128, ROWS, SEQ])
        B_kv = even([128, ROWS, 2, 2 * DIM])
        B_prod = even([128, 4, ROWS, DIM])
        B_R = even([128, 4, ROWS * HEADS])
        B_c = even([ROWS * HEADS, SEQ])
        B_top = sb("B_top", [ROWS * HEADS, 8])
        B_idx = sb("B_idx", [ROWS * HEADS, 8], mybir.dt.uint32)
        B_idxf = sb("B_idxf", [ROWS * HEADS, 8])
        B_w, B_e = sb("B_w", [ROWS * HEADS, TOPK]), sb("B_e", [ROWS * HEADS, TOPK])
        B_sum, B_rs = sb("B_sum", [ROWS * HEADS, 1]), sb("B_rs", [ROWS * HEADS, 1])
        B_g = even([ROWS * HEADS, TOPK, SEQ])
        B_gT = even([128, 2, ROWS * HEADS])
        B_G = even([128, 3, ROWS * HEADS])
        B_t = even([128, 4, ROWS, DIM])
        B_O = even([128, 2, ROWS, DIM])
        B_OT = even([128, TOK])
        E_cT = even([128, TOK])

        odd.restart()
        C_xT = even([128, TOK])
        C_top = sb("C_top", [128, TILES, 8])
        C_idx = sb("C_idx", [128, TILES, 8], mybir.dt.uint32)
        C_idxf = sb("C_idxf", [128, TILES, 2])
        C_m = sb("C_m", [128, TILES, 2, EXPERTS], bf16)
        C_p = odd([128, TILES, EXPERTS])
        C_sum = sb("C_sum", [128, TILES])
        C_mc = odd([128, TILES, 2, EXPERTS])
        C_slot = odd([128, TILES, EXPERTS])
        C_D = odd([128, TILES, EXPERTS, CAP])
        even.restart()
        C_cb = even([128, TILES, EXPERTS, CAP])
        C_in = odd([128, EXPERTS, ROWS, CAP])
        C_cT = odd([128, TILES, 4, 128])
        C_h = odd([128, 2, FF // 128, ROWS * CAP])
        C_eo = odd([128, ROWS, EXPERTS // 2, DIM])
        x3 = odd([128, TILES, DIM])

        even.restart()
        x4 = sb("x4", [128, TILES, DIM])
        D_xn = x2
        D_xT = even([128, TOK])
        D_v = even([128, TILES, INNER])
        D_t = even([128, 2, 2, TOK])
        D_sw = sb("D_sw", [128, 2, TOK])
        D_qk = even([128, 2, 2, TOK])
        D_mx, D_nb = sb("D_mx", [128, 2, 2, 2]), sb("D_nb", [128, 2, 2, 2])
        D_sum, D_rs = sb("D_sum", [128, 2, 2, 2]), sb("D_rs", [128, 2, 2, 2])
        D_p = even([128, 2, 2, KEYS])
        D_pT = even([128, 2, 2, KEYS])
        D_ao = even([128, HP, TILES, 128])
        D_aT = even([128, 2, TOK])

        even.restart(after_A_q)
        x5 = x2
        E_xT = even([128, TOK])
        E_qT, E_kT = even([128, TOK]), sb("E_kT", [128, TOK])
        E_v = sb("E_v", [128, TILES, DIM])
        E_mx, E_nb = even([128, 2, ROWS]), even([128, 2, ROWS])
        E_sum, E_rs = even([128, 2, ROWS]), even([128, 2, ROWS])
        E_p, E_pT = even([128, ROWS, KEYS]), even([128, ROWS, KEYS])

        x6 = ysum
        F_xT = even([128, TOK])
        F_h = even([128, TILES, FF])
        F_nT = even([128, FF // 128, TOK])

        w_A = signal("w_A", 0)
        dve_set, pool_set = signal("dve_set", 0), signal("pool_set", 0)
        x_in, x_early = signal("x_in", 16), signal("x_early", 0)
        out_done = signal("out_done", 16)
        var_ok, rstd_ok = signal("var_ok", LNS), signal("rstd_ok", LNS)
        x1_var_ok, x1_rstd_ok = signal("x1_var_ok", 1), signal("x1_rstd_ok", 1)
        vchain = signal("vchain", VCHAIN)
        A_xT_ps, A_xT_sb = signal("A_xT_ps", 1), signal("A_xT_sb", 1)
        A_q_ps, A_k_ps, A_v_ps = signal("A_q_ps", 1), signal("A_k_ps", 1), signal("A_v_ps", 4)
        A_q_sb = signal("A_q_sb", 1)
        A_q_act, A_q_dve, A_q_pool = signal("A_q_act", 1), signal("A_q_dve", 1), signal("A_q_pool", 2)
        A_k_sb, A_v_sb = signal("A_k_sb", 1), signal("A_v_sb", 4)
        A_s_ps = signal("A_s_ps", A_UNITS)
        A_sub = signal("A_sub", A_UNITS)
        A_exp = signal("A_exp", A_UNITS)
        A_pT_ps, A_pT_sb = signal("A_pT_ps", CHUNKS), signal("A_pT_sb", CHUNKS)
        A_ones = signal("A_ones", 1)
        A_o_ps, A_o_sb = signal("A_o_ps", A_UNITS), signal("A_o_sb", A_UNITS)
        A_y_ps, A_y_sb = signal("A_y_ps", A_UNITS), signal("A_y_sb", A_UNITS)
        x1_ok = signal("x1_ok", ROWS)
        w_B, c_in = signal("w_B", 0), signal("c_in", 16)
        B_cF_ps, B_cF_sb = signal("B_cF_ps", 1), signal("B_cF_sb", 1)
        B_kv_ps, B_kv_sb = signal("B_kv_ps", ROWS), signal("B_kv_sb", ROWS)
        B_xF_ps, B_xF_sb = signal("B_xF_ps", 1), signal("B_xF_sb", 1)
        B_q_ps, B_R_ok, B_c_ps = signal("B_q_ps", 1), signal("B_R_ok", 1), signal("B_c_ps", 1)
        B_top_ok, B_exp = signal("B_top_ok", 1), signal("B_exp", 1)
        B_g_ok, B_gT_ps, B_gT_sb = signal("B_g_ok", 1), signal("B_gT_ps", 1), signal("B_gT_sb", 1)
        B_G_ps, B_G_sb = signal("B_G_ps", 1), signal("B_G_sb", 1)
        B_tp, B_Ore, B_Oim = signal("B_tp", 1), signal("B_Ore", 1), signal("B_Oim", 1)
        B_OT_ps, B_OT_sb, B_y_ps, B_y_sb = (signal(n, 1) for n in ("B_OT_ps", "B_OT_sb", "B_y_ps", "B_y_sb"))
        x2_ok = signal("x2_ok", ROWS)
        w_C = signal("w_C", 0)
        C_xT_ps, C_xT_sb, C_lg_ps = signal("C_xT_ps", 1), signal("C_xT_sb", 1), signal("C_lg_ps", 1)
        C_sub, C_exp, C_m_ok, C_pos_ps = (signal(n, 1) for n in ("C_sub", "C_exp", "C_m_ok", "C_pos_ps"))
        C_p_ok, C_D_ok, C_cb_ok = signal("C_p_ok", 1), signal("C_D_ok", TILES), signal("C_cb_ok", TILES)
        C_in_ps, C_in_sb = signal("C_in_ps", ROWS), signal("C_in_sb", ROWS)
        C_cT_ps, C_cT_sb = signal("C_cT_ps", TILES), signal("C_cT_sb", TILES)
        C_h_ps, C_h_sb = signal("C_h_ps", EXPERTS), signal("C_h_sb", EXPERTS)
        C_eo_ps, C_eo_act, C_eo_dve = signal("C_eo_ps", 2), signal("C_eo_act", 2), signal("C_eo_dve", 2)
        C_y_ps = signal("C_y_ps", 1)
        w_D, w_F = signal("w_D", 0), signal("w_F", 0)
        A_vbias_ps = signal("A_vbias_ps", 0)
        F_abs_ok, F_tot_ps, F_chain = signal("F_abs_ok", 0), signal("F_tot_ps", 0), signal("F_chain", 0)
        D_xn_ok = signal("D_xn_ok", ROWS)
        D_xT_ps, D_xT_sb = signal("D_xT_ps", 1), signal("D_xT_sb", 1)
        D_v_ps, D_v_sb = signal("D_v_ps", 2 * TILES), signal("D_v_sb", 2 * TILES)
        D_pr_ps, D_t_ok = signal("D_pr_ps", 2 * HP), signal("D_t_ok", 2 * HP)
        D_sw_ok, D_sin_ok = signal("D_sw_ok", 2 * HP), signal("D_sin_ok", 2 * HP)
        D_qk_ok = signal("D_qk_ok", 2 * HP)
        D_s_ps, D_nb_ok, D_exp = (signal(n, ROWS * HP) for n in ("D_s_ps", "D_nb_ok", "D_exp"))
        D_pT_ps, D_pT_sb, D_o_ps, D_o_sb = (signal(n, ROWS * HP) for n in ("D_pT_ps", "D_pT_sb", "D_o_ps", "D_o_sb"))
        D_aT_ps, D_aT_sb = signal("D_aT_ps", HP), signal("D_aT_sb", HP)
        D_wo_ps = signal("D_wo_ps", HP)
        x4_ok = signal("x4_ok", ROWS)
        E_cT_ps, E_cT_sb = signal("E_cT_ps", 1), signal("E_cT_sb", 1)
        E_k_ps, E_k_sb, E_v_ps, E_v_sb = (signal(n, 1) for n in ("E_k_ps", "E_k_sb", "E_v_ps", "E_v_sb"))
        E_xT_ps, E_xT_sb, E_q_ps, E_q_sb, E_y_ps = \
            (signal(n, ROWS) for n in ("E_xT_ps", "E_xT_sb", "E_q_ps", "E_q_sb", "E_y_ps"))
        E_s_ps, E_nb_ok, E_exp, E_pT_ps, E_pT_sb = \
            (signal(n, 1) for n in ("E_s_ps", "E_nb_ok", "E_exp", "E_pT_ps", "E_pT_sb"))
        x5_ok = signal("x5_ok", ROWS)
        F_xT_ps, F_xT_sb = signal("F_xT_ps", ROWS), signal("F_xT_sb", ROWS)
        F_h_ps, F_h_sb, F_n_ok = signal("F_h_ps", TILES), signal("F_h_sb", TILES), signal("F_n_ok", ROWS)
        F_nT_ps, F_nT_sb = signal("F_nT_ps", FF // 128), signal("F_nT_sb", FF // 128)
        F_y_ps = signal("F_y_ps", ROWS)
        x6_ok = signal("x6_ok", ROWS)

        block = ctx.enter_context(nc.Block())

        def chunk_of(u, c):
            return divmod(CPU * u + c, SEQ // CHUNK)

        def start_A_scalar_q(act, p):
            act.wait_ge(*A_xT_ps(p, 1))
            act.wait_ge(*A_v_ps(p, 0))
            act.activation(A_xT[:, :, CHUNK:CHUNK + SEQ], ps[:, 0, :].rearrange("p (r t) -> p r t", r=ROWS),
                           ACT.Copy).then_inc(A_xT_sb.sem, 1)
            act.wait_ge(*A_q_ps(p, 1))
            act.wait_ge(*A_s_ps(p, 0))
            if not isinstance(p, int):
                act.wait_ge(*D_wo_ps(p - 1, 0))
            act.activation(A_qr[:], ps[:, 2, :], ACT.Identity, bias=A_bq[:]).then_inc(A_q_sb.sem, 1)

        def start_A_scalar_heads(act, p):
            act.wait_ge(*A_q_sb(p, 1))
            for h in range(HEADS // 2):
                ins = act.activation(A_q[:, 0:8, h, :], A_qr[:, 0:SEQ].rearrange("p (c q) -> p c q", q=CHUNK), ACT.Copy,
                                     scale=qscale[:, h:h + 1])
            ins.then_inc(A_q_act.sem, 1)

        def stages_AB_scalar(act, q, p, pieces):

            def exps(u):
                act.wait_ge(*A_sub(q, u + 1))
                act.activation(A_p[:, u % 2], A_p[:, u % 2], ACT.Exp).then_inc(A_exp.sem, 1)

            if q is not None:
                exps(0)
                exps(1)
            for u in range(A_UNITS):
                if q is not None:
                    act.wait_ge(*A_o_ps(q, max(u - 1, 0)))
                    for c in range(CPU):
                        act.wait_ge(*A_pT_ps(q, CPU * u + c + 1))
                        act.activation(A_pT[:, u % 2, c].rearrange("p g k -> p (g k)"), ps[0:WIN, 4 + c, :], ACT.Copy)\
                            .then_inc(A_pT_sb.sem, 1)
                for i in range(3):
                    if i == 2 and q is not None and u + 2 < A_UNITS:
                        exps(u + 2)
                    if pieces[3 * u + i]:
                        pieces[3 * u + i]()

        def start_A_tensor_qk(pe, p, x=x0, come=None):
            pe.wait_ge(*(come or x_in(p, 16)))
            for t in range(TILES):
                mm = pe.transpose(ps[:, 0, 128 * t:128 * t + 128], x[:, t, :], ident[:])
            mm.then_inc(A_xT_ps.sem, 1)
            pe.wait_ge(*A_xT_sb(p, 1))
            xT = A_xT[:, :, CHUNK:CHUNK + SEQ]
            pe.matmul(ps[:, 2, :], A_wq[:], xT, start=True, stop=True).then_inc(A_q_ps.sem, 1)
            pe.matmul(ps[:, 3, :], A_wk[:], xT, start=True, stop=True).then_inc(A_k_ps.sem, 1)

        V_BANKS = (0, 7, 1, 2)

        def start_A_tensor_v(pe, p, half):
            for i in (2 * half, 2 * half + 1):
                for j in range(4):
                    r, c = divmod(4 * i + j, SEQ // CHUNK)
                    mm = pe.matmul(ps[0:WIN, V_BANKS[i], 128 * j:128 * j + 128], A_xT[:, r, CHUNK * c:CHUNK * c + WIN],
                                   A_wv[:], start=True, stop=True)
                mm.then_inc(A_v_ps.sem, 1)

        def A_scores(pe, p, u):
            pe.wait_ge(*A_sub(p, max(u - 1, 0)))
            for c in range(CPU):
                r, cc = chunk_of(u, c)
                bank = 2 * (u % 2) + c
                side = 0 if cc == 0 else 1 if cc == SEQ // CHUNK - 1 else None
                if side is not None:
                    pe.matmul(ps[:, bank, 0:GROUPS * WIN], identb[:],
                              edgeb[:, side, :].unsqueeze(1).to_broadcast([128, GROUPS, WIN]), start=True, stop=False)
                for g in range(GROUPS):
                    mm = pe.matmul(ps[:, bank, WIN * g:WIN * g + WIN],
                                   A_q[:, CPU * u + c, 4 * g:4 * g + 4, :].rearrange("p h q -> p (h q)"),
                                   A_kT[:, r, CHUNK * cc:CHUNK * cc + WIN], start=side is None,
                                   stop=side is None or g == GROUPS - 1)
            mm.then_inc(A_s_ps.sem, 1)

        def start_A_tensor_scores(pe, p):
            pe.wait_ge(*A_k_sb(p, 1))
            pe.wait_ge(*A_q_act(p, 1))
            pe.wait_ge(*A_q_dve(p, 1))
            pe.wait_ge(*A_v_sb(p, 4))
            A_scores(pe, p, 0)
            A_scores(pe, p, 1)

        def fold_heads(pe, q, u):
            pe.wait_ge(*A_o_sb(q, u + 1))
            for c in range(CPU):
                to = 64 * (u % 2) + 32 * c
                mm = pe.matmul(ps[to:to + 32, 6, 384:512], fold[:], A_o[:, u % 2, c].rearrange("p g k -> p (g k)"),
                               start=True, stop=True, tile_position=(0, to))
            mm.then_inc(A_y_ps.sem, 1)

        def stages_AB_tensor(pe, q, p, pieces):

            def turn(u):
                pe.wait_ge(*A_exp(q, u + 1))
                for c in range(CPU):
                    pe.wait_ge(*A_pT_sb(q, max(CPU * (u - 1) + c + 1, 0)))
                    for g in range(GROUPS):
                        mm = pe.transpose(ps[0:WIN, 4 + c, 128 * g:128 * g + 128], A_p[:, u % 2, c, g, :], ident[:])
                    mm.then_inc(A_pT_ps.sem, 1)

            def attend(u):
                pe.wait_ge(*A_y_sb(q, u))
                for c in range(CPU):
                    pe.wait_ge(*A_pT_sb(q, CPU * u + c + 1))
                    for g in range(GROUPS):
                        col = 33 * (GROUPS * c + g)
                        mm = pe.matmul(ps[:, 6, col:col + 33], A_pT[:, u % 2, c, g, :], A_v[:, CPU * u + c, g, :],
                                       start=True, stop=True)
                mm.then_inc(A_o_ps.sem, 1)

            if q is not None:
                pe.wait_ge(*A_v_sb(q, 4))
                if p is not None:
                    pe.wait_ge(*A_ones(p, 0))
            for u in range(A_UNITS):
                if q is not None:
                    turn(u)
                if pieces[3 * u]:
                    pieces[3 * u]()
                if q is not None:
                    if u >= 1:
                        fold_heads(pe, q, u - 1)
                    if u + 2 < A_UNITS:
                        if u + 2 in (A_UNITS // 2, A_UNITS // 2 + 2):
                            pe.wait_ge(*A_q_pool(q, (u + 2) // 2 - 1))
                        A_scores(pe, q, u + 2)
                if pieces[3 * u + 1]:
                    pieces[3 * u + 1]()
                if q is not None:
                    attend(u)
                if pieces[3 * u + 2]:
                    pieces[3 * u + 2]()

        def start_A_gpsimd(pool, p):
            pool.wait_ge(*A_q_sb(p, 1))
            for c in (8, 12):
                q = A_qr[:, CHUNK * c:CHUNK * c + 128].rearrange("p (c q) -> p c q", q=CHUNK)
                pool.tensor_tensor(A_q[:, c:c + 4], q.unsqueeze(2).to_broadcast([128, 4, HEADS, CHUNK]),
                                   qscale[:].unsqueeze(1).unsqueeze(3).to_broadcast([128, 4, HEADS, CHUNK]), ALU.mult)\
                    .then_inc(A_q_pool.sem, 1)

        def start_A_vector_k(dve, p):
            dve.wait_ge(*A_k_ps(p, 1))
            dve.wait_ge(*A_s_ps(p, 0))
            dve.tensor_scalar(A_kT[:, :, CHUNK:CHUNK + SEQ], ps[:, 3, :].rearrange("p (r t) -> p r t", r=ROWS),
                              A_bk[:], None, ALU.add).then_inc(A_k_sb.sem, 1)

        def start_A_vector_heads(dve, p):
            dve.wait_ge(*A_q_sb(p, 1))
            for h in range(HEADS // 2, HEADS):
                ins = dve.tensor_scalar(A_q[:, 0:8, h, :], A_qr[:, 0:SEQ].rearrange("p (c q) -> p c q", q=CHUNK),
                                        qscale[:, h:h + 1], None, ALU.mult)
            ins.then_inc(A_q_dve.sem, 1)

        def start_A_vector_v(dve, p, half):
            dve.wait_ge(*A_o_ps(p, 0))
            for i in (2 * half, 2 * half + 1):
                dve.wait_ge(*A_v_ps(p, i + 1))
                split = ((0, 1, 0), (1, 4, 1)) if i % 2 == 0 else ((0, 3, 1), (3, 4, 2))
                for lo, hi, kind in split:
                    ins = dve.tensor_tensor(
                        A_v[:, 4 * i + lo:4 * i + hi, :, 0:32],
                        ps[0:WIN, V_BANKS[i], 128 * lo:128 * hi].rearrange("p (w g c) -> p w g c", g=GROUPS, c=32),
                        A_vbias[:, kind, :].rearrange("p (g c) -> p g c", g=GROUPS).unsqueeze(1)
                                           .to_broadcast([WIN, hi - lo, GROUPS, 32]), ALU.add)
                ins.then_inc(A_v_sb.sem, 1)

        def A_softmax(dve, p, link, u):
            dve.wait_ge(*A_s_ps(p, u + 1))
            b = 2 * (u % 2)
            s = ps[:, b:b + CPU, 0:GROUPS * WIN].rearrange("p c (g k) -> p c g k", k=WIN)
            mx = A_mx[:, u % 2].rearrange("p (c g) -> p c g", g=GROUPS)
            link(dve.tensor_reduce(mx, s, AX.X, ALU.max))
            dve.wait_ge(*A_pT_ps(p, CPU * max(u - 1, 0)))
            dve.tensor_tensor(A_p[:, u % 2], s, mx.unsqueeze(3).to_broadcast([128, CPU, GROUPS, WIN]),
                              ALU.subtract).then_inc(A_sub.sem, 1)

        def residual_A(dve, q, u):
            dve.wait_ge(*A_y_ps(q, u + 1))
            half = slice(64 * (u % 2), 64 * (u % 2) + 64)
            dve.tensor_tensor(x0[half, u // 2, :], ps[half, 6, 384:512], x0[half, u // 2, :], ALU.add)\
               .then_inc(A_y_sb.sem, 1)

        def stages_AB_vector(dve, q, p, pieces, link):

            def own_heads(u):
                dve.wait_ge(*A_o_ps(q, u + 1))
                o = ps[:, 6, 0:CPU * GROUPS * 33].rearrange("p (x k) -> p x k", k=33)
                link(dve.reciprocal(A_rs[:], o[:, :, 32]))
                link(dve.tensor_tensor(A_rso[:], A_rs[:].unsqueeze(2).to_broadcast([128, 8, 4]),
                                       own[:].unsqueeze(1).to_broadcast([128, 8, 4]), ALU.mult))
                dve.wait_ge(*A_y_ps(q, max(u - 1, 0)))
                dve.tensor_tensor(A_o[:, u % 2].rearrange("p c g (h d) -> p (c g) h d", d=HD),
                                  o[:, :, 0:32].rearrange("p x (h d) -> p x h d", d=HD),
                                  A_rso[:].unsqueeze(3).to_broadcast([128, 8, 4, HD]), ALU.mult).then_inc(A_o_sb.sem, 1)

            if q is not None:
                dve.wait_ge(*x_in(q, 16))
            for u in range(A_UNITS):
                if q is not None:
                    if u >= 1:
                        residual_A(dve, q, u - 1)
                    if u + 2 < A_UNITS:
                        A_softmax(dve, q, link, u + 2)
                    if u + 1 < A_UNITS:
                        own_heads(u)
                for piece in pieces[3 * u:3 * u + 3]:
                    if piece:
                        piece()
            if q is not None:
                own_heads(A_UNITS - 1)

        def B_tensor(pe, p):
            bank = ps[:, 7, :]

            def ctx_spectrum():
                pe.wait_ge(w_B.sem, 16 * len(loads_B))
                pe.wait_ge(*c_in(p, 16))
                pe.wait_ge(*var_ok(p, 0))
                for r in range(ROWS):
                    for t in range(2):
                        mm = pe.matmul(bank[:, SEQ * r:SEQ * r + SEQ], ctx0[:, 2 * r + t, :], Fm[:, t, :],
                                       start=t == 0, stop=t == 1)
                mm.then_inc(B_cF_ps.sem, 1)

            def x_spectrum():
                pe.wait_ge(*x1_ok(p, ROWS))
                pe.wait_ge(*B_cF_sb(p, 1))
                for r in range(ROWS):
                    for t in range(2):
                        mm = pe.matmul(bank[:, SEQ * r:SEQ * r + SEQ], x1[:, 2 * r + t, :], Fm[:, t, :],
                                       start=t == 0, stop=t == 1)
                mm.then_inc(B_xF_ps.sem, 1)

            def kv(r):
                pe.wait_ge(*(B_kv_sb(p, r) if r else B_xF_sb(p, 1)))
                for part in range(2):
                    dst = bank[:, 256 * part:256 * part + 256]
                    mm = pe.matmul(dst, B_cF[:, r, 128 * part:128 * part + 128], B_wkv[:], start=True, stop=part == 1)
                    if part == 0:
                        mm = pe.matmul(dst, dc[:], B_bkv[:], start=False, stop=True)
                mm.then_inc(B_kv_ps.sem, 1)

            def q():
                pe.wait_ge(*B_kv_sb(p, ROWS))
                for r in range(ROWS):
                    for part in range(2):
                        dst = bank[:, 256 * r + 128 * part:256 * r + 128 * part + 128]
                        mm = pe.matmul(dst, B_xF[:, r, 128 * part:128 * part + 128], B_wq[:], start=True, stop=part == 1)
                        if part == 0:
                            mm = pe.matmul(dst, dc[:], B_bq[:], start=False, stop=True)
                mm.then_inc(B_q_ps.sem, 1)

            def correlation():
                pe.wait_ge(*B_R_ok(p, 1))
                corr = bank[0:ROWS * HEADS, 0:SEQ]
                pe.matmul(corr, B_R[:, 0, :], corr_re[:], start=True, stop=False)
                pe.matmul(corr, B_R[:, 1, :], corr_re2[:], start=False, stop=False)
                pe.matmul(corr, B_R[:, 2, :], corr_im[:], start=False, stop=True).then_inc(B_c_ps.sem, 1)

            def shifts_T():
                wait_alone(pe, w_B, 16 * len(loads_B), *B_g_ok(p, 1))
                for t in range(2):
                    mm = pe.transpose(bank[:, 32 * t:32 * t + 32], B_g[:, 0, 128 * t:128 * t + 128], ident[0:32, 0:32])
                mm.then_inc(B_gT_ps.sem, 1)

            def shift_spectrum():
                pe.wait_ge(*B_gT_sb(p, 1))
                for i, table in enumerate((Fm[:, :, 0:128], F_im0[:], F_reN[:])):
                    for t in range(2):
                        mm = pe.matmul(bank[:, 32 * i:32 * i + 32], table[:, t, :], B_gT[:, t, :], start=t == 0, stop=t == 1)
                mm.then_inc(B_G_ps.sem, 1)

            def inverse():
                pe.wait_ge(*B_Ore(p, 1))
                pe.wait_ge(*B_Oim(p, 1))
                for r in range(ROWS):
                    dst = bank[:, SEQ * r:SEQ * r + SEQ]
                    pe.matmul(dst, B_O[:, 0, r, :], inv_re[:], start=True, stop=False)
                    mm = pe.matmul(dst, B_O[:, 1, r, :], inv_im[:], start=False, stop=True)
                mm.then_inc(B_OT_ps.sem, 1)

            def output():
                pe.wait_ge(*B_OT_sb(p, 1))
                for t in range(TILES):
                    dst = bank[:, 128 * t:128 * t + 128]
                    pe.matmul(dst, B_OT[:, 128 * t:128 * t + 128], B_wo[:], start=True, stop=False)
                    mm = pe.matmul(dst, ones[0:1, :], B_bo[:], start=False, stop=True)
                mm.then_inc(B_y_ps.sem, 1)

            return [None, ctx_spectrum, x_spectrum,
                    lambda: kv(0), lambda: kv(1), q,
                    None, None, correlation,
                    None, None, None,
                    None, None, None,
                    None, shifts_T, shift_spectrum,
                    None, None, inverse,
                    None, output, lambda: C_x_T(pe, p)]

        def B_scalar(act, p):
            bank = ps[:, 7, :]

            def ctx_spectrum():
                act.wait_ge(*B_cF_ps(p, 1))
                act.activation(B_cF[:].rearrange("p r f -> p (r f)"), bank, ACT.Copy).then_inc(B_cF_sb.sem, 1)

            def x_spectrum():
                act.wait_ge(*B_xF_ps(p, 1))
                act.activation(B_xF[:].rearrange("p r f -> p (r f)"), bank, ACT.Copy).then_inc(B_xF_sb.sem, 1)

            def kv(r):
                act.wait_ge(*B_kv_ps(p, r + 1))
                act.activation(B_kv[:, r].rearrange("p a c -> p (a c)"), bank, ACT.Copy).then_inc(B_kv_sb.sem, 1)

            def weights():
                act.wait_ge(*B_top_ok(p, 1))
                act.activation(B_e[:], B_w[:], ACT.Exp, accum_out=B_sum[:]).then_inc(B_exp.sem, 1)

            def shifts_T():
                act.wait_ge(*B_gT_ps(p, 1))
                act.activation(B_gT[:].rearrange("p t c -> p (t c)"), bank[:, 0:64], ACT.Copy).then_inc(B_gT_sb.sem, 1)

            def shift_spectrum():
                act.wait_ge(*B_G_ps(p, 1))
                act.activation(B_G[:].rearrange("p t c -> p (t c)"), bank[:, 0:96], ACT.Copy).then_inc(B_G_sb.sem, 1)

            def inverse():
                act.wait_ge(*B_OT_ps(p, 1))
                act.activation(B_OT[:], bank, ACT.Copy).then_inc(B_OT_sb.sem, 1)

            def x2_T():
                act.wait_ge(*C_xT_ps(p, 1))
                act.activation(C_xT[:], bank, ACT.Copy).then_inc(C_xT_sb.sem, 1)

            return [None, ctx_spectrum, x_spectrum,
                    lambda: kv(0), lambda: kv(1), None,
                    None, None, None,
                    None, weights, None,
                    None, None, None,
                    None, shifts_T, shift_spectrum,
                    None, None, inverse,
                    None, None, x2_T]

        def G_times_V(eng, dst, i, part):
            v = B_kv[:, :, part, DIM:].rearrange("p r (h d) -> p r h d", d=HD)
            g = B_G[:, i, :].rearrange("p (r h) -> p r h", r=ROWS).unsqueeze(3).to_broadcast([128, ROWS, HEADS, HD])
            return eng.tensor_tensor(B_t[:, dst].rearrange("p r (h d) -> p r h d", d=HD), v, g, ALU.mult)

        def B_vector(dve, p, link, layernorm):
            def products():
                dve.wait_ge(*B_q_ps(p, 1))
                dve.wait_ge(*B_kv_sb(p, ROWS))
                q = ps[:, 7, :].rearrange("p (r a c) -> p r a c", r=ROWS, a=2)
                k = B_kv[:, :, :, 0:DIM]
                dve.tensor_tensor(B_prod[:, 0:2].rearrange("p a r c -> p r a c"), q, k, ALU.mult)
                dve.tensor_tensor(B_prod[:, 2], q[:, :, 1, :], k[:, :, 0, :], ALU.mult)
                link(dve.tensor_tensor(B_prod[:, 3], q[:, :, 0, :], k[:, :, 1, :], ALU.mult))

            def head_sums():
                link(dve.tensor_reduce(B_R[:].rearrange("p k h -> p (k h)"),
                                       B_prod[:].rearrange("p k r (h d) -> p (k r h) d", d=HD), AX.X, ALU.add))
                dve.tensor_tensor(B_R[:, 2, :], B_R[:, 2, :], B_R[:, 3, :], ALU.subtract).then_inc(B_R_ok.sem, 1)

            def best_lags():
                dve.wait_ge(*B_c_ps(p, 1))
                link(dve.tensor_copy(B_c[:], ps[0:ROWS * HEADS, 7, 0:SEQ]), alone=True)
                link(dve.max(B_top[:], B_c[:]), alone=True)
                dve.max_index(B_idx[:], B_top[:], B_c[:]).then_inc(vchain.sem, 1)
                dve.tensor_scalar(B_w[:], B_top[:, 0:TOPK], B_top[:, 0:1], None, ALU.subtract).then_inc(B_top_ok.sem, 1)
                link(None)

            def lags_as_float():
                link(dve.tensor_copy(B_idxf[:], B_idx[:]))

            def weighted_shifts():
                dve.wait_ge(*B_exp(p, 1))
                link(dve.reciprocal(B_rs[:], B_sum[:]))
                link(dve.tensor_scalar(B_e[:], B_e[:], B_rs[:], None, ALU.mult))
                for i in range(TOPK):
                    ins = dve.tensor_scalar(B_g[:, i, :], iota[0:ROWS * HEADS, :], B_idxf[:, i:i + 1], B_e[:, i:i + 1],
                                            ALU.is_equal, ALU.mult)
                link(ins)

            def sum_shifts():
                dve.tensor_tensor(B_g[:, 0, :], B_g[:, 0, :], B_g[:, 4, :], ALU.add)
                link(dve.tensor_tensor(B_g[:, 1, :], B_g[:, 1, :], B_g[:, 2, :], ALU.add))
                link(dve.tensor_tensor(B_g[:, 0, :], B_g[:, 0, :], B_g[:, 3, :], ALU.add))
                dve.tensor_tensor(B_g[:, 0, :], B_g[:, 0, :], B_g[:, 1, :], ALU.add).then_inc(B_g_ok.sem, 1)

            def real_part():
                dve.wait_ge(*B_G_sb(p, 1))
                G_times_V(dve, 0, 0, 0)
                link(G_times_V(dve, 1, 1, 1))
                dve.tensor_tensor(B_O[:, 0], B_t[:, 0], B_t[:, 1], ALU.subtract).then_inc(B_Ore.sem, 1)

            def output():
                dve.wait_ge(*B_y_ps(p, 1))
                dve.wait_ge(*out_done(p, 0))
                link(dve.tensor_tensor(ysum[:].rearrange("p t c -> p (t c)"), ps[:, 7, :],
                                       x1[:].rearrange("p t c -> p (t c)"), ALU.add))
                layernorm(x2, 1, x2_ok)

            return [None, None, None,
                    None, products, head_sums,
                    None, None, best_lags,
                    None, lags_as_float, weighted_shifts,
                    None, None, sum_shifts,
                    None, None, real_part,
                    None, None, None,
                    output, None, None]

        def stage_B_gpsimd(pool, p):
            pool.wait_ge(*B_G_sb(p, 1))
            G_times_V(pool, 2, 2, 1)
            G_times_V(pool, 3, 1, 0).then_inc(B_tp.sem, 1)
            pool.wait_ge(*B_tp(p, 1))
            pool.tensor_tensor(B_O[:, 1], B_t[:, 2], B_t[:, 3], ALU.add).then_inc(B_Oim.sem, 1)

        def C_x_T(pe, p):
            pe.wait_ge(w_C.sem, 16 * len(loads_C))
            for t in range(TILES):
                pe.wait_ge(*x2_ok(p, t // 2 + 1))
                mm = pe.transpose(ps[:, 7, 128 * t:128 * t + 128], x2[:, t, :], ident[:])
            mm.then_inc(C_xT_ps.sem, 1)

        def stage_C_tensor(pe, p, units):
            if units:
                pe.wait_ge(*A_sub(p + 1, A_UNITS))
            pe.wait_ge(*C_xT_sb(p, 1))
            for t in range(TILES):
                mm = pe.matmul(ps[:, 3, 8 * t:8 * t + 8], C_xT[:, 128 * t:128 * t + 128], C_wr[:], start=True, stop=True)
            mm.then_inc(C_lg_ps.sem, 1)
            if units:
                fold_heads(pe, p + 1, A_UNITS - 1)
            pe.wait_ge(w_F.sem, 16 * len(loads_F))
            for t in range(TILES):
                mm = pe.transpose(ps[:, 0, 128 * t:128 * t + 128], ctx0[:, t, :], ident[:])
            mm.then_inc(E_cT_ps.sem, 1)
            pe.wait_ge(*E_cT_sb(p, 1))
            pe.matmul(ps[:, 1, :], E_w[:], E_cT[:], start=True, stop=True).then_inc(E_k_ps.sem, 1)
            for t in range(TILES):
                mm = pe.matmul(ps[:, 2, 128 * t:128 * t + 128], E_cT[:, 128 * t:128 * t + 128], E_w[:], start=True, stop=True)
            mm.then_inc(E_v_ps.sem, 1)
            pe.wait_ge(*C_m_ok(p, 1))
            for t in range(TILES):
                t0 = t - t % 2
                dst = ps[:, 4, 16 * t:16 * t + 16]
                both = lambda n: C_m[:, n].rearrange("p k e -> p (k e)")
                pe.matmul(dst, trib[:], both(t), start=True, stop=False)
                if t % 2:
                    pe.matmul(dst, onesb[:], both(t0), start=False, stop=False)
                pe.matmul(dst[:, 8:16], onesb[:], C_m[:, t0, 0], start=False, stop=False)
                mm = pe.matmul(dst[:, 8:16], onesb[:], C_m[:, t0 + 1, 0], start=False, stop=True)
            mm.then_inc(C_pos_ps.sem, 1)
            if units:
                pe.wait_ge(*A_y_sb(p + 1, A_UNITS))
            for r in range(ROWS):
                for t in range(2):
                    pe.wait_ge(*C_D_ok(p, 2 * r + t + 1))
                    mm = pe.matmul(ps[:, 5 + r, :], x2[:, 2 * r + t, :], C_D[:, 2 * r + t].rearrange("p e c -> p (e c)"),
                                   start=t == 0, stop=t == 1)
                mm.then_inc(C_in_ps.sem, 1)

            def combine_T(t):
                pe.wait_ge(*C_cb_ok(p, t + 1))
                if t >= 2:
                    pe.wait_ge(*C_cT_sb(p, t - 1))
                for j in range(4):
                    mm = pe.transpose(ps[:, (7, 0)[t % 2], 128 * j:128 * j + 128],
                                      C_cb[:, t, 2 * j:2 * j + 2, :].rearrange("p e c -> p (e c)"), ident[:])
                mm.then_inc(C_cT_ps.sem, 1)

            def up(e):
                if e >= 2:
                    pe.wait_ge(*C_h_sb(p, e - 1))
                for f in range(FF // 128):
                    mm = pe.matmul(ps[:, 1 + e % 2, 128 * f:128 * f + 128], C_wi[:, e, 128 * f:128 * f + 128],
                                   C_in[:, e].rearrange("p r c -> p (r c)"), start=True, stop=True)
                mm.then_inc(C_h_ps.sem, 1)

            def down(e):
                pe.wait_ge(*C_h_sb(p, e + 1))
                for f in range(FF // 128):
                    mm = pe.matmul(ps[:, 3 + e // 4, 128 * (e % 4):128 * (e % 4) + 128], C_h[:, e % 2, f, :],
                                   C_wo[:, e, f, :], start=f == 0, stop=f == FF // 128 - 1)
                if e % 4 == 3:
                    mm.then_inc(C_eo_ps.sem, 1)

            def combine(half):
                pe.wait_ge(*C_cT_sb(p, TILES))
                pe.wait_ge(*C_eo_act(p, half + 1))
                pe.wait_ge(*C_eo_dve(p, half + 1))
                for t in range(TILES):
                    for j in (2 * half, 2 * half + 1):
                        mm = pe.matmul(ps[:, 5, 128 * t:128 * t + 128], C_cT[:, t, j, :], C_eo[:, t // 2, j, :],
                                       start=t == 0 and j == 0, stop=t == TILES - 1 and j == 3)
                if half:
                    mm.then_inc(C_y_ps.sem, 1)

            pe.wait_ge(*C_in_sb(p, ROWS))
            pe.wait_ge(*E_v_sb(p, 1))
            up(0)
            for e in range(EXPERTS):
                if e < TILES:
                    combine_T(e)
                if e + 1 < EXPERTS:
                    up(e + 1)
                down(e)
                if e == EXPERTS - 3:
                    combine(0)
            combine(1)

        def slots_by_parity(half, r, odd):
            src = ps[64 * r:64 * r + 64, 3 + half, :].rearrange("p (j o c) -> p j o c", j=2, o=2)
            return C_eo[64 * odd:64 * odd + 64, r, 2 * half:2 * half + 2, :], src[:, :, odd, :]

        def stage_C_scalar(act, p):
            def eo_copy(half):
                act.wait_ge(*C_eo_ps(p, half + 1))
                ins = [act.activation(*slots_by_parity(half, 1, odd), ACT.Copy) for odd in range(2)][-1]
                ins.then_inc(C_eo_act.sem, 1)

            act.wait_ge(*E_cT_ps(p, 1))
            act.activation(E_cT[:], ps[:, 0, :], ACT.Copy).then_inc(E_cT_sb.sem, 1)
            act.wait_ge(*C_sub(p, 1))
            act.activation(C_p[:], C_p[:], ACT.Exp).then_inc(C_exp.sem, 1)
            act.wait_ge(*E_k_ps(p, 1))
            act.wait_ge(*E_s_ps(p, 0))
            act.activation(E_kT[:], ps[:, 1, :], ACT.Copy).then_inc(E_k_sb.sem, 1)
            act.wait_ge(*E_v_ps(p, 1))
            act.wait_ge(*E_y_ps(p, 0))
            act.activation(E_v[:].rearrange("p t c -> p (t c)"), ps[:, 2, :], ACT.Copy).then_inc(E_v_sb.sem, 1)
            for r in range(ROWS):
                act.wait_ge(*C_in_ps(p, r + 1))
                act.activation(C_in[:, :, r, :], ps[:, 5 + r, :].rearrange("p (e c) -> p e c", c=CAP), ACT.Copy)\
                    .then_inc(C_in_sb.sem, 1)
            for e in range(EXPERTS):
                act.wait_ge(*C_h_ps(p, e + 1))
                act.activation(C_h[:, e % 2].rearrange("p f s -> p (f s)"), ps[:, 1 + e % 2, :],
                               ACT.Gelu_apprx_tanh).then_inc(C_h_sb.sem, 1)
                if e == EXPERTS // 2:
                    eo_copy(0)
            eo_copy(1)

        def stage_C_vector(dve, p, units, link, layernorm):
            logits = ps[:, 3, 0:8 * TILES].rearrange("p (t e) -> p t e", e=8)
            wait_alone(dve, dve_set, 8, *C_lg_ps(p, 1))
            for t in range(TILES):
                ins = dve.max(C_top[:, t, :], logits[:, t, :])
            link(ins, alone=True)
            for t in range(TILES):
                ins = dve.max_index(C_idx[:, t, :], C_top[:, t, :], logits[:, t, :])
            ins.then_inc(vchain.sem, 1)
            dve.tensor_tensor(C_p[:], logits, C_top[:, :, 0:1].to_broadcast([128, TILES, EXPERTS]), ALU.subtract)\
               .then_inc(C_sub.sem, 1)
            link(None)
            link(dve.tensor_copy(C_idxf[:], C_idx[:, :, 0:2]))
            dve.tensor_tensor(C_m[:].rearrange("p t k e -> p (t k) e"),
                              iota[:, 0:EXPERTS].unsqueeze(1).to_broadcast([128, 2 * TILES, EXPERTS]),
                              C_idxf[:].rearrange("p t k -> p (t k)").unsqueeze(2).to_broadcast([128, 2 * TILES, EXPERTS]),
                              ALU.is_equal).then_inc(C_m_ok.sem, 1)
            dve.wait_ge(*C_exp(p, 1))
            link(dve.tensor_reduce(C_sum[:], C_p[:], AX.X, ALU.add))
            link(dve.reciprocal(C_sum[:], C_sum[:]))
            dve.tensor_tensor(C_p[:], C_p[:], C_sum[:].unsqueeze(2).to_broadcast([128, TILES, EXPERTS]), ALU.mult)\
               .then_inc(C_p_ok.sem, 1)
            dve.wait_ge(*C_pos_ps(p, 1))
            link(dve.tensor_tensor(C_mc[:].rearrange("p t k e -> p (t k e)"), C_m[:].rearrange("p t k e -> p (t k e)"),
                                   ps[:, 4, 0:16 * TILES], ALU.mult))
            link(dve.tensor_tensor(C_slot[:], C_mc[:, :, 0, :], C_mc[:, :, 1, :], ALU.add))
            for t in range(TILES):
                dve.tensor_tensor(C_D[:, t], iota[:, 1:1 + CAP].unsqueeze(1).to_broadcast([128, EXPERTS, CAP]),
                                  C_slot[:, t, :].unsqueeze(2).to_broadcast([128, EXPERTS, CAP]), ALU.is_equal)\
                   .then_inc(C_D_ok.sem, 1)
                if units and t == 0:
                    residual_A(dve, p + 1, A_UNITS - 1)
            for t in range(TILES):
                dve.wait_ge(*C_cT_ps(p, t + 1))
                dve.tensor_copy(C_cT[:, t].rearrange("p j k -> p (j k)"), ps[:, (7, 0)[t % 2], :]).then_inc(C_cT_sb.sem, 1)
            if units:
                dve.wait_ge(*A_y_sb(p + 1, A_UNITS))
                dve.wait_ge(*B_y_ps(p, 1))
                layernorm(x1, 0, x1_ok, src=x0, pair=p + 1)
            for half in range(2):
                dve.wait_ge(*C_eo_ps(p, half + 1))
                ins = [dve.tensor_copy(*slots_by_parity(half, 0, odd)) for odd in range(2)][-1]
                ins.then_inc(C_eo_dve.sem, 1)
            dve.wait_ge(*C_y_ps(p, 1))
            dve.wait_ge(*x2_ok(p, ROWS))
            link(dve.tensor_tensor(ysum[:].rearrange("p t c -> p (t c)"), ps[:, 5, :],
                                   x2[:].rearrange("p t c -> p (t c)"), ALU.add))
            layernorm(D_xn, 2, D_xn_ok, again=x3)

        def stage_C_gpsimd(pool, p):
            pool.wait_ge(*C_p_ok(p, 1))
            for t in range(TILES):
                pool.wait_ge(*C_D_ok(p, t + 1))
                pool.tensor_tensor(C_cb[:, t], C_D[:, t], C_p[:, t, :].unsqueeze(2).to_broadcast([128, EXPERTS, CAP]),
                                   ALU.mult).then_inc(C_cb_ok.sem, 1)

        UNITS = ROWS * HP
        AHEAD = 5
        FREE = UNITS - 4

        def proj_bank(n):
            return n if n < 4 else n % 2

        def back_bank(hp):
            return 2 if hp >= UNITS - FREE and hp % 2 else 0

        def heads_of(u):
            hp, r = divmod(u, ROWS)
            return hp, r

        def stage_D_tensor(pe, p):
            pe.wait_ge(w_D.sem, 16 * len(loads_D))
            for t in range(TILES):
                pe.wait_ge(*D_xn_ok(p, t // 2 + 1))
                mm = pe.transpose(ps[:, 6, 128 * t:128 * t + 128], D_xn[:, t, :], ident[:])
            mm.then_inc(D_xT_ps.sem, 1)
            pe.wait_ge(*D_xT_sb(p, 1))

            def project(hp, kind):
                n = 2 * hp + kind
                if n >= 4:
                    pe.wait_ge(*D_t_ok(p, n - 1 if n >= 6 else n - 3))
                pe.matmul(ps[:, proj_bank(n), :], D_w[:, kind, 128 * hp:128 * hp + 128], D_xT[:], start=True, stop=True)\
                  .then_inc(D_pr_ps.sem, 1)

            def scores(u):
                hp, r = heads_of(u)
                pe.wait_ge(*D_qk_ok(p, 2 * hp + 2))
                pe.wait_ge(*D_exp(p, max(u - 1, 0)))
                for hh in range(2):
                    part = slice(64 * hh, 64 * hh + 64)
                    bank = 2 + 2 * (u % 2) + hh
                    q = D_qk[part, hp % 2, 0, SEQ * r:SEQ * r + SEQ]
                    k = D_qk[part, hp % 2, 1, SEQ * r:SEQ * r + SEQ]
                    pe.matmul(ps[:, bank, 0:128], q[:, 0:128], k[:, 0:128], start=True, stop=False)
                    pe.matmul(ps[:, bank, 0:128], identb[:], causalb[:], start=False, stop=True)
                    pe.matmul(ps[:, bank, 128:KEYS], q[:, 128:SEQ], k, start=True, stop=False)
                    mm = pe.matmul(ps[:, bank, SEQ:KEYS], identb[:], causalb[:], start=False, stop=True)
                mm.then_inc(D_s_ps.sem, 1)

            def turn(u):
                pe.wait_ge(*D_exp(p, u + 1))
                pe.wait_ge(*D_o_sb(p, u))
                for hh in range(2):
                    for b in range(3):
                        mm = pe.transpose(ps[:, 6 + hh, 128 * b:128 * b + 128], D_p[:, u % 2, hh, 128 * b:128 * b + 128],
                                          ident[:])
                mm.then_inc(D_pT_ps.sem, 1)

            def attend(u):
                hp, r = heads_of(u)
                pe.wait_ge(*D_pT_sb(p, u + 1))
                for hh in range(2):
                    v = [D_v[:, 2 * r + t, 128 * hp + 64 * hh:128 * hp + 64 * hh + 64] for t in range(2)]
                    pT = [D_pT[:, u % 2, hh, 128 * b:128 * b + 128] for b in range(3)]
                    o = ps[:, 6 + hh, KEYS:512]
                    pe.matmul(o[:, 0:64], pT[0], v[0], start=True, stop=True)
                    pe.matmul(o[:, 64:128], pT[1], v[0], start=True, stop=False)
                    mm = pe.matmul(o[:, 64:128], pT[2], v[1], start=False, stop=True)
                mm.then_inc(D_o_ps.sem, 1)

            for n in range(2 * TILES):
                if n % 2 == 0:
                    project(*divmod(n // 2, 2))
                if n >= 2:
                    pe.wait_ge(*D_v_sb(p, n - 1))
                t, half = divmod(n, 2)
                pe.matmul(ps[:, 6 + half, :], D_xT[:, 128 * t:128 * t + 128], D_wv[:, 512 * half:512 * half + 512],
                          start=True, stop=True).then_inc(D_v_ps.sem, 1)
            def back(hp):
                pe.wait_ge(*D_t_ok(p, 2 * HP))
                pe.wait_ge(*D_o_sb(p, 2 * hp + 2))
                pe.wait_ge(*D_aT_sb(p, max(hp - 1, 0) if hp > UNITS - FREE else hp))
                if back_bank(hp) == 2:
                    pe.wait_ge(*D_exp(p, UNITS))
                for t in range(TILES):
                    mm = pe.transpose(ps[:, back_bank(hp), 128 * t:128 * t + 128], D_ao[:, hp, t, :], ident[:])
                mm.then_inc(D_aT_ps.sem, 1)

            def accumulate(hp):
                pe.wait_ge(*D_aT_sb(p, hp + 1))
                for t in range(TILES):
                    mm = pe.matmul(ps[:, 1, 128 * t:128 * t + 128], D_aT[:, hp % 2, 128 * t:128 * t + 128], D_wo[:, hp, :],
                                   start=hp == 0 and t == 0, stop=hp == HP - 1 and t == TILES - 1)
                mm.then_inc(D_wo_ps.sem, 1)

            for n in range(TILES, AHEAD):
                project(*divmod(n, 2))
            pe.wait_ge(*D_t_ok(p, 4))
            pe.wait_ge(*D_v_sb(p, 2 * TILES))
            scores(0)
            for u in range(UNITS):
                if u + 1 < UNITS:
                    scores(u + 1)
                early = u - FREE
                if early >= 1:
                    accumulate(early - 1)
                turn(u)
                if u + AHEAD < 2 * HP:
                    project(*divmod(u + AHEAD, 2))
                if early >= 0:
                    back(early)
                attend(u)
            for hp in range(UNITS - FREE, HP):
                back(hp)
                accumulate(hp - 1)
            accumulate(HP - 1)

        def stage_D_scalar(act, p):
            act.wait_ge(*D_xT_ps(p, 1))
            act.activation(D_xT[:], ps[:, 6, :], ACT.Identity, bias=D_beta[:], scale=D_gamma[:]).then_inc(D_xT_sb.sem, 1)

            def swap_halves(hp, kind):
                n = 2 * hp + kind
                act.wait_ge(*D_pr_ps(p, n + 1))
                act.wait_ge(*D_qk_ok(p, max(n - 1, 0)))
                for src, dst in ((slice(96, 128), slice(64, 96)), (slice(64, 96), slice(96, 128))):
                    ins = act.activation(D_sw[dst, kind, :], ps[src, proj_bank(n), :], ACT.Copy, scale=-1.0)
                ins.then_inc(D_sw_ok.sem, 1)

            for n in range(2 * TILES):
                if n % 2 == 0:
                    swap_halves(*divmod(n // 2, 2))
                act.wait_ge(*D_v_ps(p, n + 1))
                act.activation(D_v[:, n // 2, 512 * (n % 2):512 * (n % 2) + 512], ps[:, 6 + n % 2, :], ACT.Copy)\
                    .then_inc(D_v_sb.sem, 1)

            def exps(u):
                act.wait_ge(*D_nb_ok(p, u + 1))
                act.wait_ge(*D_pT_ps(p, max(u - 1, 0)))
                act.wait_ge(*D_o_sb(p, max(u - 1, 0)))
                for hh in range(2):
                    for t, keys in ((0, slice(0, 128)), (1, slice(128, KEYS))):
                        ins = act.activation(D_p[:, u % 2, hh, keys], ps[:, 2 + 2 * (u % 2) + hh, keys], ACT.Exp,
                                             bias=D_nb[:, u % 2, t, hh:hh + 1], scale=DH ** -0.5,
                                             accum_out=D_sum[:, u % 2, t, hh:hh + 1])
                ins.then_inc(D_exp.sem, 1)

            def pT_copy(u):
                act.wait_ge(*D_pT_ps(p, u + 1))
                act.wait_ge(*D_o_ps(p, max(u - 1, 0)))
                act.activation(D_pT[:, u % 2], ps[:, 6:8, 0:KEYS], ACT.Copy).then_inc(D_pT_sb.sem, 1)

            def aT_copy(hp):
                act.wait_ge(*D_aT_ps(p, hp + 1))
                act.wait_ge(*D_wo_ps(p, max(hp - 1, 0)))
                act.activation(D_aT[:, hp % 2, :], ps[:, back_bank(hp), :], ACT.Copy).then_inc(D_aT_sb.sem, 1)

            for n in range(TILES, AHEAD):
                swap_halves(*divmod(n, 2))
            exps(0)
            for u in range(UNITS):
                if 1 <= u and u - 1 + AHEAD < 2 * HP:
                    swap_halves(*divmod(u - 1 + AHEAD, 2))
                pT_copy(u)
                if u + 1 < UNITS:
                    exps(u + 1)
                if u >= FREE:
                    aT_copy(u - FREE)
            for hp in range(UNITS - FREE, HP):
                aT_copy(hp)

        def stage_D_vector(dve, p, link, layernorm):
            def rope_parts(hp, kind):
                n = 2 * hp + kind
                bank = proj_bank(n)
                dve.wait_ge(*D_sw_ok(p, n + 1))
                dve.wait_ge(*D_qk_ok(p, max(n - 1, 0)))
                rows = lambda x: x.rearrange("p (r t) -> p r t", r=ROWS)
                for src, dst in ((slice(32, 64), slice(0, 32)), (slice(0, 32), slice(32, 64))):
                    dve.tensor_tensor(rows(D_t[dst, kind, 1, :]), rows(ps[src, bank, :]),
                                      sin[src, :].unsqueeze(1).to_broadcast([32, ROWS, SEQ]), ALU.mult)
                dve.tensor_tensor(rows(D_t[:, kind, 0, :]), rows(ps[:, bank, :]),
                                  cos[:].unsqueeze(1).to_broadcast([128, ROWS, SEQ]), ALU.mult).then_inc(D_t_ok.sem, 1)

            def maxima(u):
                dve.wait_ge(*D_s_ps(p, u + 1))
                s = ps[:, 2 + 2 * (u % 2):4 + 2 * (u % 2), :]
                dve.tensor_reduce(D_mx[:, u % 2, 0, :], s[:, :, 0:128], AX.X, ALU.max)
                link(dve.tensor_reduce(D_mx[:, u % 2, 1, :], s[:, :, 128:KEYS], AX.X, ALU.max))
                dve.wait_ge(*D_exp(p, max(u - 1, 0)))
                dve.tensor_scalar(D_nb[:, u % 2].rearrange("p t h -> p (t h)"), D_mx[:, u % 2].rearrange("p t h -> p (t h)"),
                                  -DH ** -0.5, None, ALU.mult).then_inc(D_nb_ok.sem, 1)

            def normalise(u):
                hp, r = heads_of(u)
                dve.wait_ge(*D_o_ps(p, u + 1))
                link(dve.reciprocal(D_rs[:, u % 2].rearrange("p t h -> p (t h)"),
                                    D_sum[:, u % 2].rearrange("p t h -> p (t h)")))
                dst = D_ao[:, hp, 2 * r:2 * r + 2, :].rearrange("p t (h d) -> p h t d", d=DH)
                rs = D_rs[:, u % 2].rearrange("p t h -> p h t").unsqueeze(3).to_broadcast([128, 2, 2, DH])
                dve.tensor_tensor(dst, ps[:, 6:8, KEYS:512].rearrange("p h (t d) -> p h t d", d=DH), rs, ALU.mult)\
                   .then_inc(D_o_sb.sem, 1)

            for n in range(AHEAD):
                rope_parts(*divmod(n, 2))
            maxima(0)
            for u in range(UNITS):
                if u + 1 < UNITS:
                    maxima(u + 1)
                if 1 <= u and u - 1 + AHEAD < 2 * HP:
                    rope_parts(*divmod(u - 1 + AHEAD, 2))
                normalise(u)
            dve.wait_ge(*D_wo_ps(p, HP))
            link(dve.tensor_tensor(ysum[:], ps[:, 1, :].rearrange("p (t c) -> p t c", c=DIM), x3[:], ALU.add))
            layernorm(x4, 3, x4_ok)

        def stage_D_gpsimd(pool, p):
            for n in range(2 * HP):
                hp, kind = divmod(n, 2)
                second = slice(64, 128)
                pool.wait_ge(*(D_qk_ok(p, n) if n else rstd_ok(p, 2)))
                pool.wait_ge(*D_sw_ok(p, n + 1))
                pool.tensor_tensor(D_t[second, kind, 1, :].rearrange("p (r t) -> p r t", r=ROWS),
                                   D_sw[second, kind, :].rearrange("p (r t) -> p r t", r=ROWS),
                                   sin[second, :].unsqueeze(1).to_broadcast([64, ROWS, SEQ]), ALU.mult)\
                    .then_inc(D_sin_ok.sem, 1)
                pool.wait_ge(*D_sin_ok(p, n + 1))
                pool.wait_ge(*D_t_ok(p, n + 1))
                pool.wait_ge(*D_s_ps(p, max(ROWS * (hp - 1), 0)))
                pool.tensor_tensor(D_qk[:, hp % 2, kind, :], D_t[:, kind, 0, :], D_t[:, kind, 1, :], ALU.add)\
                    .then_inc(D_qk_ok.sem, 1)

        E_XT_BANKS, E_Q_BANKS, E_Y_BANKS = (1, 4), (7, 5), (6, 4)

        def of_row(r):
            return slice(SEQ * r, SEQ * r + SEQ)

        def stage_E_tensor(pe, p, more):
            if more:
                start_A_tensor_qk(pe, p + 2)
            for r in range(ROWS):
                pe.wait_ge(*x4_ok(p, r + 1))
                for t in range(2):
                    mm = pe.transpose(ps[:, E_XT_BANKS[r], 128 * t:128 * t + 128], x4[:, 2 * r + t, :], ident[:])
                mm.then_inc(E_xT_ps.sem, 1)
            for r in range(ROWS):
                pe.wait_ge(*E_xT_sb(p, r + 1))
                pe.matmul(ps[:, E_Q_BANKS[r], 0:SEQ], E_w[:], E_xT[:, of_row(r)], start=True, stop=True)\
                  .then_inc(E_q_ps.sem, 1)
            pe.wait_ge(*E_k_sb(p, 1))
            if more:
                pe.wait_ge(*A_q_sb(p + 2, 1))
                pe.wait_ge(*A_k_sb(p + 2, 1))
            for r in range(ROWS):
                pe.wait_ge(*E_q_sb(p, r + 1))
                q, k = (x[:, of_row(r)] for x in (E_qT, E_kT))
                pe.matmul(ps[:, 2 + r, 0:128], q[:, 0:128], k[:, 0:128], start=True, stop=False)
                pe.matmul(ps[:, 2 + r, 0:128], identb[:], causalb[:], start=False, stop=True)
                pe.matmul(ps[:, 2 + r, 128:KEYS], q[:, 128:SEQ], k, start=True, stop=False)
                mm = pe.matmul(ps[:, 2 + r, SEQ:KEYS], identb[:], causalb[:], start=False, stop=True)
            mm.then_inc(E_s_ps.sem, 1)
            if more:
                start_A_tensor_v(pe, p + 2, 0)
            pe.wait_ge(*E_exp(p, 1))
            for r in range(ROWS):
                for b in range(3):
                    mm = pe.transpose(ps[:, 4 + r, 128 * b:128 * b + 128], E_p[:, r, 128 * b:128 * b + 128], ident[:])
            mm.then_inc(E_pT_ps.sem, 1)
            pe.wait_ge(*E_v_sb(p, 1))
            pe.wait_ge(*E_pT_sb(p, 1))
            for r in range(ROWS):
                pT = [E_pT[:, r, 128 * b:128 * b + 128] for b in range(3)]
                o = ps[:, E_Y_BANKS[r], 0:SEQ]
                pe.matmul(o[:, 0:128], pT[0], E_v[:, 2 * r, :], start=True, stop=True)
                pe.matmul(o[:, 128:256], pT[1], E_v[:, 2 * r, :], start=True, stop=False)
                pe.matmul(o[:, 128:256], pT[2], E_v[:, 2 * r + 1, :], start=False, stop=True).then_inc(E_y_ps.sem, 1)
            if more:
                start_A_tensor_v(pe, p + 2, 1)

        def stage_E_scalar(act, p, more):
            if more:
                start_A_scalar_q(act, p + 2)
            for r in range(ROWS):
                act.wait_ge(*E_xT_ps(p, r + 1))
                act.activation(E_xT[:, of_row(r)], ps[:, E_XT_BANKS[r], 0:SEQ], ACT.Copy).then_inc(E_xT_sb.sem, 1)
            for r in range(ROWS):
                act.wait_ge(*E_q_ps(p, r + 1))
                act.activation(E_qT[:, of_row(r)], ps[:, E_Q_BANKS[r], 0:SEQ], ACT.Copy).then_inc(E_q_sb.sem, 1)
            act.wait_ge(*E_nb_ok(p, 1))
            for r in range(ROWS):
                for t, keys in ((0, slice(0, 128)), (1, slice(128, KEYS))):
                    ins = act.activation(E_p[:, r, keys], ps[:, 2 + r, keys], ACT.Exp, bias=E_nb[:, t, r:r + 1],
                                         scale=float(DIM ** -0.5), accum_out=E_sum[:, t, r:r + 1])
            ins.then_inc(E_exp.sem, 1)
            act.wait_ge(*E_pT_ps(p, 1))
            act.activation(E_pT[:], ps[:, 4:6, 0:KEYS], ACT.Copy).then_inc(E_pT_sb.sem, 1)
            if more:
                start_A_scalar_heads(act, p + 2)

        def stage_E_vector(dve, p, more, link, layernorm):
            if more:
                start_A_vector_k(dve, p + 2)
            dve.wait_ge(*E_s_ps(p, 1))
            dve.tensor_reduce(E_mx[:, 0, :], ps[:, 2:4, 0:128], AX.X, ALU.max)
            link(dve.tensor_reduce(E_mx[:, 1, :], ps[:, 2:4, 128:KEYS], AX.X, ALU.max))
            dve.tensor_scalar(E_nb[:].rearrange("p t r -> p (t r)"), E_mx[:].rearrange("p t r -> p (t r)"),
                              -float(DIM ** -0.5), None, ALU.mult).then_inc(E_nb_ok.sem, 1)
            if more:
                start_A_vector_v(dve, p + 2, 0)
            dve.wait_ge(*E_exp(p, 1))
            link(dve.reciprocal(E_rs[:].rearrange("p t r -> p (t r)"), E_sum[:].rearrange("p t r -> p (t r)")))
            dve.wait_ge(*x4_ok(p, ROWS))

            def fill(r):
                dve.wait_ge(*E_y_ps(p, r + 1))
                y = ysum[:, 2 * r:2 * r + 2, :]
                link(dve.tensor_tensor(y, ps[:, E_Y_BANKS[r], 0:SEQ].rearrange("p (t c) -> p t c", t=2),
                                       E_rs[:, :, r:r + 1].to_broadcast([128, 2, DIM]), ALU.mult))
                link(dve.tensor_tensor(y, y, x4[:, 2 * r:2 * r + 2, :], ALU.add))

            layernorm(x5, 4, x5_ok, fill=fill)

        F_NT_BANKS = (5, 6, 4, 5)
        F_XT_BANKS, F_Y_BANKS = (0, 7), (7, 6)

        def stage_F_tensor(pe, p, more):
            if more:
                pe.wait_ge(*A_v_sb(p + 2, 2))
            for r in range(ROWS):
                pe.wait_ge(*x5_ok(p, r + 1))
                for t in range(2):
                    mm = pe.transpose(ps[:, F_XT_BANKS[r], 128 * t:128 * t + 128], x5[:, 2 * r + t, :], ident[:])
                mm.then_inc(F_xT_ps.sem, 1)
            pe.wait_ge(F_chain.sem, 7)
            if more:
                pe.wait_ge(*A_v_sb(p + 2, 4))
            for t in range(TILES):
                pe.wait_ge(*F_xT_sb(p, t // 2 + 1))
                pe.matmul(ps[:, 1 + t, :], F_xT[:, 128 * t:128 * t + 128], F_w1[:], start=True, stop=True)\
                  .then_inc(F_h_ps.sem, 1)
            if more:
                pe.wait_ge(*F_h_sb(p, 3))
                start_A_tensor_scores(pe, p + 2)

            def transpose_n(k, t):
                return pe.transpose(ps[:, F_NT_BANKS[k], 128 * t:128 * t + 128], F_h[:, t, 128 * k:128 * k + 128], ident[:])

            for r in range(ROWS):
                pe.wait_ge(*F_n_ok(p, r + 1))
                for k in range(3):
                    for t in range(2 * r, 2 * r + 2):
                        mm = transpose_n(k, t)
                    if r == ROWS - 1:
                        mm.then_inc(F_nT_ps.sem, 1)
            pe.wait_ge(*F_nT_sb(p, 1))
            for t in range(TILES):
                mm = transpose_n(3, t)
            mm.then_inc(F_nT_ps.sem, 1)
            for r in range(ROWS):
                for k in range(FF // 128):
                    if r == 0:
                        pe.wait_ge(*F_nT_sb(p, k + 1))
                    for t in range(2):
                        tokens = slice(SEQ * r + 128 * t, SEQ * r + 128 * t + 128)
                        mm = pe.matmul(ps[:, F_Y_BANKS[r], 128 * t:128 * t + 128], F_nT[:, k, tokens], F_w2[:, k, :],
                                       start=k == 0 and t == 0, stop=k == FF // 128 - 1 and t == 1)
                mm.then_inc(F_y_ps.sem, 1)

        def stage_F_scalar(act, p):
            for r in range(ROWS):
                act.wait_ge(*F_xT_ps(p, r + 1))
                act.activation(F_xT[:, of_row(r)], ps[:, F_XT_BANKS[r], 0:SEQ], ACT.Copy).then_inc(F_xT_sb.sem, 1)
            for t in range(TILES):
                act.wait_ge(*F_h_ps(p, t + 1))
                act.activation(F_h[:, t, :], ps[:, 1 + t, :], ACT.Gelu).then_inc(F_h_sb.sem, 1)
            for k in range(FF // 128):
                act.wait_ge(*F_nT_ps(p, k + 1))
                act.activation(F_nT[:, k, :], ps[:, F_NT_BANKS[k], :], ACT.Identity, bias=F_lb[:, k:k + 1],
                               scale=F_lw[:, k:k + 1]).then_inc(F_nT_sb.sem, 1)

        def stage_F_vector(dve, p, more, link, layernorm):
            if more:
                start_A_vector_v(dve, p + 2, 1)
                start_A_vector_heads(dve, p + 2)
            layernorm(F_h, 5, F_n_ok, F_h, come=F_h_sb)
            if more:
                for u in range(2):
                    A_softmax(dve, p + 2, link, u)

            def fill(r):
                dve.wait_ge(*F_y_ps(p, r + 1))
                link(dve.tensor_tensor(ysum[:, 2 * r:2 * r + 2, :].rearrange("p t c -> p (t c)"),
                                       ps[:, F_Y_BANKS[r], 0:SEQ],
                                       x5[:, 2 * r:2 * r + 2, :].rearrange("p t c -> p (t c)"), ALU.add))

            layernorm(x6, 6, x6_ok, fill=fill)

        def ternary_vector(dve):
            dve.wait_ge(F_tot_ps.sem, 1)
            dve.tensor_scalar(F_thr[:, 0, :], ps[:, 7, 0:2], 1.0 / (DIM * FF), ABS_EPS, ALU.mult, ALU.add)\
               .then_inc(F_chain.sem, 1)
            dve.wait_ge(F_chain.sem, 1)
            dve.tensor_scalar(F_thr[:, 1, :], F_thr[:, 0, :], -0.5, None, ALU.mult).then_inc(F_chain.sem, 1)
            dve.wait_ge(F_chain.sem, 2)
            dve.tensor_scalar(F_thr[:, 0, :], F_thr[:, 0, :], 0.5, None, ALU.mult).then_inc(F_chain.sem, 1)
            dve.wait_ge(F_chain.sem, 3)
            for i, (w, raw) in enumerate(((F_w1[:], F_w1r[:]), (F_w2[:].rearrange("p k c -> p (k c)"),
                                                              F_w2r[:].rearrange("p k c -> p (k c)")))):
                dve.tensor_scalar(w, raw, F_thr[:, 0, i:i + 1], None, ALU.is_gt)
                dve.tensor_scalar(F_abs[:], raw, F_thr[:, 1, i:i + 1], None, ALU.is_lt).then_inc(F_chain.sem, 1)
                dve.wait_ge(F_chain.sem, 4 + 2 * i)
                dve.tensor_tensor(w, w, F_abs[:], ALU.subtract).then_inc(F_chain.sem, 1)
                dve.wait_ge(F_chain.sem, 5 + 2 * i)

        @block.sync
        def _(sp):
            rows = lambda t, p: t[bass.ds(p * ROWS, ROWS), :, :].rearrange("r (t q) d -> q (r t) d", q=128)

            def load(loads, w):
                for dst, src in loads:
                    sp.dma_start(dst[:], src).then_inc(w.sem, 16)

            sp.dma_start(x0[:], rows(a["x"], 0)).then_inc(x_in.sem, 16)
            load(loads_A, w_A)
            load(loads_F, w_F)
            sp.dma_start(x4[:], rows(a["x"], 1)).then_inc(x_early.sem, 16)
            sp.dma_start(ctx0[:], rows(a["ctx"], 0)).then_inc(c_in.sem, 16)
            load(loads_B, w_B)
            load(loads_C, w_C)
            load(loads_D, w_D)

            def next_x(p):
                sp.wait_ge(*x1_ok(p - 1, ROWS))
                sp.dma_start(x0[:], rows(a["x"], p)).then_inc(x_in.sem, 16)

            def pair(p, units, head):
                if units:
                    sp.wait_ge(*E_cT_ps(p, 1))
                    sp.dma_start(ctx0[:], rows(a["ctx"], p + 1)).then_inc(c_in.sem, 16)
                if head:
                    next_x(p + 2)
                sp.wait_ge(*x6_ok(p, ROWS))
                sp.dma_start(rows(out, p), x6[:]).then_inc(out_done.sem, 16)

            next_x(1)
            with sp.Fori(0, PAIRS - 2) as p:
                pair(p, True, True)
            pair(PAIRS - 2, True, False)
            pair(PAIRS - 1, False, False)
            sp.wait_ge(out_done.sem, 16 * PAIRS + 1)

        @block.gpsimd
        def _(pool):
            pool.memset(ones[:], 1.0).then_inc(pool_set.sem, 1)
            pool.memset(minus_half[:], -0.5).then_inc(pool_set.sem, 1)
            pool.memset(A_xT[:], 0.0).then_inc(pool_set.sem, 1)
            pool.memset(A_kT[:], 0.0).then_inc(pool_set.sem, 1)
            pool.memset(A_v[:, :, :, 32:33], 1.0).then_inc(pool_set.sem, 1)
            pool.wait_ge(pool_set.sem, 5)
            def power_x1(q):
                pool.wait_ge(*x1_var_ok(q, 1))
                x = rstd[:, 0, :]
                pool.tensor_tensor(x, x, minus_half[:, 0:TILES], ALU.pow).then_inc(x1_rstd_ok.sem, 1)

            def pair(p, units, head):
                def power(n, both=False):
                    pool.wait_ge(*var_ok(p, n))
                    x = rstd[:, 0:1 + both].rearrange("p k t -> p (k t)")
                    pool.tensor_tensor(x, x, minus_half[:, 0:TILES * (1 + both)], ALU.pow).then_inc(rstd_ok.sem, 1)

                stage_B_gpsimd(pool, p)
                power(1)
                stage_C_gpsimd(pool, p)
                if units:
                    power_x1(p + 1)
                power(2, both=True)
                stage_D_gpsimd(pool, p)
                if head:
                    wait_alone(pool, pool_set, 5, *C_y_ps(p, 1))
                    pool.memset(A_v[:, :, :, 32:33], 1.0).then_inc(A_ones.sem, 1)
                power(3)
                if head:
                    start_A_gpsimd(pool, p + 2)
                for n in range(4, LNS + 1):
                    power(n)

            start_A_gpsimd(pool, 0)
            power_x1(0)
            start_A_gpsimd(pool, 1)
            with pool.Fori(0, PAIRS - 2) as p:
                pair(p, True, True)
            pair(PAIRS - 2, True, False)
            pair(PAIRS - 1, False, False)

        @block.scalar
        def _(act):
            for s in signals:
                if s.per:
                    act.sem_inc(s.sem, 1)
            act.wait_ge(w_A.sem, 16 * len(loads_A))
            act.wait_ge(pool_set.sem, 5)
            act.wait_ge(dve_set.sem, 8)

            def magnitudes():
                act.wait_ge(w_F.sem, 16 * len(loads_F))
                for i, raw in enumerate((F_w1r[:], F_w2r[:].rearrange("p k c -> p (k c)"))):
                    ins = act.activation(F_abs[:], raw, ACT.Abs, accum_out=F_sum[:, i:i + 1])
                    ins.then_inc(F_abs_ok.sem, 1)
                    act.wait_ge(F_abs_ok.sem, i + 1)

            def pair(p, units, head):
                stages_AB_scalar(act, p + 1 if units else None, p, B_scalar(act, p))
                stage_C_scalar(act, p)
                stage_D_scalar(act, p)
                stage_E_scalar(act, p, head)
                stage_F_scalar(act, p)

            start_A_scalar_q(act, 0)
            start_A_scalar_heads(act, 0)
            setup = [None] * SLOTS
            setup[8] = magnitudes
            stages_AB_scalar(act, 0, None, setup)
            start_A_scalar_q(act, 1)
            start_A_scalar_heads(act, 1)
            act.wait_ge(F_chain.sem, 7)
            with act.Fori(0, PAIRS - 2) as p:
                pair(p, True, True)
            pair(PAIRS - 2, True, False)
            pair(PAIRS - 1, False, False)

        @block.tensor
        def _(pe):
            pe.wait_ge(w_A.sem, 16 * len(loads_A))
            for kind in range(3):
                mm = pe.matmul(ps[0:WIN, 6, 128 * kind:128 * kind + 128], valid[:, kind, :], A_bv[:], start=True, stop=True)
            mm.then_inc(A_vbias_ps.sem, 1)
            pe.wait_ge(pool_set.sem, 5)
            pe.wait_ge(dve_set.sem, 8)

            def totals():
                pe.wait_ge(F_abs_ok.sem, 2)
                pe.wait_ge(*A_v_sb(0, 2))
                pe.matmul(ps[:, 7, 0:2], ones[:], F_sum[:], start=True, stop=True).then_inc(F_tot_ps.sem, 1)

            def pair(p, units, head):
                stages_AB_tensor(pe, p + 1 if units else None, p, B_tensor(pe, p))
                stage_C_tensor(pe, p, units)
                stage_D_tensor(pe, p)
                stage_E_tensor(pe, p, head)
                stage_F_tensor(pe, p, head)

            def start_A_v(q):
                start_A_tensor_v(pe, q, 0)
                pe.wait_ge(*A_q_sb(q, 1))
                start_A_tensor_v(pe, q, 1)

            start_A_tensor_qk(pe, 0)
            start_A_v(0)
            start_A_tensor_scores(pe, 0)
            setup = [None] * SLOTS
            setup[11] = totals
            stages_AB_tensor(pe, 0, None, setup)
            pe.wait_ge(*A_sub(0, A_UNITS))
            start_A_tensor_qk(pe, 1, x4, (x_early.sem, 16))
            fold_heads(pe, 0, A_UNITS - 1)
            pe.wait_ge(F_chain.sem, 1)
            start_A_v(1)
            start_A_tensor_scores(pe, 1)
            with pe.Fori(0, PAIRS - 2) as p:
                pair(p, True, True)
            pair(PAIRS - 2, True, False)
            pair(PAIRS - 1, False, False)

        @block.vector
        def _(dve):
            dve.wait_ge(w_A.sem, 16 * len(loads_A))
            dve.tensor_copy(identb[:], ident[:]).then_inc(dve_set.sem, 1)
            dve.tensor_copy(edgeb[:].rearrange("p s k -> p (s k)"), edge[:]).then_inc(dve_set.sem, 1)
            dve.tensor_copy(trib[:], tri[:]).then_inc(dve_set.sem, 1)
            dve.memset(onesb[:], 1.0).then_inc(dve_set.sem, 1)
            dve.tensor_copy(causalb[:], causal[:]).then_inc(dve_set.sem, 1)
            dve.wait_ge(A_vbias_ps.sem, 1)
            for kind in range(3):
                dve.tensor_copy(A_vbias[:, kind, :], ps[0:WIN, 6, 128 * kind:128 * kind + 128]).then_inc(dve_set.sem, 1)
            dve.wait_ge(dve_set.sem, 8)
            dve.wait_ge(pool_set.sem, 5)

            def linker(p, before):
                links = [0]

                def link(ins, alone=False):
                    links[0] += 1
                    if ins is not None:
                        ins.then_inc(vchain.sem, 1)
                    if alone:
                        wait_alone(dve, dve_set, 8, *vchain(p, before + links[0]))
                    else:
                        dve.wait_ge(*vchain(p, before + links[0]))

                return link, links

            def normaliser(p, link):
                def layernorm(dst, n, ready, src=ysum, again=None, pair=p, come=None, fill=None):
                    for t in range(TILES):
                        if fill is not None and t % 2 == 0:
                            fill(t // 2)
                        if come is not None:
                            dve.wait_ge(*come(pair, t + 1))
                        ins = dve.bn_stats(stats[:, t, :], src[:, t, :])
                    link(ins, alone=True)
                    for t in range(TILES):
                        ins = dve.bn_aggr(mv[:, t, :], stats[:, t, :])
                    link(ins)
                    if again is not None:
                        dve.tensor_scalar(rstd[:, 1, :], mv[:, :, 1], 1 + LN_EPS, LN_EPS ** 2, ALU.mult, ALU.add)
                    dve.tensor_scalar(rstd[:, 0, :], mv[:, :, 1], LN_EPS, None, ALU.add)\
                       .then_inc((var_ok if n else x1_var_ok).sem, 1)
                    dve.wait_ge(*(rstd_ok(p, n) if n else x1_rstd_ok(pair, 1)))
                    for t in range(TILES):
                        ins = dve.tensor_scalar(dst[:, t, :], src[:, t, :], mv[:, t, 0:1],
                                                rstd[:, 0 if again is None else 1, t:t + 1], ALU.subtract, ALU.mult)
                        if t % 2:
                            ins.then_inc(ready.sem, 1)
                    if again is not None:
                        for t in range(TILES):
                            ins = dve.tensor_scalar(again[:, t, :], src[:, t, :], mv[:, t, 0:1], rstd[:, 0, t:t + 1],
                                                    ALU.subtract, ALU.mult)
                        link(ins)
                    wait_alone(dve, dve_set, 8, *ready(pair, ROWS))

                return layernorm

            def pair(p, units, head, before):
                link, links = linker(p, before)
                layernorm = normaliser(p, link)
                stages_AB_vector(dve, p + 1 if units else None, p, B_vector(dve, p, link, layernorm), link)
                stage_C_vector(dve, p, units, link, layernorm)
                stage_D_vector(dve, p, link, layernorm)
                stage_E_vector(dve, p, head, link, layernorm)
                stage_F_vector(dve, p, head, link, layernorm)
                return links[0]

            def start_A(q):
                start_A_vector_k(dve, q)
                start_A_vector_v(dve, q, 0)
                start_A_vector_v(dve, q, 1)
                start_A_vector_heads(dve, q)

            link, links = linker(0, 0)
            layernorm = normaliser(0, link)
            start_A(0)
            A_softmax(dve, 0, link, 0)
            A_softmax(dve, 0, link, 1)
            setup = [None] * SLOTS
            setup[12] = lambda: ternary_vector(dve)
            stages_AB_vector(dve, 0, None, setup, link)
            start_A(1)
            residual_A(dve, 0, A_UNITS - 1)
            dve.wait_ge(*A_y_sb(0, A_UNITS))
            layernorm(x1, 0, x1_ok, src=x0)
            A_softmax(dve, 1, link, 0)
            A_softmax(dve, 1, link, 1)
            before = links[0]
            with dve.Fori(0, PAIRS - 2) as p:
                done = pair(p, True, True, before)
                assert done == VCHAIN, done
            done = pair(PAIRS - 2, True, False, before)
            pair(PAIRS - 1, False, False, before + done - VCHAIN)


PACKS = {"pack_A": {"ident": 128, "A_wq": 128, "A_wk": 128, "A_wv": 128, "A_bq": 1, "A_bk": 1, "qscale": HEADS,
                    "own": 4, "fold": CHUNK},
         "pack_raw": {"edge": 2 * WIN, "tri": 128, "causal": 128}}
A_Q_WORDS = TOK + CHUNKS * HEADS * CHUNK
ODD_WORDS, EVEN_WORDS = 10368 - 2048, 16896
VCHAIN = 101
LNS = 6


def kernel(**inputs):
    import concourse.bacc as bacc
    from concourse.bass_utils import run_bass_kernel_spmd as run

    arrays = dict(shape_constants())
    i = inputs
    arrays["x"] = i["x"]
    for n in "qkv":
        arrays[f"A_w{n}"] = i[f"L0_attn_W{n}"].T
    arrays["A_bq"], arrays["A_bk"] = i["L0_attn_bq"][:, None], i["L0_attn_bk"][:, None]
    arrays["A_bv"] = i["L0_attn_bv"][None]
    for n in "qo":
        arrays[f"B_w{n}"], arrays[f"B_b{n}"] = i[f"L0_xattn_W{n}"].T, i[f"L0_xattn_b{n}"][None]
    arrays["B_wkv"] = np.concatenate([i["L0_xattn_Wk"].T, i["L0_xattn_Wv"].T], 1)
    arrays["B_bkv"] = np.concatenate([i["L0_xattn_bk"], i["L0_xattn_bv"]])[None]
    arrays["C_wr"] = i["L0_ffn_w_router"]
    arrays["C_wi"] = i["L0_ffn_wi"].transpose(1, 0, 2)
    arrays["C_wo"] = i["L0_ffn_wo"].reshape(EXPERTS, FF // 128, 128, DIM).transpose(2, 0, 1, 3)
    arrays["D_gamma"], arrays["D_beta"] = i["L1_attn_gamma"][:, None], i["L1_attn_beta"][:, None]
    arrays["D_w"] = np.stack([i["L1_attn_Wq"], i["L1_attn_Wkv"][:, :INNER]], 1)
    arrays["D_wv"] = i["L1_attn_Wkv"][:, INNER:]
    arrays["D_wo"] = i["L1_attn_Wo"].reshape(HP, 128, DIM).transpose(1, 0, 2)
    arrays["E_w"] = i["L1_xattn_Wq"].T
    arrays["F_w1"] = i["L1_ffn_W_fc"].T
    arrays["F_w2"] = i["L1_ffn_W_proj"].T.reshape(FF // 128, 128, DIM).transpose(1, 0, 2)
    arrays["F_lw"], arrays["F_lb"] = (i[f"L1_ffn_ln_{n}"].reshape(FF // 128, 128).T for n in "wb")
    arrays["ctx"] = i["ctx_1024"]
    for name, parts in PACKS.items():
        arrays[name] = np.concatenate([arrays.pop(part) for part in parts], 1)
    arrays = {k: np.ascontiguousarray(v) for k, v in arrays.items()}
    nc = bacc.Bacc("TRN2", target_bir_lowering=False, num_devices=1)
    aps = {k: nc.dram_tensor(f"in_{k}", v.shape, mybir.dt.from_np(v.dtype), kind="ExternalInput").ap()
           for k, v in arrays.items()}
    out = nc.dram_tensor("out", (BATCH, SEQ, DIM), mybir.dt.float32, kind="ExternalOutput").ap()
    decoder(nc, aps, out)
    r = run(nc, [{f"in_{k}": v for k, v in arrays.items()}], core_ids=[0])
    return r.results[0]["out"]
```
